# Optimizing a Trainium2 kernel written in Bass

```python
import numpy as np
import jax
import jax.numpy as jnp

def _softmax(x, axis=-1):
    return jax.nn.softmax(x, axis=axis)

def _gelu(x):
    return jax.nn.gelu(x, approximate=True)

def _silu(x):
    return jax.nn.silu(x)

def _sigmoid(x):
    return jax.nn.sigmoid(x)

def _layernorm(x, axis=-1, eps=1e-05):
    m = jnp.mean(x, axis=axis, keepdims=True)
    v = jnp.var(x, axis=axis, keepdims=True)
    return (x - m) / jnp.sqrt(v + eps)

def _scatter_add(tgt, idx, src, axis=0):
    return tgt.at[idx].add(src)

def _segment_sum(src, seg, n):
    return jax.ops.segment_sum(src, seg, n)
kernel_name = 'mk_decoder_postln_d2_seqx_r4_83bf5f'

def setup_inputs(seed: int=0):
    np.random.seed(seed)
    _w = jnp.asarray

    def _rec_inputs():
        import jax
        import jax.numpy as jnp
        _rk = jax.random.key(seed)
        x = -0.0002928 + 1 * jax.random.normal(jax.random.fold_in(_rk, 1), (16, 256, 256), jnp.float32)
        _lenS = 256 - jax.random.randint(jax.random.fold_in(_rk, 7), (16,), 0, max(1, 256 // 4) + 1, jnp.int32)
        _lenS2 = 77 - jax.random.randint(jax.random.fold_in(_rk, 8), (16,), 0, max(1, 77 // 4) + 1, jnp.int32)
        _ctx_1024P = jax.random.normal(jax.random.fold_in(_rk, 11), (16, 16, 256), jnp.float32)
        _ctx_1024c = jax.random.dirichlet(jax.random.fold_in(_rk, 511), 0.3 * jnp.ones((16,), jnp.float32), (16, 77))
        _ctx_1024t = jnp.einsum('bsk,bkd->bsd', _ctx_1024c, _ctx_1024P)
        _ctx_1024t = _ctx_1024t * jax.lax.rsqrt(jnp.mean(jnp.square(_ctx_1024t)) + 1e-12) * 0.953939
        ctx_1024 = -1.39393e-06 + 0.999914 * (_ctx_1024t + 0.3 * jax.random.normal(jax.random.fold_in(_rk, 611), (16, 77, 256), jnp.float32))
        _validS = jnp.arange(256)[None, :] < _lenS[:, None]
        _validS2 = jnp.arange(77)[None, :] < _lenS2[:, None]
        _causal = jnp.tril(jnp.ones((256, 256), dtype=bool))
        mask_Bx1xSxS2_ik1 = jnp.where(jnp.broadcast_to(_validS2[:, None, None, :], (16, 1, 256, 77)), 1, 0).astype(jnp.int32)
        mask_BxS2_ik0 = jnp.where(jnp.broadcast_to(_validS2[:, :], (16, 77)), 0, 1).astype(jnp.int32)
        return (x, ctx_1024, mask_Bx1xSxS2_ik1, mask_BxS2_ik0)
    x, ctx_1024, mask_Bx1xSxS2_ik1, mask_BxS2_ik0 = _rec_inputs()

    def _L0_attn_setup():
        import jax, jax.numpy as jnp
        import numpy as np
        D_MODEL = 256
        D_INNER = 2 * D_MODEL
        D_STATE = 16
        D_CONV = 4
        DT_RANK = (D_MODEL + 15) // 16
        B_SZ, L_SEQ = (2, 512)
        LN_EPS = 1e-06

        def _mamba_block(x, ln_g, ln_b, W_in, conv_w, conv_b, W_x, W_dt, b_dt, A_log, Dp, W_out):
            B, L, D = x.shape
            mu = jnp.mean(x, axis=-1, keepdims=True)
            var = jnp.mean(jnp.square(x - mu), axis=-1, keepdims=True)
            h = (x - mu) * jax.lax.rsqrt(var + LN_EPS) * ln_g + ln_b
            xz = jnp.einsum('bld,ed->ble', h, W_in)
            xi, z = jnp.split(xz, 2, axis=-1)
            xc = jnp.transpose(xi, (0, 2, 1))
            xc = jax.lax.conv_general_dilated(xc, conv_w, window_strides=(1,), padding=[(D_CONV - 1, 0)], feature_group_count=D_INNER, dimension_numbers=('NCH', 'OIH', 'NCH'))
            xc = xc + conv_b[None, :, None]
            u = jax.nn.silu(jnp.transpose(xc, (0, 2, 1)))
            x_dbl = jnp.einsum('bld,ed->ble', u, W_x)
            dt = x_dbl[..., :DT_RANK]
            Bm = x_dbl[..., DT_RANK:DT_RANK + D_STATE]
            Cm = x_dbl[..., DT_RANK + D_STATE:]
            dt = jnp.einsum('blr,dr->bld', dt, W_dt)
            dt = jax.nn.softplus(dt + b_dt)
            A = -jnp.exp(A_log.astype(jnp.float32))
            dA = jnp.exp(jnp.einsum('bld,dn->bldn', dt, A))
            dBu = jnp.einsum('bld,bln->bldn', dt * u, Bm)

            def step(hst, inp):
                dA_t, dBu_t, C_t = inp
                hst = dA_t * hst + dBu_t
                y_t = jnp.einsum('bdn,bn->bd', hst, C_t)
                return (hst, y_t)
            h0 = jnp.zeros((B, D_INNER, D_STATE), dt.dtype)
            _, ys = jax.lax.scan(step, h0, (jnp.swapaxes(dA, 0, 1), jnp.swapaxes(dBu, 0, 1), jnp.swapaxes(Cm, 0, 1)))
            y = jnp.swapaxes(ys, 0, 1)
            y = y + u * Dp
            y = y * jax.nn.silu(z)
            out = jnp.einsum('bld,ed->ble', y, W_out)
            return x + out
        key = jax.random.key(seed)
        ks = jax.random.split(key, 12)
        s = 0.02
        x = jax.random.normal(ks[0], (B_SZ, L_SEQ, D_MODEL), jnp.float32)
        ln_g = jnp.ones((D_MODEL,), jnp.float32)
        ln_b = jnp.zeros((D_MODEL,), jnp.float32)
        W_in = jax.random.normal(ks[1], (2 * D_INNER, D_MODEL), jnp.float32) * s
        conv_w = jax.random.normal(ks[2], (D_INNER, 1, D_CONV), jnp.float32) * 0.2
        conv_b = jax.random.normal(ks[3], (D_INNER,), jnp.float32) * 0.02
        W_x = jax.random.normal(ks[4], (DT_RANK + 2 * D_STATE, D_INNER), jnp.float32) * s
        W_dt = jax.random.normal(ks[5], (D_INNER, DT_RANK), jnp.float32) * DT_RANK ** (-0.5)
        u = jax.random.uniform(ks[6], (D_INNER,), jnp.float32)
        dt0 = jnp.exp(u * (np.log(0.1) - np.log(0.001)) + np.log(0.001))
        b_dt = dt0 + jnp.log(-jnp.expm1(-dt0))
        A_log = jnp.log(jnp.tile(jnp.arange(1, D_STATE + 1, dtype=jnp.float32), (D_INNER, 1)))
        Dp = jnp.ones((D_INNER,), jnp.float32)
        W_out = jax.random.normal(ks[7], (D_MODEL, D_INNER), jnp.float32) * s
        return {'x': x, 'ln_g': ln_g, 'ln_b': ln_b, 'W_in': W_in, 'conv_w': conv_w, 'conv_b': conv_b, 'W_x': W_x, 'W_dt': W_dt, 'b_dt': b_dt, 'A_log': A_log, 'Dp': Dp, 'W_out': W_out}
    _L0_attn_all = _L0_attn_setup()
    _L0_attn_in = {k: v for k, v in _L0_attn_all.items() if k in ('ln_g', 'ln_b', 'W_in', 'conv_w', 'conv_b', 'W_x', 'W_dt', 'b_dt', 'A_log', 'Dp', 'W_out')}
    del _L0_attn_all

    def _L0_xattn_setup():
        import jax, jax.numpy as jnp
        import numpy as np
        DIM = 256
        HEADS = 16
        HEAD_DIM = DIM // HEADS
        key = jax.random.key(seed)
        ks = jax.random.split(key, 12)
        B, Tq, Tk = (2, 512, 512)
        inp = {'query': jax.random.normal(ks[0], (B, Tq, DIM), jnp.float32), 'key': jax.random.normal(ks[1], (B, Tk, DIM), jnp.float32), 'value': jax.random.normal(ks[2], (B, Tk, DIM), jnp.float32), 'mask': jax.random.randint(ks[3], (B, 1, Tq, Tk), 0, 2, jnp.int32), 'wq': jax.random.uniform(ks[4], (DIM, DIM), jnp.float32, -1.0, 1.0) * np.sqrt(6.0 / (2 * DIM)), 'wk': jax.random.uniform(ks[5], (DIM, DIM), jnp.float32, -1.0, 1.0) * np.sqrt(6.0 / (2 * DIM)), 'wv': jax.random.uniform(ks[6], (DIM, DIM), jnp.float32, -1.0, 1.0) * np.sqrt(6.0 / (2 * DIM)), 'wo': jax.random.uniform(ks[7], (DIM, DIM), jnp.float32, -1.0, 1.0) * np.sqrt(6.0 / (2 * DIM)), 'bq': jnp.zeros((DIM,), jnp.float32), 'bk': jnp.zeros((DIM,), jnp.float32), 'bv': jnp.zeros((DIM,), jnp.float32), 'bo': jnp.zeros((DIM,), jnp.float32)}
        return inp
    _L0_xattn_all = _L0_xattn_setup()
    _L0_xattn_in = {k: v for k, v in _L0_xattn_all.items() if k in ('wq', 'wk', 'wv', 'wo', 'bq', 'bk', 'bv', 'bo')}
    del _L0_xattn_all

    def _L0_ffn_setup():
        import jax, jax.numpy as jnp
        import numpy as np
        EMB = 256
        FF = 4 * EMB

        def _ternary(w):
            scale = jnp.maximum(jnp.mean(jnp.abs(w)), 1e-08)
            w_t = jnp.clip(jnp.round(w / scale), -1.0, 1.0)
            return w + jax.lax.stop_gradient(w_t - w)
        key = jax.random.key(seed)
        kx, k1, k2, kb1, kb2 = jax.random.split(key, 5)
        x = jax.random.normal(kx, (4, 512, EMB), dtype=jnp.float32)
        lim1 = 1.0 / np.sqrt(EMB)
        lim2 = 1.0 / np.sqrt(FF)
        W1 = jax.random.uniform(k1, (FF, EMB), jnp.float32, -lim1, lim1)
        b1 = jax.random.uniform(kb1, (FF,), jnp.float32, -lim1, lim1)
        W2 = jax.random.uniform(k2, (EMB, FF), jnp.float32, -lim2, lim2)
        b2 = jax.random.uniform(kb2, (EMB,), jnp.float32, -lim2, lim2)
        return {'x': x, 'W1': W1, 'b1': b1, 'W2': W2, 'b2': b2}
    _L0_ffn_all = _L0_ffn_setup()
    _L0_ffn_in = {k: v for k, v in _L0_ffn_all.items() if k in ('W1', 'b1', 'W2', 'b2')}
    del _L0_ffn_all

    def _L1_attn_setup():
        import jax, jax.numpy as jnp
        import numpy as np
        N_EMBD = 256
        N_HEAD = 16
        HEAD_SIZE = 64
        LN_EPS = 0.001
        key = jax.random.key(seed)
        ks = jax.random.split(key, 7)
        B, S, D, H, E = (4, 512, N_EMBD, N_HEAD, HEAD_SIZE)
        x = jax.random.normal(ks[0], (B, S, D), dtype=jnp.float32)
        scale = 1.0 / np.sqrt(D)
        Wq = jax.random.normal(ks[1], (H, D, E), dtype=jnp.float32) * scale
        Wk = jax.random.normal(ks[2], (H, D, E), dtype=jnp.float32) * scale
        Wv = jax.random.normal(ks[3], (H, D, E), dtype=jnp.float32) * scale
        Wo = jax.random.normal(ks[4], (H * E, D), dtype=jnp.float32) * scale
        gamma = jnp.ones((D,), dtype=jnp.float32)
        beta = jnp.zeros((D,), dtype=jnp.float32)
        return {'x': x, 'Wq': Wq, 'Wk': Wk, 'Wv': Wv, 'Wo': Wo, 'gamma': gamma, 'beta': beta}
    _L1_attn_all = _L1_attn_setup()
    _L1_attn_in = {k: v for k, v in _L1_attn_all.items() if k in ('Wq', 'Wk', 'Wv', 'Wo', 'gamma', 'beta')}
    del _L1_attn_all

    def _L1_xattn_setup():
        import jax, jax.numpy as jnp
        import numpy as np
        LN_EPS = 1e-05

        def layer_norm(x, w, b):
            mu = jnp.mean(x, axis=-1, keepdims=True)
            var = jnp.mean(jnp.square(x - mu), axis=-1, keepdims=True)
            return (x - mu) * jax.lax.rsqrt(var + LN_EPS) * w + b
        key = jax.random.key(seed)
        ks = jax.random.split(key, 8)
        B, F, Q, D = (8, 1024, 64, 256)
        H, DH = (16, 64)
        inner = H * DH
        s = 1.0 / np.sqrt(D)
        return {'features': jax.random.normal(ks[0], (B, F, D), jnp.float32), 'latents': jax.random.normal(ks[1], (B, Q, D), jnp.float32), 'key_attention_mask': jax.random.randint(ks[2], (B, F), 0, 2, jnp.int32), 'ln_m_w': jnp.ones((D,), jnp.float32), 'ln_m_b': jnp.zeros((D,), jnp.float32), 'ln_l_w': jnp.ones((D,), jnp.float32), 'ln_l_b': jnp.zeros((D,), jnp.float32), 'Wq': jax.random.normal(ks[3], (D, inner), jnp.float32) * s, 'Wk': jax.random.normal(ks[4], (D, inner), jnp.float32) * s, 'Wv': jax.random.normal(ks[5], (D, inner), jnp.float32) * s, 'Wo': jax.random.normal(ks[6], (inner, D), jnp.float32) * (1.0 / np.sqrt(inner))}
    _L1_xattn_all = _L1_xattn_setup()
    _L1_xattn_in = {k: v for k, v in _L1_xattn_all.items() if k in ('ln_m_w', 'ln_m_b', 'ln_l_w', 'ln_l_b', 'Wq', 'Wk', 'Wv', 'Wo')}
    del _L1_xattn_all

    def _L1_ffn_setup():
        import jax, jax.numpy as jnp
        import numpy as np
        BLOCK = 32
        W_BITS = 4
        ACT_BITS = 16

        def act_qdq(x):
            qmax = 2.0 ** (ACT_BITS - 1) - 1.0
            scale = jnp.maximum(jnp.max(jnp.abs(x)) / qmax, 1e-12)
            return jnp.clip(jnp.round(x / scale), -qmax - 1.0, qmax) * scale

        def fixed_qdq_u16(x):
            scale = 1.0 / 65536.0
            return jnp.clip(jnp.round(x / scale), 0.0, 65535.0) * scale

        def lpbq_dequant(w):
            O, I = w.shape
            qmax = 2.0 ** (W_BITS - 1) - 1.0
            wb = w.reshape(O, I // BLOCK, BLOCK)
            s = jnp.maximum(jnp.max(jnp.abs(wb), axis=-1, keepdims=True) / qmax, 1e-12)
            wq = jnp.clip(jnp.round(wb / s), -qmax - 1.0, qmax) * s
            return wq.reshape(O, I)
        key = jax.random.key(seed)
        k1, k2, k3, k4 = jax.random.split(key, 4)
        B, S, H, I = (2, 1024, 256, 768)
        x = jax.random.normal(k1, (B, S, H), jnp.float32)
        w_gate = jax.random.normal(k2, (I, H), jnp.float32) * 0.02
        w_up = jax.random.normal(k3, (I, H), jnp.float32) * 0.02
        w_down = jax.random.normal(k4, (H, I), jnp.float32) * 0.02
        return {'x': x, 'w_gate': w_gate, 'w_up': w_up, 'w_down': w_down}
    _L1_ffn_all = _L1_ffn_setup()
    _L1_ffn_in = {k: v for k, v in _L1_ffn_all.items() if k in ('w_gate', 'w_up', 'w_down')}
    del _L1_ffn_all
    return {'x': x, 'ctx_1024': ctx_1024, 'mask_Bx1xSxS2_ik1': mask_Bx1xSxS2_ik1, 'mask_BxS2_ik0': mask_BxS2_ik0, 'L0_attn_ln_g': _L0_attn_in['ln_g'], 'L0_attn_ln_b': _L0_attn_in['ln_b'], 'L0_attn_W_in': _L0_attn_in['W_in'], 'L0_attn_conv_w': _L0_attn_in['conv_w'], 'L0_attn_conv_b': _L0_attn_in['conv_b'], 'L0_attn_W_x': _L0_attn_in['W_x'], 'L0_attn_W_dt': _L0_attn_in['W_dt'], 'L0_attn_b_dt': _L0_attn_in['b_dt'], 'L0_attn_A_log': _L0_attn_in['A_log'], 'L0_attn_Dp': _L0_attn_in['Dp'], 'L0_attn_W_out': _L0_attn_in['W_out'], 'L0_xattn_wq': _L0_xattn_in['wq'], 'L0_xattn_wk': _L0_xattn_in['wk'], 'L0_xattn_wv': _L0_xattn_in['wv'], 'L0_xattn_wo': _L0_xattn_in['wo'], 'L0_xattn_bq': _L0_xattn_in['bq'], 'L0_xattn_bk': _L0_xattn_in['bk'], 'L0_xattn_bv': _L0_xattn_in['bv'], 'L0_xattn_bo': _L0_xattn_in['bo'], 'L0_ffn_W1': _L0_ffn_in['W1'], 'L0_ffn_b1': _L0_ffn_in['b1'], 'L0_ffn_W2': _L0_ffn_in['W2'], 'L0_ffn_b2': _L0_ffn_in['b2'], 'L1_attn_Wq': _L1_attn_in['Wq'], 'L1_attn_Wk': _L1_attn_in['Wk'], 'L1_attn_Wv': _L1_attn_in['Wv'], 'L1_attn_Wo': _L1_attn_in['Wo'], 'L1_attn_gamma': _L1_attn_in['gamma'], 'L1_attn_beta': _L1_attn_in['beta'], 'L1_xattn_ln_m_w': _L1_xattn_in['ln_m_w'], 'L1_xattn_ln_m_b': _L1_xattn_in['ln_m_b'], 'L1_xattn_ln_l_w': _L1_xattn_in['ln_l_w'], 'L1_xattn_ln_l_b': _L1_xattn_in['ln_l_b'], 'L1_xattn_Wq': _L1_xattn_in['Wq'], 'L1_xattn_Wk': _L1_xattn_in['Wk'], 'L1_xattn_Wv': _L1_xattn_in['Wv'], 'L1_xattn_Wo': _L1_xattn_in['Wo'], 'L1_ffn_w_gate': _L1_ffn_in['w_gate'], 'L1_ffn_w_up': _L1_ffn_in['w_up'], 'L1_ffn_w_down': _L1_ffn_in['w_down']}

def reference(x, ctx_1024, mask_Bx1xSxS2_ik1, mask_BxS2_ik0, L0_attn_ln_g, L0_attn_ln_b, L0_attn_W_in, L0_attn_conv_w, L0_attn_conv_b, L0_attn_W_x, L0_attn_W_dt, L0_attn_b_dt, L0_attn_A_log, L0_attn_Dp, L0_attn_W_out, L0_xattn_wq, L0_xattn_wk, L0_xattn_wv, L0_xattn_wo, L0_xattn_bq, L0_xattn_bk, L0_xattn_bv, L0_xattn_bo, L0_ffn_W1, L0_ffn_b1, L0_ffn_W2, L0_ffn_b2, L1_attn_Wq, L1_attn_Wk, L1_attn_Wv, L1_attn_Wo, L1_attn_gamma, L1_attn_beta, L1_xattn_ln_m_w, L1_xattn_ln_m_b, L1_xattn_ln_l_w, L1_xattn_ln_l_b, L1_xattn_Wq, L1_xattn_Wk, L1_xattn_Wv, L1_xattn_Wo, L1_ffn_w_gate, L1_ffn_w_up, L1_ffn_w_down):
    import jax
    import jax.numpy as jnp

    def _L0_attn_ref(x, ln_g, ln_b, W_in, conv_w, conv_b, W_x, W_dt, b_dt, A_log, Dp, W_out):
        import jax, jax.numpy as jnp
        import numpy as np
        D_MODEL = 256
        D_INNER = 2 * D_MODEL
        D_STATE = 16
        D_CONV = 4
        DT_RANK = (D_MODEL + 15) // 16
        B_SZ, L_SEQ = (2, 512)
        LN_EPS = 1e-06

        def _mamba_block(x, ln_g, ln_b, W_in, conv_w, conv_b, W_x, W_dt, b_dt, A_log, Dp, W_out):
            B, L, D = x.shape
            mu = jnp.mean(x, axis=-1, keepdims=True)
            var = jnp.mean(jnp.square(x - mu), axis=-1, keepdims=True)
            h = (x - mu) * jax.lax.rsqrt(var + LN_EPS) * ln_g + ln_b
            xz = jnp.einsum('bld,ed->ble', h, W_in)
            xi, z = jnp.split(xz, 2, axis=-1)
            xc = jnp.transpose(xi, (0, 2, 1))
            xc = jax.lax.conv_general_dilated(xc, conv_w, window_strides=(1,), padding=[(D_CONV - 1, 0)], feature_group_count=D_INNER, dimension_numbers=('NCH', 'OIH', 'NCH'))
            xc = xc + conv_b[None, :, None]
            u = jax.nn.silu(jnp.transpose(xc, (0, 2, 1)))
            x_dbl = jnp.einsum('bld,ed->ble', u, W_x)
            dt = x_dbl[..., :DT_RANK]
            Bm = x_dbl[..., DT_RANK:DT_RANK + D_STATE]
            Cm = x_dbl[..., DT_RANK + D_STATE:]
            dt = jnp.einsum('blr,dr->bld', dt, W_dt)
            dt = jax.nn.softplus(dt + b_dt)
            A = -jnp.exp(A_log.astype(jnp.float32))
            dA = jnp.exp(jnp.einsum('bld,dn->bldn', dt, A))
            dBu = jnp.einsum('bld,bln->bldn', dt * u, Bm)

            def step(hst, inp):
                dA_t, dBu_t, C_t = inp
                hst = dA_t * hst + dBu_t
                y_t = jnp.einsum('bdn,bn->bd', hst, C_t)
                return (hst, y_t)
            h0 = jnp.zeros((B, D_INNER, D_STATE), dt.dtype)
            _, ys = jax.lax.scan(step, h0, (jnp.swapaxes(dA, 0, 1), jnp.swapaxes(dBu, 0, 1), jnp.swapaxes(Cm, 0, 1)))
            y = jnp.swapaxes(ys, 0, 1)
            y = y + u * Dp
            y = y * jax.nn.silu(z)
            out = jnp.einsum('bld,ed->ble', y, W_out)
            return x + out
        return _mamba_block(x, ln_g, ln_b, W_in, conv_w, conv_b, W_x, W_dt, b_dt, A_log, Dp, W_out)

    def _L0_xattn_ref(query, key, value, mask, wq, wk, wv, wo, bq, bk, bv, bo):
        import jax, jax.numpy as jnp
        import numpy as np
        DIM = 256
        HEADS = 16
        HEAD_DIM = DIM // HEADS
        B, Tq, C = query.shape
        Tk = key.shape[1]
        scale = 1.0 / np.sqrt(HEAD_DIM)
        q = (query @ wq.T + bq).reshape(B, Tq, HEADS, HEAD_DIM).transpose(0, 2, 1, 3)
        k = (key @ wk.T + bk).reshape(B, Tk, HEADS, HEAD_DIM).transpose(0, 2, 1, 3)
        v = (value @ wv.T + bv).reshape(B, Tk, HEADS, HEAD_DIM).transpose(0, 2, 1, 3)
        scores = jnp.einsum('bhqd,bhkd->bhqk', q, k) * scale
        scores = jnp.clip(scores, -100.0, 100.0)
        scores = jnp.where(mask == 0, -jnp.inf, scores)
        attn = jax.nn.softmax(scores, axis=-1)
        out = jnp.einsum('bhqk,bhkd->bhqd', attn, v)
        out = out.transpose(0, 2, 1, 3).reshape(B, Tq, HEADS * HEAD_DIM)
        return out @ wo.T + bo

    def _L0_ffn_ref(x, W1, b1, W2, b2):
        import jax, jax.numpy as jnp
        import numpy as np
        EMB = 256
        FF = 4 * EMB

        def _ternary(w):
            scale = jnp.maximum(jnp.mean(jnp.abs(w)), 1e-08)
            w_t = jnp.clip(jnp.round(w / scale), -1.0, 1.0)
            return w + jax.lax.stop_gradient(w_t - w)
        h = jnp.einsum('bsd,fd->bsf', x, _ternary(W1)) + b1
        h = jax.nn.gelu(h, approximate=False)
        out = jnp.einsum('bsf,df->bsd', h, _ternary(W2)) + b2
        return out

    def _L1_attn_ref(x, Wq, Wk, Wv, Wo, gamma, beta):
        import jax, jax.numpy as jnp
        import numpy as np
        N_EMBD = 256
        N_HEAD = 16
        HEAD_SIZE = 64
        LN_EPS = 0.001
        B, S, D = x.shape
        H, _, E = Wq.shape
        q = jnp.einsum('bsd,hde->bhse', x, Wq)
        k = jnp.einsum('bsd,hde->bhse', x, Wk)
        v = jnp.einsum('bsd,hde->bhse', x, Wv)
        scores = jnp.einsum('bhse,bhte->bhst', q, k)
        causal = jnp.tril(jnp.ones((S, S), dtype=bool))
        scores = jnp.where(causal, scores / jnp.sqrt(jnp.float32(E)), jnp.float32(-jnp.inf))
        attn = jax.nn.softmax(scores, axis=-1)
        out = jnp.einsum('bhst,bhte->bhse', attn, v)
        heads = out.transpose(0, 2, 1, 3).reshape(B, S, H * E)
        y = x + heads @ Wo
        mu = jnp.mean(y, axis=-1, keepdims=True)
        var = jnp.mean(jnp.square(y - mu), axis=-1, keepdims=True)
        y = (y - mu) * jax.lax.rsqrt(var + LN_EPS) * gamma + beta
        return y

    def _L1_xattn_ref(features, latents, key_attention_mask, ln_m_w, ln_m_b, ln_l_w, ln_l_b, Wq, Wk, Wv, Wo):
        import jax, jax.numpy as jnp
        import numpy as np
        LN_EPS = 1e-05

        def layer_norm(x, w, b):
            mu = jnp.mean(x, axis=-1, keepdims=True)
            var = jnp.mean(jnp.square(x - mu), axis=-1, keepdims=True)
            return (x - mu) * jax.lax.rsqrt(var + LN_EPS) * w + b
        H, DH = (16, 64)
        B, F, D = features.shape
        Q = latents.shape[1]
        scale = DH ** (-0.5)
        x = layer_norm(features, ln_m_w, ln_m_b)
        lat = layer_norm(latents, ln_l_w, ln_l_b)
        q = (lat @ Wq).reshape(B, Q, H, DH).transpose(0, 2, 1, 3)
        kv_in = jnp.concatenate([x, lat], axis=1)
        k = (kv_in @ Wk).reshape(B, F + Q, H, DH).transpose(0, 2, 1, 3)
        v = (kv_in @ Wv).reshape(B, F + Q, H, DH).transpose(0, 2, 1, 3)
        q = q * scale
        sim = jnp.einsum('bhqd,bhfd->bhqf', q, k)
        full_mask = jnp.concatenate([key_attention_mask, jnp.ones((B, Q), key_attention_mask.dtype)], axis=1)
        sim = jnp.where(full_mask[:, None, None, :] == 0, -jnp.inf, sim)
        sim = sim - jax.lax.stop_gradient(jnp.max(sim, axis=-1, keepdims=True))
        alphas = jax.nn.softmax(sim, axis=-1)
        out = jnp.einsum('bhqf,bhfv->bhqv', alphas, v)
        out = out.transpose(0, 2, 1, 3).reshape(B, Q, H * DH)
        return out @ Wo

    def _L1_ffn_ref(x, w_gate, w_up, w_down):
        import jax, jax.numpy as jnp
        import numpy as np
        BLOCK = 32
        W_BITS = 4
        ACT_BITS = 16

        def act_qdq(x):
            qmax = 2.0 ** (ACT_BITS - 1) - 1.0
            scale = jnp.maximum(jnp.max(jnp.abs(x)) / qmax, 1e-12)
            return jnp.clip(jnp.round(x / scale), -qmax - 1.0, qmax) * scale

        def fixed_qdq_u16(x):
            scale = 1.0 / 65536.0
            return jnp.clip(jnp.round(x / scale), 0.0, 65535.0) * scale

        def lpbq_dequant(w):
            O, I = w.shape
            qmax = 2.0 ** (W_BITS - 1) - 1.0
            wb = w.reshape(O, I // BLOCK, BLOCK)
            s = jnp.maximum(jnp.max(jnp.abs(wb), axis=-1, keepdims=True) / qmax, 1e-12)
            wq = jnp.clip(jnp.round(wb / s), -qmax - 1.0, qmax) * s
            return wq.reshape(O, I)
        x = act_qdq(x)
        up = act_qdq(x @ lpbq_dequant(w_up).T)
        gate = act_qdq(x @ lpbq_dequant(w_gate).T)
        sig = fixed_qdq_u16(jax.nn.sigmoid(gate))
        gate = act_qdq(gate * sig)
        o = act_qdq(gate * up)
        return o @ lpbq_dequant(w_down).T
    x = _layernorm(x + _L0_attn_ref(x, L0_attn_ln_g, L0_attn_ln_b, L0_attn_W_in, L0_attn_conv_w, L0_attn_conv_b, L0_attn_W_x, L0_attn_W_dt, L0_attn_b_dt, L0_attn_A_log, L0_attn_Dp, L0_attn_W_out), axis=-1)
    x = _layernorm(x + _L0_xattn_ref(x, ctx_1024, ctx_1024, mask_Bx1xSxS2_ik1, L0_xattn_wq, L0_xattn_wk, L0_xattn_wv, L0_xattn_wo, L0_xattn_bq, L0_xattn_bk, L0_xattn_bv, L0_xattn_bo), axis=-1)
    x = _layernorm(x + _L0_ffn_ref(x, L0_ffn_W1, L0_ffn_b1, L0_ffn_W2, L0_ffn_b2), axis=-1)
    x = _layernorm(x + _L1_attn_ref(x, L1_attn_Wq, L1_attn_Wk, L1_attn_Wv, L1_attn_Wo, L1_attn_gamma, L1_attn_beta), axis=-1)
    x = _layernorm(x + _L1_xattn_ref(ctx_1024, x, mask_BxS2_ik0, L1_xattn_ln_m_w, L1_xattn_ln_m_b, L1_xattn_ln_l_w, L1_xattn_ln_l_b, L1_xattn_Wq, L1_xattn_Wk, L1_xattn_Wv, L1_xattn_Wo), axis=-1)
    x = _layernorm(x + _L1_ffn_ref(x, L1_ffn_w_gate, L1_ffn_w_up, L1_ffn_w_down), axis=-1)
    return x

_drawn_inputs = setup_inputs


def setup_inputs(seed=0):
    import zlib

    import numpy as np

    out = dict(_drawn_inputs(seed))
    spreads = {'L0_attn_ln_g': (1.0, 0.6),
     'L0_attn_ln_b': (0.0, 0.8),
     'L0_attn_Dp': (1.0, 0.6),
     'L0_xattn_bq': (0.0, 0.367),
     'L0_xattn_bk': (0.0, 0.8),
     'L0_xattn_bv': (0.0, 0.1),
     'L0_xattn_bo': (0.0, 0.1),
     'L1_attn_gamma': (1.0, 0.2),
     'L1_attn_beta': (0.0, 0.1),
     'L1_xattn_ln_m_w': (1.0, 0.6),
     'L1_xattn_ln_m_b': (0.0, 0.771),
     'L1_xattn_ln_l_w': (1.0, 0.2),
     'L1_xattn_ln_l_b': (0.0, 0.1)}
    factors = {'L0_attn_W_in': 8.0,
     'L0_attn_conv_w': 8.0,
     'L0_attn_conv_b': 8.0,
     'L0_attn_W_x': 8.0,
     'L0_attn_W_dt': 8.0,
     'L0_attn_b_dt': 8.0,
     'L0_attn_A_log': 8.0,
     'L0_attn_W_out': 8.0,
     'L0_ffn_b1': 8.0,
     'L0_ffn_b2': 8.0}
    for name, (base, spread) in spreads.items():
        noise = np.random.default_rng([zlib.crc32(name.encode()), seed]).standard_normal(out[name].shape)
        drawn = base * np.exp(spread * noise) if base else spread * noise
        out[name] = jnp.asarray(drawn.astype(out[name].dtype))
    for name, factor in factors.items():
        out[name] = (out[name] * factor).astype(out[name].dtype)
    return out
```

```python
from contextlib import ExitStack

import concourse.bass as bass
from concourse import mybir

F32 = mybir.dt.float32
BF16 = mybir.dt.bfloat16
I32 = mybir.dt.int32
I16 = mybir.dt.int16
U16 = mybir.dt.uint16
ALU = mybir.AluOpType
ACT = mybir.ActivationFunctionType
AX = mybir.AxisListType
RMAX = bass.bass_isa.ReduceOp.max
RADD = bass.bass_isa.ReduceOp.add

P = 128
BANK = 512
NEG = -1e30
RNE = 12582912.0
EXP_LN = "natural_log_exp_and_others"


class Later:

    def __init__(self, engine):
        self.engine = engine

    def matmul(self, *a, **k):
        return lambda: self.engine.matmul(*a, **k)

    def transpose(self, *a, **k):
        return lambda: self.engine.transpose(*a, **k)

    def activation(self, *a, **k):
        return lambda: self.engine.activation(*a, **k)

    def preload_act_table_set(self, *a, **k):
        return lambda: self.engine.preload_act_table_set(*a, **k)

    def memset(self, *a, **k):
        return lambda: self.engine.memset(*a, **k)

    def tensor_copy(self, *a, **k):
        return lambda: self.engine.tensor_copy(*a, **k)

    def tensor_tensor(self, *a, **k):
        return lambda: self.engine.tensor_tensor(*a, **k)

    def tensor_scalar(self, *a, **k):
        return lambda: self.engine.tensor_scalar(*a, **k)

    def scalar_tensor_tensor(self, *a, **k):
        return lambda: self.engine.scalar_tensor_tensor(*a, **k)

    def tensor_tensor_scan(self, *a, **k):
        return lambda: self.engine.tensor_tensor_scan(*a, **k)

    def tensor_reduce(self, *a, **k):
        return lambda: self.engine.tensor_reduce(*a, **k)

    def reciprocal(self, *a, **k):
        return lambda: self.engine.reciprocal(*a, **k)

    def bn_stats(self, *a, **k):
        return lambda: self.engine.bn_stats(*a, **k)

    def bn_aggr(self, *a, **k):
        return lambda: self.engine.bn_aggr(*a, **k)

    def affine_select(self, *a, **k):
        return lambda: self.engine.affine_select(*a, **k)

    def partition_all_reduce(self, *a, **k):
        return lambda: self.engine.partition_all_reduce(*a, **k)

    def copy_predicated(self, *a, **k):
        return lambda: self.engine.copy_predicated(*a, **k)

    def dma_start(self, *a, **k):
        return lambda: self.engine.dma_start(*a, **k)


class Step:

    def __init__(self, issue, after):
        self.issue, self.after = issue, after
        self.sem, self.value, self.amount, self.wanted = None, 0, 1, False


class Queue:

    def __init__(self, engine, sem):
        self.later, self.sem, self.steps = Later(engine), sem, []

    def __call__(self, instruction, *after):
        step = Step(instruction(self.later), [a for a in after if a is not None])
        for a in step.after:
            a.wanted = True
        self.steps.append(step)
        return step

    def dma(self, counter, out, in_, *after):
        step = self(lambda e: e.dma_start(out, in_), *after)
        counter.count += 16
        step.sem, step.value, step.amount, step.wanted = counter.sem, counter.count, 16, True
        return step

    def number(self):
        count = 0
        for s in self.steps:
            if s.wanted and s.sem is None:
                count += 1
                s.sem, s.value = self.sem, count

    def emit(self, engine):
        reached = {}
        for s in self.steps:
            for a in s.after:
                if reached.get(id(a.sem), 0) < a.value:
                    engine.wait_ge(a.sem, a.value)
                    reached[id(a.sem)] = a.value
            made = s.issue()
            if s.wanted:
                made.then_inc(s.sem, s.amount)


class Counter:

    def __init__(self, sem):
        self.sem, self.count = sem, 0


class Slot:

    def __init__(self, ap, free=None):
        self.ap, self.free = ap, free


class Ring:

    def __init__(self, slots):
        self.slots, self.at = slots, -1

    def next(self):
        self.at = (self.at + 1) % len(self.slots)
        return self.slots[self.at]


def interleave(strands):
    lengths = [w for w, _ in strands]
    live = [[0.0, 1.0 / w, g] for w, g in strands]
    while live:
        live.sort(key=lambda s: s[0])
        s = live[0]
        try:
            next(s[2])
            s[0] += s[1]
        except StopIteration:
            live.pop(0)


def decoder_kernel(nc, I, out):
    B, T, D = I["x"].shape
    S2 = I["ctx"].shape[1]
    NT, ND = T // P, D // P
    DI = I["m_w_out"].shape[0]
    NI = DI // P
    NS = I["m_a_log"].shape[1]
    DR = I["m_w_dt"].shape[0]
    KC = I["m_conv_w"].shape[1]
    H = 16
    HD0 = D // H
    F0 = I["f_w1"].shape[1]
    NF0 = F0 // P
    E = I["a_wq"].shape[1]
    HD = E // H
    NE = E // P
    F1 = I["g_gate"].shape[0]
    NF1 = F1 // P
    KEYS = T + S2
    NK = 3
    assert T == 2 * P and D == 2 * P and HD == 64 and NS == 16 and KEYS < NK * P

    ctx = ExitStack()
    with ctx:
        def counter(name):
            return Counter(ctx.enter_context(nc.semaphore(name)))

        pe, dve, act, pool, sync = (
            Queue(engine, ctx.enter_context(nc.semaphore(n))) for engine, n in (
                (nc.tensor, "pe_done"), (nc.vector, "dve_done"), (nc.scalar, "act_done"),
                (nc.gpsimd, "pool_done"), (nc.sync, "sync_done")))
        const_load = counter("const_load")
        weight_load = [counter(f"weight_load{i}") for i in range(8)]
        x_load, ctx_load, mask_load, spill = (counter(n) for n in ("x_load", "ctx_load", "mask_load", "spill"))
        reload_rows, final_rows = ([counter(f"{n}{i}") for i in range(3)] for n in ("reload_rows", "final_rows"))

        def sb(scope, name, shape, dt=F32):
            return scope.enter_context(nc.sbuf_tensor(name, shape, dt))

        banks = [ctx.enter_context(nc.psum_tensor(f"bank{i}", [P, BANK], F32)) for i in range(8)]
        x5_dram = nc.dram_tensor("x5_spill", (B, T, D), F32)
        x5_dram = x5_dram.ap() if hasattr(x5_dram, "ap") else x5_dram

        ident = sb(ctx, "ident", [P, P])
        zeroed = dve(lambda e: e.memset(ident[:], 0.0))
        ident_ready = pool(lambda e: e.affine_select(
            out=ident[:], in_=ident[:], compare_op=ALU.not_equal, fill=1.0, base=0,
            pattern=[[-1, P]], channel_multiplier=1), zeroed)
        amax5 = sb(ctx, "amax5", [P, B])

        def layernorm(scope_tiles, src, dst, eps, rows, tiles, *after, eng2=None):
            st, mv, r, t = scope_tiles
            n = tiles
            for i in range(n):
                s = dve(lambda e: e.bn_stats(st[0:rows, i, :], src(i)), *after)
            for i in range(n):
                s = dve(lambda e: e.bn_aggr(mv[0:rows, i, :], st[0:rows, i, :]), s)
            v = mv[0:rows, 0:n, 1]
            s0 = dve(lambda e: e.tensor_scalar(t[0:rows, 3, 0:n], v, eps, None, ALU.add), s)
            s1 = act(lambda e: e.activation(t[0:rows, 0, 0:n], t[0:rows, 3, 0:n], ACT.Ln), s0)
            s2 = act(lambda e: e.activation(r[0:rows, 0:n], t[0:rows, 0, 0:n], ACT.Exp, scale=-0.5), s1)
            s3 = dve(lambda e: e.tensor_tensor(t[0:rows, 1, 0:n], r[0:rows, 0:n], r[0:rows, 0:n], ALU.mult), s2)
            s4 = dve(lambda e: e.tensor_tensor(t[0:rows, 2, 0:n], t[0:rows, 1, 0:n], t[0:rows, 3, 0:n], ALU.mult), s3)
            s5 = dve(lambda e: e.tensor_scalar(t[0:rows, 2, 0:n], t[0:rows, 2, 0:n], -0.5, 1.5, ALU.mult, ALU.add), s4)
            s6 = dve(lambda e: e.tensor_tensor(r[0:rows, 0:n], r[0:rows, 0:n], t[0:rows, 2, 0:n], ALU.mult), s5)
            for i in range(n):
                s = dve(lambda e: e.tensor_scalar(dst(i), src(i), mv[0:rows, i, 0:1], r[0:rows, i:i + 1],
                                                       ALU.subtract, ALU.mult), s6)
            return s

        def norm_tiles(scope, name, n):
            return (sb(scope, name + "_st", [P, n, 6]), sb(scope, name + "_mv", [P, n, 2]),
                    sb(scope, name + "_r", [P, n]), sb(scope, name + "_t", [P, 4, n]))

        ph1 = ctx.enter_context(ExitStack())
        W = {}

        def weight(name, shape, src, load=0):
            W[name] = sb(ph1, name + "_sb", shape)
            return sync.dma(weight_load[load], W[name][:], src)

        def chunks(ap):
            return ap.rearrange("(c p) n -> p c n", p=P)

        weight("m_w_in", [P, ND, 2 * DI], chunks(I["m_w_in"]))
        weight("m_w_x", [P, NI, DR + 2 * NS], chunks(I["m_w_x"]))
        weight("m_w_dt", [DR, DI], I["m_w_dt"])
        weight("m_w_out", [P, NI, D], chunks(I["m_w_out"]))
        weight("m_conv_w", [P, NI, KC], chunks(I["m_conv_w"]))
        weight("m_a_log", [P, NI, NS], chunks(I["m_a_log"]))
        for n in ("m_conv_b", "m_b_dt", "m_dp"):
            weight(n, [P, NI], I[n])
        for n in ("m_ln_g", "m_ln_b"):
            mamba_loaded = weight(n, [P, ND], I[n])
        for n in ("c_wq", "c_wk", "c_wv", "c_wo"):
            weight(n, [P, ND, D], chunks(I[n]), 1)
        for n in ("c_bq", "c_bk"):
            weight(n, [P, ND], I[n], 1)
        for n in ("c_bv", "c_bo"):
            cross_loaded = weight(n, [P, D], I[n].partition_broadcast(P), 1)
        weight("f_w1", [P, ND, F0], chunks(I["f_w1"]), 2)
        weight("f_b1", [P, NF0], I["f_b1"], 2)
        weight("f_b2", [P, D], I["f_b2"].partition_broadcast(P), 2)
        ffn_loaded = weight("f_w2", [P, NF0, D], chunks(I["f_w2"]), 2)
        for n in ("a_wq", "a_wk", "a_wv"):
            weight(n, [P, ND, E], chunks(I[n]), 3)
        weight("a_wo", [P, NE, D], chunks(I["a_wo"]), 3)
        for n in ("a_gamma", "a_beta"):
            attn_loaded = weight(n, [P, D], I[n].partition_broadcast(P), 3)
        for n in ("p_wq", "p_wk", "p_wv"):
            weight(n, [P, ND, E], chunks(I[n]), 4)
        weight("p_wo", [P, NE, D], chunks(I["p_wo"]), 4)
        for n in ("p_ln_m_w", "p_ln_m_b", "p_ln_l_w", "p_ln_l_b"):
            perc_loaded = weight(n, [P, ND], I[n], 4)

        a_neg = sb(ph1, "a_neg", [P, NI, NS])
        w_bc = sb(ph1, "w_bc", [P, NI, 3, 2 * NS])
        sel = sb(ph1, "sel", [P, P], BF16)
        ident_bf = sb(ph1, "ident_bf", [P, P], BF16)
        causal = sb(ph1, "causal", [P, P], BF16)
        head_of = sb(ph1, "head_of", [P, P // HD0])
        ones_bf = sb(ph1, "ones_bf", [1, P], BF16)

        a_exp = act(lambda e: e.activation(a_neg[:], W["m_a_log"][:], ACT.Exp), mamba_loaded)
        a_ready = dve(lambda e: e.tensor_scalar(a_neg[:], a_neg[:], -1.0, None, ALU.mult), a_exp)
        for r in range(3):
            bc_w_ready = dve(lambda e: e.tensor_copy(w_bc[:, :, r, :], W["m_w_x"][:, :, DR:DR + 2 * NS]), mamba_loaded)
        ident_bf_ready = dve(lambda e: e.tensor_copy(ident_bf[:], ident[:]), ident_ready)
        s = dve(lambda e: e.tensor_tensor(sel[:, 0:2 * NS], ident[:, 0:2 * NS], ident[:, 2 * NS:4 * NS], ALU.add), ident_ready)
        sel_ready = dve(lambda e: e.tensor_tensor(sel[:, 0:2 * NS], sel[:, 0:2 * NS], ident[:, 4 * NS:6 * NS], ALU.add), s)
        s = dve(lambda e: e.memset(causal[:], 0.0))
        causal_ready = pool(lambda e: e.affine_select(
            out=causal[:], in_=causal[:], compare_op=ALU.is_ge, fill=NEG, base=0,
            pattern=[[-1, P]], channel_multiplier=1), s)
        heads_ready = dve(lambda e: e.tensor_reduce(
            head_of[:], ident[:].rearrange("p (h d) -> p h d", d=HD0), AX.X, ALU.add), ident_ready)
        ones_ready = dve(lambda e: e.memset(ones_bf[:], 1.0))

        x_in = Slot(sb(ph1, "x_in", [P, NT, D]))
        m_tmp = sb(ph1, "m_tmp", [P, NI, T])
        m_hT = m_tmp[:, 0:ND, :]
        m_rows = m_tmp[:, ND:NI, :]
        xi_pad = sb(ph1, "xi_pad", [P, NI, KC - 1 + T])
        zT = sb(ph1, "zT", [P, NI, T])
        uT = sb(ph1, "uT", [P, NI, T])
        dtT = sb(ph1, "dtT", [P, NI, T])
        dtuT = sb(ph1, "dtuT", [P, NI, T])
        dt_low = sb(ph1, "dt_low", [DR, T])
        bc_split = sb(ph1, "bc_split", [6 * NS, T], BF16)
        decay = [Slot(sb(ph1, f"decay{i}", [P, 2, T])) for i in range(3)]
        state = [Slot(sb(ph1, f"state{i}", [P, 2, T])) for i in range(NI)]
        y_sum = sb(ph1, "y_sum", [P, NI, 2, T])
        m_norm = norm_tiles(ph1, "m_norm", NT)
        m_work, bank_b, bank_c = (Slot(b[:]) for b in banks[0:3])
        carry = Slot(sb(ph1, "x1", [P, NT, D]))

        s = dve(lambda e: e.memset(xi_pad[:, :, 0:KC - 1], 0.0))
        for i in range(len(decay)):
            pads_ready = dve(lambda e: e.memset(decay[i].ap[:, :, 0:1], 0.0))
        mamba_consts = (a_ready, bc_w_ready, sel_ready, pads_ready)

        context = Slot(sb(ph1, "context", [P, D]))
        mask_in = Slot(sb(ph1, "mask_in", [P, NT + 1, S2], I32))
        kvT = sb(ph1, "kvT", [P, ND, KEYS])
        xT = kvT[:, :, 0:T]
        x_a = sb(ph1, "x_a", [P, NT, D])
        aT = sb(ph1, "aT", [P, NE, T])
        pairs = [Slot(sb(ph1, f"pair{i}", [P, T + KEYS + NK * P])) for i in range(3)]
        x_b = pairs[0].ap[:, 0:NT * D].rearrange("p (t d) -> p t d", t=NT)
        d_norm = norm_tiles(ph1, "d_norm", NT)
        bias_row = sb(ph1, "bias_row", [1, S2], BF16)
        bound = sb(ph1, "bound", [P, NT, S2])
        PW = NK * P
        attn = sb(ph1, "attn", [P, NT * H * S2 + 2 * 2 * T])
        probs = [Slot(attn[:, i * PW:(i + 1) * PW]) for i in range(4)]
        probsT = [Slot(attn[:, (4 + 2 * i) * PW:(6 + 2 * i) * PW]) for i in range(2)]
        stat = sb(ph1, "stat", [P, 8, 6])
        front = Ring([Slot(b[:]) for b in banks[3:5]])
        turn = Ring([Slot(b[:]) for b in banks[5:7]])
        gather = Slot(banks[7][:])

        tern = attn[:, 0:F0 * ND]
        tsum = stat[:, 0, :]
        tern_free = None
        for n in ("f_w1", "f_w2"):
            w = W[n][:].rearrange("p c n -> p (c n)")
            cnt = float(F0 * D)
            t = tern
            s = dve(lambda e: e.tensor_reduce(tsum[:, 0:1], w, AX.X, ALU.add, apply_absolute_value=True),
                    ffn_loaded, tern_free)
            s = pool(lambda e: e.partition_all_reduce(tsum[:, 1:2], tsum[:, 0:1], P, RADD), s)
            s = dve(lambda e: e.tensor_scalar(tsum[:, 2:3], tsum[:, 1:2], 1.0 / cnt, 1e-8, ALU.mult, ALU.max), s)
            s = dve(lambda e: e.reciprocal(tsum[:, 3:4], tsum[:, 2:3]), s)
            s = dve(lambda e: e.tensor_scalar(t, w, tsum[:, 3:4], RNE, ALU.mult, ALU.add), s)
            s = dve(lambda e: e.tensor_scalar(t, t, RNE, 1.0, ALU.subtract, ALU.min), s)
            s = dve(lambda e: e.tensor_scalar(t, t, -1.0, None, ALU.max), s)
            s = dve(lambda e: e.tensor_tensor(t, t, w, ALU.subtract), s)
            s = tern_free = dve(lambda e: e.tensor_tensor(w, w, t, ALU.add), s)
        ternary_ready = s

        for sl in probs:
            sl.free = dve(lambda e: e.memset(sl.ap[:, 0:PW], 0.0), s)
        Q, K, V = (slice(0, T), slice(T, T + KEYS), slice(T + KEYS, T + KEYS + NK * P))
        for sl in pairs:
            sl.free = dve(lambda e: e.memset(sl.ap[:, V], 0.0))
        pads2_ready = sl.free

        L0 = attn[:, 0:4 * PW]
        kblk = aT[:, NE // 2:, :].rearrange("p c t -> p (c t)")[:, 0:P // HD0 * S2]
        vpad = sb(ph1, "vpad", [S2, H, 2 * HD0])
        s = dve(lambda e: e.memset(vpad[:], 0.0))
        vpad_ready = s
        last_turn = {}

        def mamba(b):
            xs = x_in
            load = sync.dma(x_load, xs.ap[:], I["x"][b].rearrange("(t p) d -> p t d", p=P), xs.free)
            s = layernorm(m_norm, lambda i: xs.ap[:, i, :], lambda i: m_rows[:, i, :], 1e-6, P, NT, load)
            yield
            for t in range(NT):
                for c in range(ND):
                    m = pe(lambda e: e.transpose(m_work.ap[:, c * T + t * P:c * T + (t + 1) * P],
                                                           m_rows[:, t, c * P:(c + 1) * P], ident[:]),
                           s, m_work.free, ident_ready)
            for c in range(ND):
                h = dve(lambda e: e.tensor_scalar(m_hT[:, c, :], m_work.ap[:, c * T:(c + 1) * T],
                                                       W["m_ln_g"][:, c:c + 1], W["m_ln_b"][:, c:c + 1],
                                                       ALU.mult, ALU.add), m, mamba_loaded)
            m_work.free = h
            yield
            for j in range(NI):
                for q in range(2):
                    for c in range(ND):
                        m = pe(lambda e: e.matmul(
                            m_work.ap[:, q * T:(q + 1) * T],
                            W["m_w_in"][:, c, (2 * j + q) * P:(2 * j + q + 1) * P], m_hT[:, c, :],
                            start=c == 0, stop=c == ND - 1), h, m_work.free)
                dst = xi_pad[:, 2 * j:2 * j + 2, KC - 1:] if j < NI // 2 else zT[:, 2 * j - NI:2 * j - NI + 2, :]
                m_work.free = xi = act(lambda e: e.activation(
                    dst, m_work.ap.rearrange("p (q t) -> p q t", q=2), ACT.Copy), m)
                yield
            for c in range(NI):
                cv = dve(lambda e: e.tensor_scalar(uT[:, c, :], xi_pad[:, c, 0:T], W["m_conv_w"][:, c, 0:1],
                                                        W["m_conv_b"][:, c:c + 1], ALU.mult, ALU.add), xi)
                for k in range(1, KC):
                    cv = dve(lambda e: e.scalar_tensor_tensor(
                        uT[:, c, :], xi_pad[:, c, k:k + T], W["m_conv_w"][:, c, k:k + 1], uT[:, c, :],
                        ALU.mult, ALU.add), cv)
                if c % 2:
                    yield
            zs = act(lambda e: e.activation(zT[:], zT[:], ACT.Silu), xi)
            us = act(lambda e: e.activation(uT[:], uT[:], ACT.Silu), cv)
            act(lambda e: e.preload_act_table_set(EXP_LN))
            yield
            for c in range(NI):
                pe(lambda e: e.matmul(m_work.ap[0:DR, 0:T], W["m_w_x"][:, c, 0:DR], uT[:, c, :],
                                           start=c == 0, stop=c == NI - 1), us, m_work.free)
            for c in range(NI):
                m = pe(lambda e: e.matmul(m_work.ap[0:6 * NS, T:2 * T],
                                               w_bc[:, c, :, :].rearrange("p r n -> p (r n)"), uT[:, c, :],
                                               start=c == 0, stop=c == NI - 1), bc_w_ready)
            low = dve(lambda e: e.tensor_copy(dt_low[:], m_work.ap[0:DR, 0:T]), m)
            bcp = m_work.ap[0:6 * NS, T:2 * T]
            r = m_rows[0:6 * NS, 0, :]
            hi = m_hT[0:6 * NS, 0, :].bitcast(BF16)[:, 0:T]
            s = dve(lambda e: e.tensor_copy(hi, bcp), m)
            s1 = dve(lambda e: e.tensor_copy(bc_split[0:2 * NS, :], hi[0:2 * NS]), s, bank_c.free)
            s2 = dve(lambda e: e.tensor_tensor(r, bcp, hi, ALU.subtract), s)
            m_work.free = s2
            s3 = dve(lambda e: e.tensor_copy(hi, r), s2, s1)
            s4 = dve(lambda e: e.tensor_copy(bc_split[2 * NS:4 * NS, :], hi[2 * NS:4 * NS]), s3)
            s5 = dve(lambda e: e.tensor_tensor(r, r, hi, ALU.subtract), s3)
            bc_ready = dve(lambda e: e.tensor_copy(bc_split[4 * NS:6 * NS, :], r[4 * NS:6 * NS]), s5, s4)
            yield
            for q in range(2):
                for c in range(2):
                    m = pe(lambda e: e.matmul(
                        m_work.ap[:, c * T:(c + 1) * T], W["m_w_dt"][:, (2 * q + c) * P:(2 * q + c + 1) * P],
                        dt_low[:], start=True, stop=True), low, m_work.free)
                for c in range(2):
                    v = dve(lambda e: e.tensor_scalar(
                        dtT[:, 2 * q + c, :], m_work.ap[:, c * T:(c + 1) * T],
                        W["m_b_dt"][:, 2 * q + c:2 * q + c + 1], None, ALU.add), m)
                m_work.free = v
            s = act(lambda e: e.activation(m_tmp[:], dtT[:], ACT.Abs), v, bc_ready)
            ex = act(lambda e: e.activation(m_tmp[:], m_tmp[:], ACT.Exp, scale=-1.0), s)
            one_plus = dtuT
            w1 = dve(lambda e: e.tensor_scalar(one_plus[:], m_tmp[:], 1.0, None, ALU.add), ex)
            series, small = y_sum[:, :, 0, :], y_sum[:, :, 1, :].bitcast(I32)
            dve(lambda e: e.tensor_scalar(small, m_tmp[:], 2.0 ** -8, None, ALU.is_lt), last_turn.get("adds"))
            s = dve(lambda e: e.tensor_scalar(series, m_tmp[:], 1.0 / 3.0, -0.5, ALU.mult, ALU.add))
            s = dve(lambda e: e.tensor_tensor(series, series, m_tmp[:], ALU.mult), s)
            sr = dve(lambda e: e.scalar_tensor_tensor(series, series, 1.0, m_tmp[:], ALU.add, ALU.mult), s)
            s = dve(lambda e: e.scalar_tensor_tensor(m_tmp[:], one_plus[:], -1.0, m_tmp[:], ALU.add, ALU.subtract), w1)
            ln = act(lambda e: e.activation(one_plus[:], one_plus[:], ACT.Ln), s)
            yield
            s = dve(lambda e: e.tensor_tensor(one_plus[:], one_plus[:], m_tmp[:], ALU.subtract), ln)
            s = dve(lambda e: e.copy_predicated(one_plus[:], small, series), s, sr)
            dt = dve(lambda e: e.scalar_tensor_tensor(dtT[:], dtT[:], 0.0, one_plus[:], ALU.max, ALU.add), s)
            dtu = dve(lambda e: e.tensor_tensor(dtuT[:], dtT[:], uT[:], ALU.mult), dt)
            yield
            y_free = last_turn.get("y")
            for n in range(0, NS, 2):
                for k in range(2):
                    mb = pe(lambda e: e.matmul(
                        bank_b.ap[:, k * T:(k + 1) * T], sel[0:6 * NS, n + k:n + k + 1].to_broadcast([6 * NS, P]),
                        bc_split[:], start=True, stop=True), bc_ready, sel_ready, bank_b.free)
                for k in range(2):
                    mc = pe(lambda e: e.matmul(
                        bank_c.ap[:, k * T:(k + 1) * T],
                        sel[0:6 * NS, NS + n + k:NS + n + k + 1].to_broadcast([6 * NS, P]),
                        bc_split[:], start=True, stop=True), bank_c.free)
                sc = [None] * NI

                def decays(c, n=n):
                    d = decay[(n // 2 * NI + c) % len(decay)]
                    for k in range(2):
                        d.ready = act(lambda e: e.activation(
                            d.ap[:, k, 1:T], dtT[:, c, 1:T], ACT.Exp, scale=a_neg[:, c, n + k:n + k + 1]),
                            dt, d.free, a_ready, pads_ready)

                for c in range(2):
                    decays(c)
                yield
                for c in range(NI):
                    out_t = state[c].ap
                    s = dve(lambda e, c=c, o=out_t: e.tensor_tensor(
                        o[:], dtuT[:, c:c + 1, :].to_broadcast([P, 2, T]),
                        bank_b.ap.rearrange("p (k t) -> p k t", k=2), ALU.mult), mb, dtu, state[c].free)
                    sc[c] = s
                bank_b.free = s
                yield
                for c in range(NI):
                    if c + 2 < NI:
                        decays(c + 2)
                    d = decay[(n // 2 * NI + c) % len(decay)]
                    f = state[c].ap[:].rearrange("p k t -> p (k t)")
                    g = d.ap[:].rearrange("p k t -> p (k t)")
                    d.free = sc[c] = dve(lambda e: e.tensor_tensor_scan(
                        f, g, f, 0.0, ALU.mult, ALU.add), d.ready, sc[c])
                yield
                for c in range(NI):
                    f = state[c].ap[:].rearrange("p k t -> p (k t)")
                    d = y_sum[:, c, :, :].rearrange("p k t -> p (k t)") if n == 0 else f
                    s = dve(lambda e: e.tensor_tensor(d, f, bank_c.ap, ALU.mult), sc[c], mc,
                            y_free if n == 0 else None)
                    if n == 0:
                        state[c].free = ys = s
                    else:
                        yc = y_sum[:, c, :, :].rearrange("p k t -> p (k t)")
                        state[c].free = ys = pool(lambda e: e.tensor_tensor(yc, yc, f, ALU.add), s, first if n == 2 else None)
                bank_c.free = s
                first = s
                yield
            y = m_tmp
            s = dve(lambda e: e.tensor_tensor(y[:], y_sum[:, :, 0, :], y_sum[:, :, 1, :], ALU.add), ys)
            last_turn["y"], last_turn["adds"] = s, ys
            for c in range(NI):
                s = dve(lambda e: e.scalar_tensor_tensor(y[:, c, :], uT[:, c, :], W["m_dp"][:, c:c + 1],
                                                              y[:, c, :], ALU.mult, ALU.add), s)
            yd = dve(lambda e: e.tensor_tensor(y[:], y[:], zT[:], ALU.mult), s, zs)
            yield
            for t in range(NT):
                for c in range(NI):
                    m = pe(lambda e: e.matmul(m_work.ap[:, t * D:(t + 1) * D], y[:, c, t * P:(t + 1) * P],
                                                        W["m_w_out"][:, c, :], start=c == 0, stop=c == NI - 1),
                           yd, m_work.free)
            fl = lambda a: a.rearrange("p t d -> p (t d)")
            m_work.free = xs.free = s = dve(lambda e: e.scalar_tensor_tensor(
                fl(m_rows), fl(xs.ap[:]), 2.0, m_work.ap, ALU.mult, ALU.add), m)
            cy = carry
            cy.ready = layernorm(m_norm, lambda i: m_rows[:, i, :], lambda i: cy.ap[:, i, :], 1e-5, P, NT, s, cy.free)
            yield

        fl = lambda a: a.rearrange("p t d -> p (t d)")

        def transposed(src, dst, ready, dst_free, rows=P, tiles=NT, width=T):
            bank = turn.next()
            for t in range(tiles):
                for c in range(ND):
                    m = pe(lambda e: e.transpose(
                        bank.ap[:, c * width + t * P:c * width + t * P + rows],
                        src(t)[:, c * P:(c + 1) * P], ident[0:rows, 0:rows]), ready, bank.free)
            bank.free = s = dve(lambda e: e.tensor_copy(dst, bank.ap[:, 0:ND * width].rearrange("p (c t) -> p c t", c=ND)),
                                m, dst_free)
            return s

        def rows_out(lhs, n, w, ready):
            bank = front.next()
            for t in range(NT):
                for c in range(n):
                    m = pe(lambda e: e.matmul(bank.ap[:, t * D:(t + 1) * D], lhs[:, c, t * P:(t + 1) * P],
                                                        w[:, c, :], start=c == 0, stop=c == n - 1), ready, bank.free)
            return bank, m

        def bcast(row):
            return row.unsqueeze(1).to_broadcast([P, NT, D])

        def attention(kind, qT, kT, ready, wq, wk, wv, wo, prev):
            keys = T if kind == "causal" else KEYS
            per_head = 1 if kind == "causal" else NT
            units = [(h, t) for h in range(H) for t in range(per_head)]
            lag = 2 if kind == "causal" else 3
            made, turned = {}, {}
            outs = [None]

            def project(pair):
                sl = pairs[pair % 3]
                col = slice(pair * P, (pair + 1) * P)
                bank = front.next()
                for c in range(ND):
                    m = pe(lambda e: e.matmul(bank.ap[:, 0:T], wq[:, c, col], qT[:, c, 0:T], start=c == 0,
                                                   stop=c == ND - 1), ready, bank.free)
                bank.free = q = act(lambda e: e.activation(sl.ap[:, Q], bank.ap[:, 0:T], ACT.Copy,
                                                                      scale=HD ** -0.5), m, sl.free)
                bank = front.next()
                for c in range(ND):
                    m = pe(lambda e: e.matmul(bank.ap[:, 0:keys], wk[:, c, col], kT[:, c, 0:keys],
                                                              start=c == 0, stop=c == ND - 1), ready, bank.free)
                bank.free = k = dve(lambda e: e.tensor_copy(sl.ap[:, T:T + keys], bank.ap[:, 0:keys]), m, sl.free)
                bank = front.next()
                nk = (keys + P - 1) // P
                for i in range(nk):
                    n = min(P, keys - i * P)
                    for c in range(ND):
                        m = pe(lambda e: e.matmul(
                            bank.ap[0:n, i * P:(i + 1) * P], kT[:, c, i * P:i * P + n], wv[:, c, col],
                            start=c == 0, stop=c == ND - 1), ready, bank.free)
                v0 = T + KEYS
                v = act(lambda e: e.activation(sl.ap[:, v0:v0 + T], bank.ap[:, 0:T], ACT.Copy), m, sl.free)
                if nk == NK:
                    n = keys - 2 * P
                    v = act(lambda e: e.activation(sl.ap[0:n, v0 + T:v0 + T + P], bank.ap[0:n, T:T + P],
                                                              ACT.Copy), m)
                bank.free = v
                sl.q, sl.k, sl.v = q, k, v

            def scores(u):
                h, t = units[u]
                sl, o = pairs[h // 2 % 3], h % 2 * HD
                bank, pr, st = front.next(), probs[u % 4], stat[:, u % 8, :]
                qs = lambda i: sl.ap[o:o + HD, i * P:(i + 1) * P]
                if kind == "causal":
                    spans = [(0, P, 0), (P, T, 1)]
                    for a, n, i in spans:
                        pe(lambda e: e.matmul(bank.ap[:, a:a + n], qs(i), sl.ap[o:o + HD, T:T + n],
                                                             start=True, stop=False), sl.q, sl.k, bank.free)
                        m = pe(lambda e: e.matmul(bank.ap[:, a + n - P:a + n], ident_bf[:], causal[:],
                                                            start=False, stop=True),
                               causal_ready, ident_bf_ready)
                else:
                    spans = [(0, KEYS, t)]
                    pe(lambda e: e.matmul(bank.ap[:, 0:KEYS], qs(t), sl.ap[o:o + HD, K], start=True, stop=False),
                       sl.q, sl.k, bank.free)
                    m = pe(lambda e: e.matmul(bank.ap[:, T:KEYS], ones_bf[:], bias_row[:], start=False, stop=True),
                           mask_done[0])
                for j, (a, n, i) in enumerate(spans):
                    mx = dve(lambda e: e.tensor_reduce(st[:, j:j + 1], bank.ap[:, a:a + n], AX.X,
                                                                      ALU.max, negate=True), m, stat_free[u % 8])
                for j, (a, n, i) in enumerate(spans):
                    ex = act(lambda e: e.activation(
                        pr.ap[:, a:a + n], bank.ap[:, a:a + n], ACT.Exp, bias=st[:, j:j + 1],
                        accum_out=st[:, 2 + j:3 + j]), mx, pr.free)
                bank.free = ex
                ns = len(spans)
                rc = dve(lambda e: e.reciprocal(st[:, 4:4 + ns], st[:, 2:2 + ns]), ex)
                for j, (a, n, i) in enumerate(spans):
                    s = pool(lambda e: e.tensor_scalar(
                        pr.ap[:, a:a + n], pr.ap[:, a:a + n], st[:, 4 + j:5 + j], 1.0, ALU.mult, ALU.mult), rc)
                stat_free[u % 8] = s
                made[u] = s

            def turn_probs(u):
                h, t = units[u]
                bank, pr, pt = turn.next(), probs[u % 4], probsT[h % 2]
                for i in range(NK):
                    m = pe(lambda e: e.transpose(bank.ap[:, i * P:(i + 1) * P], pr.ap[:, i * P:(i + 1) * P],
                                                      ident[:]), made[u], bank.free)
                pr.free = m
                if kind == "causal":
                    s = dve(lambda e: e.tensor_copy(pt.ap[:, 0:PW], bank.ap[:, 0:PW]), m, pt.free)
                else:
                    dst = pt.ap.rearrange("p (k q) -> p k q", q=T)[:, :, t * P:(t + 1) * P]
                    src = bank.ap[:, 0:PW].rearrange("p (k q) -> p k q", q=P)
                    if u % 2:
                        s = dve(lambda e: e.tensor_copy(dst, src), m, pt.free)
                    else:
                        s = act(lambda e: e.activation(dst, src, ACT.Copy), m, pt.free)
                bank.free = s
                turned[u] = s

            def weigh(h):
                sl, o, pt = pairs[h // 2 % 3], h % 2 * HD, probsT[h % 2]
                g = gather.ap[:, h // 2 % 2 * T:(h // 2 % 2 + 1) * T]
                us = [turned[u] for u in range(len(units)) if units[u][0] == h]
                v0 = T + KEYS
                parts = [(0, 0, T, 0), (1, T, PW, P)] if kind == "causal" else [(i, i * T, (i + 1) * T, 0) for i in range(NK)]
                for j, (i, a, z, q0) in enumerate(parts):
                    m = pe(lambda e: e.matmul(
                        g[o:o + HD, q0:T], sl.ap[:, v0 + i * P + o:v0 + i * P + o + HD], pt.ap[:, a:z],
                        start=j == 0, stop=j == len(parts) - 1), *us, sl.v, gather.free, pads2_ready)
                pt.free = m
                if h % 2:
                    sl.free = m
                    gather.free = outs[0] = act(lambda e: e.activation(aT[:, h // 2, :], g, ACT.Copy), m)

            project(0)
            yield
            total = len(units)
            upp = total // NE
            for u in range(total + lag + 1):
                if u < total:
                    scores(u)
                if 0 <= u - lag < total:
                    turn_probs(u - lag)
                v = u - lag - 1
                if 0 <= v < total and (v + 1) % per_head == 0:
                    weigh(units[v][0])
                yield
                if (u + 1) % upp == upp - 1 and (u + 1) // upp + 1 < NE:
                    project((u + 1) // upp + 1)
                    yield
            result[0] = outs[0]

        stat_free, mask_done, result = [None] * 8, [None], [None]

        def load_context(b):
            cs, ms = context, mask_in
            cs.ready = sync.dma(ctx_load, cs.ap[0:S2, :], I["ctx"][b], cs.free)
            sync.dma(mask_load, ms.ap[:, 0:NT, :], I["mask_q"][b, 0].rearrange("(t p) k -> p t k", p=P), ms.free)
            ms.ready = sync.dma(mask_load, ms.ap[0:1, NT, :], I["mask_k"][b:b + 1, :], ms.free)

        def decoder(b):
            cy, cs, ms = carry, context, mask_in
            x1T = transposed(lambda t: cy.ap[:, t, :], xT[:], cy.ready, None)
            ctxT = kvT[:, :, T:KEYS]
            c_T = transposed(lambda t: cs.ap[0:S2, :], ctxT, cs.ready, None, rows=S2, tiles=1, width=S2)
            s = dve(lambda e: e.tensor_scalar(bound[:], ms.ap[:, 0:NT, :], 0.0, NEG, ALU.is_equal, ALU.mult), ms.ready)
            bd = dve(lambda e: e.tensor_scalar(bound[:], bound[:], 100.0, None, ALU.add), s)
            ms.free = mask_done[0] = dve(lambda e: e.tensor_scalar(bias_row[:], ms.ap[0:1, NT, :], 0.0, NEG,
                                                                   ALU.is_equal, ALU.mult), ms.ready)
            yield
            G = P // HD0
            qT0 = pairs[0].ap[:, 0:ND * T].rearrange("p (c t) -> p c t", c=ND)
            kT0 = pairs[1].ap[:, 0:ND * S2].rearrange("p (c t) -> p c t", c=ND)
            bank = front.next()
            for c2 in range(ND):
                for c in range(ND):
                    m = pe(lambda e: e.matmul(bank.ap[:, c2 * T:(c2 + 1) * T], W["c_wq"][:, c, c2 * P:(c2 + 1) * P],
                                                          xT[:, c, :], start=c == 0, stop=c == ND - 1),
                           x1T, bank.free, cross_loaded)
            for c2 in range(ND):
                q = dve(lambda e: e.tensor_scalar(
                    qT0[:, c2, :], bank.ap[:, c2 * T:(c2 + 1) * T], W["c_bq"][:, c2:c2 + 1], HD0 ** -0.5,
                    ALU.add, ALU.mult), m, pairs[0].free)
            bank.free = q
            bank = front.next()
            for c2 in range(ND):
                for c in range(ND):
                    m = pe(lambda e: e.matmul(
                        bank.ap[:, c2 * S2:(c2 + 1) * S2], W["c_wk"][:, c, c2 * P:(c2 + 1) * P], ctxT[:, c, :],
                        start=c == 0, stop=c == ND - 1), c_T, bank.free)
            for c2 in range(ND):
                k = act(lambda e: e.activation(
                    kT0[:, c2, :], bank.ap[:, c2 * S2:(c2 + 1) * S2], ACT.Identity, bias=W["c_bk"][:, c2:c2 + 1]),
                    m, pairs[1].free)
            bank.free = k
            bank = front.next()
            for c in range(ND):
                m = pe(lambda e: e.matmul(bank.ap[0:S2, 0:D], ctxT[:, c, :], W["c_wv"][:, c, :],
                                                          start=c == 0, stop=c == ND - 1), c_T, bank.free)
            for par in range(2):
                v = dve(lambda e: e.tensor_tensor(
                    vpad[:, par::2, par * HD0:(par + 1) * HD0],
                    bank.ap[0:S2, 0:D].rearrange("k (h d) -> k h d", d=HD0)[:, par::2, :],
                    W["c_bv"][0:S2, :].rearrange("k (h d) -> k h d", d=HD0)[:, par::2, :], ALU.add), m, vpad_ready)
            bank.free = v
            yield
            kblk_free[0] = phase1_last[0]
            sc = [attn[:, t * H * S2:(t + 1) * H * S2].rearrange("p (h k) -> p h k", k=S2) for t in range(NT)]
            half = G // 2
            sdone = [None] * NT
            for c in range(ND):
                kb = dve(lambda e: e.tensor_tensor(
                    kblk.rearrange("p (h k) -> p h k", k=S2), kT0[:, c:c + 1, :].to_broadcast([P, G, S2]),
                    head_of[:].unsqueeze(2).to_broadcast([P, G, S2]), ALU.mult), k, kblk_free[0], heads_ready)
                for t in range(NT):
                    for g in range(2):
                        bank = front.next()
                        kblk_free[0] = m = pe(lambda e: e.matmul(
                            bank.ap[:, 0:half * S2], qT0[:, c, t * P:(t + 1) * P],
                            kblk[:, g * half * S2:(g + 1) * half * S2], start=True, stop=True), q, kb, bank.free)
                        h0 = c * G + g * half
                        bank.free = sdone[t] = dve(lambda e: e.scalar_tensor_tensor(
                            sc[t][:, h0:h0 + half, :], bank.ap[:, 0:half * S2].rearrange("p (h k) -> p h k", k=S2), -100.0,
                            bound[:, t:t + 1, :].to_broadcast([P, half, S2]), ALU.max, ALU.min), m, bd)
                        yield
            pm = []
            for t in range(NT):
                m = dve(lambda e: e.tensor_reduce(l0_stat[:, t, 0, :], sc[t], AX.X, ALU.max), sdone[t])
                s = dve(lambda e: e.tensor_tensor(sc[t], sc[t], l0_stat[:, t, 0, :].unsqueeze(2).to_broadcast([P, H, S2]),
                                                       ALU.subtract), m)
                s = act(lambda e: e.activation(sc[t], sc[t], ACT.Exp), s)
                m = dve(lambda e: e.tensor_reduce(l0_stat[:, t, 1, :], sc[t], AX.X, ALU.add), s)
                m = dve(lambda e: e.reciprocal(l0_stat[:, t, 0, :], l0_stat[:, t, 1, :]), m)
                pm.append(pool(lambda e: e.tensor_tensor(
                    sc[t], sc[t], l0_stat[:, t, 0, :].unsqueeze(2).to_broadcast([P, H, S2]), ALU.mult), m))
                yield
            pT = [Slot(attn[:, NT * H * S2 + i * 2 * T:NT * H * S2 + (i + 1) * 2 * T]) for i in range(2)]
            a0 = aT[:, 0:ND, :]
            for hp in range(H // 2):
                bank, pt = turn.next(), pT[hp % 2]
                for j in range(2):
                    for t in range(NT):
                        m = pe(lambda e: e.transpose(
                            bank.ap[0:S2, j * T + t * P:j * T + (t + 1) * P], sc[t][:, 2 * hp + j, :], ident[:]),
                            pm[t], bank.free)
                bank.free = s = act(lambda e: e.activation(pt.ap[0:S2, :], bank.ap[0:S2, :], ACT.Copy), m, pt.free)
                o = hp % 4 * 2 * HD0
                g = gather.ap[o:o + 2 * HD0, hp // 4 * T:(hp // 4 + 1) * T]
                for j in range(2):
                    pt.free = m = pe(lambda e: e.matmul(
                        g, vpad[:, 2 * hp + j, :], pt.ap[0:S2, j * T:(j + 1) * T], start=j == 0, stop=j == 1,
                        tile_position=(0, o)), s, v, gather.free)
                if hp % 2:
                    yield
            gather.free = a = act(lambda e: e.activation(a0, gather.ap.rearrange("p (c t) -> p c t", c=ND), ACT.Copy), m)
            bank, m = rows_out(a0, ND, W["c_wo"], a)
            s = dve(lambda e: e.tensor_tensor(x_a[:], cy.ap[:], bank.ap.rearrange("p (t d) -> p t d", t=NT), ALU.add), m)
            bank.free = cy.free = s
            s = dve(lambda e: e.tensor_tensor(x_a[:], x_a[:], bcast(W["c_bo"][:]), ALU.add), s)
            x2 = layernorm(d_norm, lambda i: x_a[:, i, :], lambda i: x_a[:, i, :], 1e-5, P, NT, s)
            yield
            x2T = transposed(lambda t: x_a[:, t, :], xT[:], x2, None)
            for f in range(0, NF0, 2):
                bank = front.next()
                for q in range(2):
                    for c in range(ND):
                        m = pe(lambda e: e.matmul(
                            bank.ap[:, q * T:(q + 1) * T], W["f_w1"][:, c, (f + q) * P:(f + q + 1) * P], xT[:, c, :],
                            start=c == 0, stop=c == ND - 1), x2T, bank.free, ternary_ready)
                for q in range(2):
                    g = dve(lambda e: e.tensor_scalar(
                        aT[:, f + q, :], bank.ap[:, q * T:(q + 1) * T], W["f_b1"][:, f + q:f + q + 1], None, ALU.add), m)
                bank.free = g
                yield
            g = act(lambda e: e.activation(aT[:], aT[:], ACT.Gelu), g)
            act(lambda e: e.preload_act_table_set(EXP_LN))
            bank, m = rows_out(aT, NF0, W["f_w2"], g)
            s = dve(lambda e: e.tensor_tensor(x_a[:], x_a[:], bank.ap.rearrange("p (t d) -> p t d", t=NT), ALU.add), m)
            bank.free = s
            s = dve(lambda e: e.tensor_tensor(x_a[:], x_a[:], bcast(W["f_b2"][:]), ALU.add), s)
            x3 = layernorm(d_norm, lambda i: x_a[:, i, :], lambda i: x_a[:, i, :], 1e-5, P, NT, s)
            yield
            x3T = transposed(lambda t: x_a[:, t, :], xT[:], x3, None)
            for _ in attention("causal", xT, xT, x3T, W["a_wq"], W["a_wk"], W["a_wv"], W["a_wo"], x3):
                yield
            bank, m = rows_out(aT, NE, W["a_wo"], result[0])
            s = dve(lambda e: e.tensor_tensor(x_b, x_a[:], bank.ap.rearrange("p (t d) -> p t d", t=NT), ALU.add), m)
            bank.free = s
            s = layernorm(d_norm, lambda i: x_b[:, i, :], lambda i: x_b[:, i, :], 1e-3, P, NT, s)
            s = dve(lambda e: e.tensor_tensor(x_b, x_b, bcast(W["a_gamma"][:]), ALU.mult), s)
            s = dve(lambda e: e.tensor_tensor(x_b, x_b, bcast(W["a_beta"][:]), ALU.add), s)
            s = dve(lambda e: e.tensor_tensor(x_a[:], x_a[:], x_b, ALU.add), s)
            x4 = layernorm(d_norm, lambda i: x_a[:, i, :], lambda i: x_a[:, i, :], 1e-5, P, NT, s)
            yield
            s = layernorm(d_norm, lambda i: x_a[:, i, :], lambda i: x_b[:, i, :], 1e-5, P, NT, x4)
            bank = turn.next()
            for t in range(NT):
                for c in range(ND):
                    m = pe(lambda e: e.transpose(bank.ap[:, c * T + t * P:c * T + (t + 1) * P],
                                                                      x_b[:, t, c * P:(c + 1) * P], ident[:]), s, bank.free)
            for c in range(ND):
                lt = dve(lambda e: e.tensor_scalar(
                    kvT[:, c, 0:T], bank.ap[:, c * T:(c + 1) * T], W["p_ln_l_w"][:, c:c + 1],
                    W["p_ln_l_b"][:, c:c + 1], ALU.mult, ALU.add), m, perc_loaded)
            bank.free = lt
            s = layernorm(d_norm, lambda i: cs.ap[0:S2, :], lambda i: x_b[0:S2, 0, :], 1e-5, S2, 1, cs.ready, m)
            cs.free = s
            if b + 1 < B:
                load_context(b + 1)
            bank = turn.next()
            for c in range(ND):
                m = pe(lambda e: e.transpose(bank.ap[:, c * S2:(c + 1) * S2],
                                                             x_b[0:S2, 0, c * P:(c + 1) * P], ident[0:S2, 0:S2]), s, bank.free)
            for c in range(ND):
                kv = dve(lambda e: e.tensor_scalar(
                    kvT[:, c, T:KEYS], bank.ap[:, c * S2:(c + 1) * S2], W["p_ln_m_w"][:, c:c + 1],
                    W["p_ln_m_b"][:, c:c + 1], ALU.mult, ALU.add), m)
            bank.free = kv
            yield
            for sl in probs:
                sl.free = dve(lambda e: e.memset(sl.ap[:, KEYS:PW], 0.0), sl.free)
            for sl in pairs:
                dve(lambda e: e.memset(sl.ap[:, T + KEYS + T:T + KEYS + PW], 0.0), sl.free)
            pad = dve(lambda e: e.memset(stat[:, 0, 0:1], 0.0), stat_free[0])
            for sl in pairs:
                sl.free = pad
            stat_free[0] = pad
            for _ in attention("all", kvT, kvT, kv, W["p_wq"], W["p_wk"], W["p_wv"], W["p_wo"], x4):
                yield
            bank, m = rows_out(aT, NE, W["p_wo"], result[0])
            s = dve(lambda e: e.tensor_tensor(x_a[:], x_a[:], bank.ap.rearrange("p (t d) -> p t d", t=NT), ALU.add), m)
            bank.free = s
            o5 = pairs[1].ap[:, 0:NT * D].rearrange("p (t d) -> p t d", t=NT)
            s = layernorm(d_norm, lambda i: x_a[:, i, :], lambda i: o5[:, i, :], 1e-5, P, NT, s, pairs[1].free)
            am = dve(lambda e: e.tensor_reduce(amax5[:, b:b + 1], fl(o5), AX.X, ALU.max, apply_absolute_value=True), s)
            pairs[1].free = sync.dma(spill, x5_dram[b].rearrange("(t p) d -> p t d", p=P), o5, s)
            phase1_last[0], phase1_last[1] = am, pairs[1].free
            yield

        kblk_free = [None]

        l0_stat = sb(ph1, "l0_stat", [P, NT, 2, H])
        phase1_last = [None, None]

        load_context(0)
        for _ in mamba(0):
            pass
        for b in range(B):
            strands = [(260.0, decoder(b))]
            if b + 1 < B:
                strands.append((50.0, mamba(b + 1)))
            interleave(strands)

        ends = [q.steps[-1] for q in (pe, act, pool)]
        for s in ends:
            s.wanted = True
        ph1.close()
        begin = (phase1_last[0], phase1_last[1], *ends)
        W_MAX, A_MAX = 7.0, 32767.0
        LPB = 32
        TB = 2 * T
        NP = B * T // TB if B > 1 else 1
        TB = B * T // NP
        big = sb(ctx, "big", [P, NF1, B * T])
        up_int = sb(ctx, "up_int", [P, NF1, B * T], I16)
        xqT = sb(ctx, "xqT", [P, ND, B * T])
        gateT, upT = sb(ctx, "gateT", [P, ND, F1]), sb(ctx, "upT", [P, ND, F1])
        downT = sb(ctx, "downT", [P, NF1, D])
        rows = [Slot(sb(ctx, f"rows{i}", [P, NT, D])) for i in range(3)]
        q_norm = norm_tiles(ctx, "q_norm", NT)
        part = sb(ctx, "part", [P, 4, 64])
        scales = sb(ctx, "scales", [P, 5, 4])
        ring = Ring([Slot(b[:]) for b in banks])

        def scale_of(which, partial, *after):
            v = scales[:, which, :]
            s = dve(lambda e: e.tensor_reduce(v[:, 0:1], partial, AX.X, ALU.max), *after)
            s = pool(lambda e: e.partition_all_reduce(v[:, 1:2], v[:, 0:1], P, RMAX), s)
            s = dve(lambda e: e.tensor_scalar(v[:, 2:3], v[:, 1:2], 1.0 / A_MAX, 1e-12, ALU.mult, ALU.max), s)
            return v[:, 2:3], v[:, 3:4], dve(lambda e: e.reciprocal(v[:, 3:4], v[:, 2:3]), s)

        sx, sx_inv, sx_ready = scale_of(0, amax5[:], *begin)

        stage = big[:].rearrange("p c t -> p (c t)") if B > 4 else sb(ctx, "stage", [P, 8 * F1 * ND])[:]
        for n, (name, dst) in enumerate((("g_up", upT), ("g_gate", gateT), ("g_down", downT))):
            nr, width = I[name].shape[0] // P, I[name].shape[1]
            size = nr * width
            w = stage[:, n * size:(n + 1) * size]
            q = stage[:, (3 + n) * size:(4 + n) * size]
            blocks = lambda a: a.rearrange("p (b k) -> p b k", k=LPB)
            nb = size // LPB
            sc = stage[:, 7 * size + n * 2 * nb:7 * size + (n * 2 + 1) * nb]
            inv = stage[:, 7 * size + (n * 2 + 1) * nb:7 * size + (n * 2 + 2) * nb]
            load = sync.dma(weight_load[5 + n], w.rearrange("p (c n) -> p c n", c=nr), I[name].rearrange("(c p) n -> p c n", p=P), *begin)
            s = dve(lambda e: e.tensor_reduce(sc, blocks(w), AX.X, ALU.max, apply_absolute_value=True), load)
            s = dve(lambda e: e.tensor_scalar(sc, sc, 1.0 / W_MAX, 1e-12, ALU.mult, ALU.max), s)
            s = dve(lambda e: e.reciprocal(inv, sc), s)
            s = dve(lambda e: e.tensor_tensor(blocks(q), blocks(w), inv.unsqueeze(2).to_broadcast([P, nb, LPB]), ALU.mult), s)
            s = dve(lambda e: e.tensor_scalar(q, q, RNE, RNE, ALU.add, ALU.subtract), s)
            s = dve(lambda e: e.tensor_scalar(q, q, W_MAX, -W_MAX - 1.0, ALU.min, ALU.max), s)
            s = dve(lambda e: e.tensor_tensor(blocks(q), blocks(q), sc.unsqueeze(2).to_broadcast([P, nb, LPB]), ALU.mult), s)
            nc_, qv = width // P, q.rearrange("p (r c) -> p r c", r=nr)
            for c in range(nc_):
                for r0 in range(0, nr, 4):
                    bank, k = ring.next(), min(4, nr - r0)
                    for r in range(k):
                        m = pe(lambda e: e.transpose(bank.ap[:, r * P:(r + 1) * P], qv[:, r0 + r, c * P:(c + 1) * P], ident[:]),
                               s, bank.free, ident_ready)
                    bank.free = ready = act(lambda e: e.activation(dst[:, c, r0 * P:(r0 + k) * P], bank.ap[:, 0:k * P], ACT.Copy), m, *begin)
            w_ready = ready
        staged = ready

        for b in range(B):
            r = rows[b % 3]
            load = sync.dma(reload_rows[b % 3], r.ap[:], x5_dram[b].rearrange("(t p) d -> p t d", p=P), r.free, *begin)
            bank = ring.next()
            for t in range(NT):
                for c in range(ND):
                    m = pe(lambda e: e.transpose(bank.ap[:, c * T + t * P:c * T + (t + 1) * P],
                                                 r.ap[:, t, c * P:(c + 1) * P], ident[:]), load, bank.free)
            r.free = m
            xs = xqT[:, :, b * T:(b + 1) * T]
            s = dve(lambda e: e.tensor_scalar(xs, bank.ap.rearrange("p (c t) -> p c t", c=ND), sx_inv, RNE,
                                              ALU.mult, ALU.add), m, sx_ready)
            bank.free = s
            s = dve(lambda e: e.tensor_scalar(xs, xs, RNE, A_MAX, ALU.subtract, ALU.min), s)
            x_ready = dve(lambda e: e.tensor_scalar(xs, xs, -A_MAX - 1.0, sx, ALU.max, ALU.mult), s)

        def piece(a, p):
            return a[:, :, p * TB:(p + 1) * TB]

        def project_up(w, which, free):
            at = 0
            done = [None] * NP
            for p in range(NP):
                for i in range(NF1):
                    bank = ring.next()
                    for c in range(ND):
                        m = pe(lambda e: e.matmul(bank.ap[:, 0:TB], w[:, c, i * P:(i + 1) * P], piece(xqT, p)[:, c, :],
                                                  start=c == 0, stop=c == ND - 1), x_ready, w_ready, bank.free)
                    bank.free = a = act(lambda e: e.activation(piece(big, p)[:, i, :], bank.ap[:, 0:TB], ACT.Copy), m, free[p], staged)
                    done[p] = dve(lambda e: e.tensor_reduce(part[:, which, at:at + 1], piece(big, p)[:, i, :], AX.X, ALU.max,
                                                            apply_absolute_value=True), a)
                    at += 1
            return done, part[:, which, 0:at]

        done, partial = project_up(upT, 0, [None] * NP)
        su, su_inv, su_ready = scale_of(1, partial, done[-1])
        free = [None] * NP
        rne = sb(ctx, "rne", [P, 1])
        rne_ready = dve(lambda e: e.memset(rne[:], RNE), *begin)
        for p in range(NP):
            s = act(lambda e: e.activation(piece(big, p), piece(big, p), ACT.Identity, bias=rne[:], scale=su_inv), su_ready, rne_ready)
            free[p] = up_ready = dve(lambda e: e.tensor_scalar(piece(up_int, p), piece(big, p), RNE, A_MAX,
                                                               ALU.subtract, ALU.min), s)

        done, partial = project_up(gateT, 1, free)
        sg, sg_inv, sg_ready = scale_of(2, partial, done[-1])
        xq_flat = xqT[:].rearrange("p c t -> p (c t)")
        n_tmp = 2
        tmp = Ring([Slot(xq_flat[:, i * NF1 * TB:(i + 1) * NF1 * TB].rearrange("p (c t) -> p c t", c=NF1)) for i in range(n_tmp)]
                   if B > 4 else
                   [Slot(sb(ctx, f"tmp{i}", [P, NF1, TB])[:]) for i in range(n_tmp)])
        for p in range(NP):
            g, sl = piece(big, p), tmp.next()
            s = act(lambda e: e.activation(g, g, ACT.Identity, bias=rne[:], scale=sg_inv), sg_ready)
            s = dve(lambda e: e.tensor_scalar(g, g, RNE, A_MAX, ALU.subtract, ALU.min), s)
            gq = dve(lambda e: e.tensor_scalar(g, g, -A_MAX - 1.0, sg, ALU.max, ALU.mult), s)
            s = act(lambda e: e.activation(sl.ap, g, ACT.Sigmoid), gq, sl.free)
            s = pool(lambda e: e.tensor_scalar(sl.ap, sl.ap, 65536.0, RNE, ALU.mult, ALU.add), s)
            s = dve(lambda e: e.tensor_scalar(sl.ap, sl.ap, RNE, 65535.0, ALU.subtract, ALU.min), s)
            fg, fs = g, sl.ap
            s = sl.free = dve(lambda e: e.scalar_tensor_tensor(fg, fs, 2.0 ** -16, fg, ALU.mult, ALU.mult), s)
            done = dve(lambda e: e.tensor_reduce(part[:, 2, p:p + 1], g, AX.XY, ALU.max, apply_absolute_value=True), s)
        s2, s2_inv, s2_ready = scale_of(3, part[:, 2, 0:NP], done)
        for p in range(NP):
            g, sl = piece(big, p), tmp.next()
            u = act(lambda e: e.activation(sl.ap, piece(up_int, p), ACT.Copy, scale=su), up_ready, su_ready, sl.free)
            s = act(lambda e: e.activation(g, g, ACT.Identity, bias=rne[:], scale=s2_inv), s2_ready)
            s = dve(lambda e: e.tensor_scalar(g, g, RNE, A_MAX, ALU.subtract, ALU.min), s)
            s = dve(lambda e: e.tensor_scalar(g, g, -A_MAX - 1.0, s2, ALU.max, ALU.mult), s)
            fg, fs = g, sl.ap
            s = sl.free = dve(lambda e: e.tensor_tensor(fg, fg, fs, ALU.mult), s, u)
            done = dve(lambda e: e.tensor_reduce(part[:, 3, p:p + 1], g, AX.XY, ALU.max, apply_absolute_value=True), s)
        so, so_inv, so_ready = scale_of(4, part[:, 3, 0:NP], done)
        act(lambda e: e.preload_act_table_set(EXP_LN))
        for p in range(NP):
            g = piece(big, p)
            s = act(lambda e: e.activation(g, g, ACT.Identity, bias=rne[:], scale=so_inv), so_ready)
            s = dve(lambda e: e.tensor_scalar(g, g, RNE, A_MAX, ALU.subtract, ALU.min), s)
            o_ready = dve(lambda e: e.tensor_scalar(g, g, -A_MAX - 1.0, so, ALU.max, ALU.mult), s)
            for b in range(p * TB // T, (p + 1) * TB // T):
                r = rows[b % 3]
                load = sync.dma(reload_rows[b % 3], r.ap[:], x5_dram[b].rearrange("(t p) d -> p t d", p=P), r.free)
                bank = ring.next()
                for t in range(NT):
                    for i in range(NF1):
                        t0 = b * T + t * P
                        m = pe(lambda e: e.matmul(bank.ap[:, t * D:(t + 1) * D], big[:, i, t0:t0 + P], downT[:, i, :],
                                                  start=i == 0, stop=i == NF1 - 1), o_ready, bank.free)
                fr = r.ap[:].rearrange("p t d -> p (t d)")
                bank.free = s = dve(lambda e: e.tensor_tensor(fr, fr, bank.ap, ALU.add), m, load)
                s = layernorm(q_norm, lambda i: r.ap[:, i, :], lambda i: r.ap[:, i, :], 1e-5, P, NT, s)
                r.free = sync.dma(final_rows[b % 3], out[b].rearrange("(t p) d -> p t d", p=P), r.ap[:], s)
        block = ctx.enter_context(nc.Block())
        for q in (pe, dve, act, pool, sync):
            q.number()

        @block.tensor
        def _(e):
            pe.emit(e)

        @block.vector
        def _(e):
            dve.emit(e)

        @block.scalar
        def _(e):
            e.preload_act_table_set(EXP_LN)
            act.emit(e)

        @block.gpsimd
        def _(e):
            pool.emit(e)

        @block.sync
        def _(e):
            sync.emit(e)
            for c in (spill, *final_rows):
                if c.count:
                    e.wait_ge(c.sem, c.count)


def laid_out(inputs):
    import numpy as np

    a = {k: np.asarray(v) for k, v in inputs.items()}
    m = {k: a["L0_attn_" + k] for k in ("W_in", "W_x", "W_dt", "W_out", "conv_w", "conv_b", "b_dt", "A_log", "Dp", "ln_g", "ln_b")}
    r = {
        "x": a["x"], "ctx": a["ctx_1024"], "mask_q": a["mask_Bx1xSxS2_ik1"], "mask_k": a["mask_BxS2_ik0"],
        "m_w_in": m["W_in"].T, "m_w_x": m["W_x"].T, "m_w_dt": m["W_dt"].T, "m_w_out": m["W_out"].T,
        "m_conv_w": m["conv_w"][:, 0, :], "m_conv_b": m["conv_b"], "m_b_dt": m["b_dt"], "m_a_log": m["A_log"],
        "m_dp": m["Dp"], "m_ln_g": m["ln_g"], "m_ln_b": m["ln_b"],
        "f_w1": a["L0_ffn_W1"].T, "f_b1": a["L0_ffn_b1"], "f_w2": a["L0_ffn_W2"].T, "f_b2": a["L0_ffn_b2"],
        "a_wo": a["L1_attn_Wo"], "a_gamma": a["L1_attn_gamma"], "a_beta": a["L1_attn_beta"],
        "g_gate": a["L1_ffn_w_gate"], "g_up": a["L1_ffn_w_up"], "g_down": a["L1_ffn_w_down"],
    }
    for w in ("q", "k", "v", "o"):
        r["c_w" + w] = a["L0_xattn_w" + w].T
        r["c_b" + w] = a["L0_xattn_b" + w]
        r["p_w" + w] = a["L1_xattn_W" + w]
    for w in ("q", "k", "v"):
        t = a["L1_attn_W" + w].transpose(1, 0, 2)
        r["a_w" + w] = t.reshape(t.shape[0], -1)
    for n in ("ln_m_w", "ln_m_b", "ln_l_w", "ln_l_b"):
        r["p_" + n] = a["L1_xattn_" + n]
    for n in ("m_conv_b", "m_b_dt", "m_dp", "m_ln_g", "m_ln_b", "f_b1", "c_bq", "c_bk",
              "p_ln_m_w", "p_ln_m_b", "p_ln_l_w", "p_ln_l_b"):
        r[n] = r[n].reshape(-1, P).T
    return {k: np.ascontiguousarray(v) for k, v in r.items()}


def kernel(**inputs):
    import concourse.bacc as bacc
    from concourse.bass_utils import run_bass_kernel_spmd

    arrays = laid_out(inputs)
    nc = bacc.Bacc("TRN2", target_bir_lowering=False, num_devices=1)
    ins = {n: nc.dram_tensor(n, a.shape, mybir.dt.from_np(a.dtype), kind="ExternalInput").ap()
           for n, a in arrays.items()}
    out = nc.dram_tensor("out", arrays["x"].shape, F32, kind="ExternalOutput").ap()
    decoder_kernel(nc, ins, out)
    return run_bass_kernel_spmd(nc, [arrays], core_ids=[0]).results[0]["out"]
```

```python
from contextlib import ExitStack

import concourse.bass as bass
from concourse import mybir

F32 = mybir.dt.float32
BF16 = mybir.dt.bfloat16
I32 = mybir.dt.int32
I16 = mybir.dt.int16
U16 = mybir.dt.uint16
ALU = mybir.AluOpType
ACT = mybir.ActivationFunctionType
AX = mybir.AxisListType
RMAX = bass.bass_isa.ReduceOp.max
RADD = bass.bass_isa.ReduceOp.add

P = 128
BANK = 512
NEG = -1e30
RNE = 12582912.0
EXP_LN = "natural_log_exp_and_others"




def columns(ap):
    n = 1
    for size in ap.shape[1:]:
        n *= size
    return n


class Later:

    def __init__(self, engine):
        self.engine = engine

    def matmul(self, out, lhs, *a, **k):
        passes = 1 if lhs.dtype == BF16 else 4
        return columns(out) * passes, lambda: self.engine.matmul(out, lhs, *a, **k)

    def transpose(self, out, *a, **k):
        return columns(out), lambda: self.engine.transpose(out, *a, **k)

    def activation(self, out, *a, **k):
        return columns(out), lambda: self.engine.activation(out, *a, **k)

    def memset(self, out, *a, **k):
        return columns(out), lambda: self.engine.memset(out, *a, **k)

    def tensor_copy(self, out, *a, **k):
        return columns(out), lambda: self.engine.tensor_copy(out, *a, **k)

    def tensor_tensor(self, out, *a, **k):
        return columns(out), lambda: self.engine.tensor_tensor(out, *a, **k)

    def tensor_scalar(self, out, *a, **k):
        return columns(out), lambda: self.engine.tensor_scalar(out, *a, **k)

    def scalar_tensor_tensor(self, out, *a, **k):
        return columns(out), lambda: self.engine.scalar_tensor_tensor(out, *a, **k)

    def tensor_tensor_scan(self, out, *a, **k):
        return columns(out), lambda: self.engine.tensor_tensor_scan(out, *a, **k)

    def tensor_reduce(self, out, in_, *a, **k):
        return columns(in_), lambda: self.engine.tensor_reduce(out, in_, *a, **k)

    def reciprocal(self, out, *a, **k):
        return columns(out), lambda: self.engine.reciprocal(out, *a, **k)

    def bn_stats(self, out, in_, *a, **k):
        return columns(in_), lambda: self.engine.bn_stats(out, in_, *a, **k)

    def bn_aggr(self, out, in_, *a, **k):
        return columns(in_), lambda: self.engine.bn_aggr(out, in_, *a, **k)

    def affine_select(self, out, *a, **k):
        return columns(out), lambda: self.engine.affine_select(out, *a, **k)

    def partition_all_reduce(self, out, *a, **k):
        return columns(out), lambda: self.engine.partition_all_reduce(out, *a, **k)

    def copy_predicated(self, out, *a, **k):
        return columns(out), lambda: self.engine.copy_predicated(out, *a, **k)

    def preload_act_table_set(self, *a, **k):
        return 1400, lambda: self.engine.preload_act_table_set(*a, **k)

    def dma_start(self, out, in_):
        return columns(out), lambda: self.engine.dma_start(out, in_)


class Step:

    def __init__(self, queue, issue, after, cost):
        self.queue, self.issue, self.after, self.cost, self.end = queue, issue, after, cost, 0.0
        self.sem, self.value, self.amount, self.wanted = None, 0, 1, False


HOP = 0.15


class Queue:

    made = None

    def __init__(self, engine, sem, fixed, column):
        self.later, self.sem, self.steps = Later(engine), sem, []
        self.fixed, self.column, self.clock = fixed, column, 0.0

    def __call__(self, instruction, *after):
        length, issue = instruction(self.later)
        step = Step(self, issue, [a for a in after if a is not None], self.fixed + self.column * length)
        for a in step.after:
            a.wanted = True
        if Queue.made is None:
            self.add(step)
        else:
            Queue.made.append(step)
        return step

    def add(self, step):
        start = max([self.clock] + [a.end + HOP for a in step.after])
        self.clock = step.end = start + step.cost
        self.steps.append(step)

    def dma(self, counter, out, in_, *after):
        step = self(lambda e: e.dma_start(out, in_), *after)
        step.cost = 0.1
        counter.count += 16
        step.sem, step.value, step.amount, step.wanted = counter.sem, counter.count, 16, True
        return step

    def number(self):
        count = 0
        for s in self.steps:
            if s.wanted and s.sem is None:
                count += 1
                s.sem, s.value = self.sem, count

    def emit(self, engine):
        reached = {}
        for s in self.steps:
            for a in s.after:
                if reached.get(id(a.sem), 0) < a.value:
                    engine.wait_ge(a.sem, a.value)
                    reached[id(a.sem)] = a.value
            made = s.issue()
            if s.wanted:
                made.then_inc(s.sem, s.amount)


class Counter:

    def __init__(self, sem):
        self.sem, self.count = sem, 0


class Slot:

    def __init__(self, ap, free=None):
        self.ap, self.free = ap, free


class Ring:

    def __init__(self, slots):
        self.slots, self.at = slots, -1

    def next(self):
        self.at = (self.at + 1) % len(self.slots)
        return self.slots[self.at]


def interleave(strands, weights):
    live = [[start, length, steps, name, []] for name, start, length, steps in strands]
    while live:
        ready = []
        for s in list(live):
            more = None
            while not s[4] and more is not WAIT:
                Queue.made = s[4]
                more = next(s[2], END)
                Queue.made = None
                if more is END and not s[4]:
                    live.remove(s)
                    break
            if s[4]:
                ready.append(s)
        assert ready or not live, "each strand waits for another"
        if not ready:
            break
        behind = min(s[0] for s in ready)
        best = None
        for s in ready:
            step = s[4][0]
            now = step.queue.clock
            start = max([now] + [a.end + HOP for a in step.after])
            score = (start - now) * weights.get(step.queue, 0.0) + AHEAD * (s[0] - behind)
            if best is None or score < best[0]:
                best = (score, s)
        s = best[1]
        step = s[4].pop(0)
        step.queue.add(step)
        if weights.get(step.queue, 0.0) >= 1.0:
            s[0] += step.cost / s[1]


WAIT, END = "wait", "end"
AHEAD = 90.0
M_US, A_US, X_US = 107.0, 143.0, 118.0
A_START, X_START = 1.0, 2.18

def decoder_kernel(nc, I, out):
    B, T, D = I["x"].shape
    S2 = I["ctx"].shape[1]
    NT, ND = T // P, D // P
    DI = I["m_w_out"].shape[0]
    NI = DI // P
    NS = I["m_a_log"].shape[1]
    DR = I["m_w_dt"].shape[0]
    KC = I["m_conv_w"].shape[1]
    H = 16
    HD0 = D // H
    F0 = I["f_w1"].shape[1]
    NF0 = F0 // P
    E = I["a_wq"].shape[1]
    HD = E // H
    NE = E // P
    F1 = I["g_gate"].shape[0]
    NF1 = F1 // P
    KEYS = T + S2
    NK = 3
    assert T == 2 * P and D == 2 * P and HD == 64 and NS == 16 and KEYS < NK * P

    ctx = ExitStack()
    with ctx:
        def counter(name):
            return Counter(ctx.enter_context(nc.semaphore(name)))

        pe, dve, act, pool, sync = (
            Queue(engine, ctx.enter_context(nc.semaphore(n)), fixed, column)
                for engine, n, fixed, column in (
                    (nc.tensor, "pe_done", 0.01, 0.42e-3), (nc.vector, "dve_done", 0.07, 1.05e-3),
                    (nc.scalar, "act_done", 0.2, 0.7e-3), (nc.gpsimd, "pool_done", 0.15, 2.1e-3),
                    (nc.sync, "sync_done", 0.1, 0.0)))
        weights = {pe: 1.0, dve: 1.0, act: 0.5, pool: 0.3}
        const_load = counter("const_load")
        weight_load = [counter(f"weight_load{i}") for i in range(8)]
        x_load, ctx_a_load, mask_a_load, ctx_x_load, mask_x_load, w_in_load, shared_load, spill = (counter(n) for n in (
            "x_load", "ctx_a_load", "mask_a_load", "ctx_x_load", "mask_x_load", "w_in_load", "shared_load", "spill"))
        w1_load, w1_store = counter("w1_load"), counter("w1_store")
        reload_rows, final_rows = ([counter(f"{n}{i}") for i in range(3)] for n in ("reload_rows", "final_rows"))

        def sb(scope, name, shape, dt=F32):
            return scope.enter_context(nc.sbuf_tensor(name, shape, dt))

        banks = [ctx.enter_context(nc.psum_tensor(f"bank{i}", [P, BANK], F32)) for i in range(8)]
        x5_dram = nc.dram_tensor("x5_spill", (B, T, D), F32)
        x5_dram = x5_dram.ap() if hasattr(x5_dram, "ap") else x5_dram

        w1_dram = nc.dram_tensor("w1_ternary", (P, ND, F0), F32)
        w1_dram = w1_dram.ap() if hasattr(w1_dram, "ap") else w1_dram

        ident = sb(ctx, "ident", [P, P])
        zeroed = dve(lambda e: e.memset(ident[:], 0.0))
        ident_ready = pool(lambda e: e.affine_select(
            out=ident[:], in_=ident[:], compare_op=ALU.not_equal, fill=1.0, base=0,
            pattern=[[-1, P]], channel_multiplier=1), zeroed)
        amax5 = sb(ctx, "amax5", [P, B])

        def layernorm(scope_tiles, src, dst, eps, rows, tiles, *after, eng2=None):
            st, mv, r, t = scope_tiles
            n = tiles
            for i in range(n):
                s = dve(lambda e: e.bn_stats(st[0:rows, i, :], src(i)), *after)
            for i in range(n):
                s = dve(lambda e: e.bn_aggr(mv[0:rows, i, :], st[0:rows, i, :]), s)
            v = mv[0:rows, 0:n, 1]
            s0 = dve(lambda e: e.tensor_scalar(t[0:rows, 3, 0:n], v, eps, None, ALU.add), s)
            s1 = act(lambda e: e.activation(t[0:rows, 0, 0:n], t[0:rows, 3, 0:n], ACT.Ln), s0)
            s2 = act(lambda e: e.activation(r[0:rows, 0:n], t[0:rows, 0, 0:n], ACT.Exp, scale=-0.5), s1)
            s3 = dve(lambda e: e.tensor_tensor(t[0:rows, 1, 0:n], r[0:rows, 0:n], r[0:rows, 0:n], ALU.mult), s2)
            s4 = dve(lambda e: e.tensor_tensor(t[0:rows, 2, 0:n], t[0:rows, 1, 0:n], t[0:rows, 3, 0:n], ALU.mult), s3)
            s5 = dve(lambda e: e.tensor_scalar(t[0:rows, 2, 0:n], t[0:rows, 2, 0:n], -0.5, 1.5, ALU.mult, ALU.add), s4)
            s6 = dve(lambda e: e.tensor_tensor(r[0:rows, 0:n], r[0:rows, 0:n], t[0:rows, 2, 0:n], ALU.mult), s5)
            for i in range(n):
                s = dve(lambda e: e.tensor_scalar(dst(i), src(i), mv[0:rows, i, 0:1], r[0:rows, i:i + 1],
                                                       ALU.subtract, ALU.mult), s6)
            return s

        def norm_tiles(scope, name, n):
            return (sb(scope, name + "_st", [P, n, 6]), sb(scope, name + "_mv", [P, n, 2]),
                    sb(scope, name + "_r", [P, n]), sb(scope, name + "_t", [P, 4, n]))

        ph1 = ctx.enter_context(ExitStack())
        W = {}

        def weight(name, shape, src, load=0):
            W[name] = sb(ph1, name + "_sb", shape)
            return sync.dma(weight_load[load], W[name][:], src)

        def chunks(ap):
            return ap.rearrange("(c p) n -> p c n", p=P)

        weight("m_w_x", [P, NI, DR + 2 * NS], chunks(I["m_w_x"]))
        weight("m_w_dt", [DR, DI], I["m_w_dt"])
        weight("m_w_out", [P, NI, D], chunks(I["m_w_out"]))
        weight("m_conv_w", [P, NI, KC], chunks(I["m_conv_w"]))
        weight("m_a_log", [P, NI, NS], chunks(I["m_a_log"]))
        for n in ("m_conv_b", "m_b_dt", "m_dp"):
            weight(n, [P, NI], I[n])
        for n in ("m_ln_g", "m_ln_b"):
            mamba_loaded = weight(n, [P, ND], I[n])
        shared = Slot(sb(ph1, "cross_or_a_wo", [P, NE, D]))
        cross = ("c_wq", "c_wk", "c_wv", "c_wo")
        for i, n in enumerate(cross):
            W[n] = shared.ap[:, i * ND:(i + 1) * ND, :]
        W["a_wo"] = shared.ap[:]
        w1_or_wv = Slot(sb(ph1, "w1_or_a_wv", [P, ND, F0]))
        W["f_w1"] = W["a_wv"] = w1_or_wv.ap[:]
        assert F0 == E and len(cross) * ND == NE

        def load_cross():
            for n in cross:
                shared.ready = sync.dma(shared_load, W[n], chunks(I[n]), shared.free)

        load_cross()
        for n in ("c_bq", "c_bk"):
            weight(n, [P, ND], I[n], 1)
        for n in ("c_bv", "c_bo"):
            cross_loaded = weight(n, [P, D], I[n].partition_broadcast(P), 1)
        w1_or_wv.ready = sync.dma(w1_load, W["f_w1"], chunks(I["f_w1"]))
        weight("f_b1", [P, NF0], I["f_b1"], 2)
        weight("f_b2", [P, D], I["f_b2"].partition_broadcast(P), 2)
        ffn_loaded = weight("f_w2", [P, NF0, D], chunks(I["f_w2"]), 2)
        for n in ("a_wq", "a_wk"):
            weight(n, [P, ND, E], chunks(I[n]), 3)
        for n in ("a_gamma", "a_beta"):
            attn_loaded = weight(n, [P, D], I[n].partition_broadcast(P), 3)
        for n in ("p_wq", "p_wk", "p_wv"):
            weight(n, [P, ND, E], chunks(I[n]), 4)
        weight("p_wo", [P, NE, D], chunks(I["p_wo"]), 4)
        for n in ("p_ln_m_w", "p_ln_m_b", "p_ln_l_w", "p_ln_l_b"):
            perc_loaded = weight(n, [P, ND], I[n], 4)

        a_neg = sb(ph1, "a_neg", [P, NI, NS])
        w_bc = sb(ph1, "w_bc", [P, NI, 3, 2 * NS])
        sel = sb(ph1, "sel", [P, P], BF16)
        ident_bf = sb(ph1, "ident_bf", [P, P], BF16)
        causal = sb(ph1, "causal", [P, P], BF16)
        head_of = sb(ph1, "head_of", [P, P // HD0])
        ones_bf = sb(ph1, "ones_bf", [1, P], BF16)

        a_exp = act(lambda e: e.activation(a_neg[:], W["m_a_log"][:], ACT.Exp), mamba_loaded)
        a_ready = dve(lambda e: e.tensor_scalar(a_neg[:], a_neg[:], -1.0, None, ALU.mult), a_exp)
        for r in range(3):
            bc_w_ready = dve(lambda e: e.tensor_copy(w_bc[:, :, r, :], W["m_w_x"][:, :, DR:DR + 2 * NS]), mamba_loaded)
        ident_bf_ready = dve(lambda e: e.tensor_copy(ident_bf[:], ident[:]), ident_ready)
        s = dve(lambda e: e.tensor_tensor(sel[:, 0:2 * NS], ident[:, 0:2 * NS], ident[:, 2 * NS:4 * NS], ALU.add), ident_ready)
        sel_ready = dve(lambda e: e.tensor_tensor(sel[:, 0:2 * NS], sel[:, 0:2 * NS], ident[:, 4 * NS:6 * NS], ALU.add), s)
        s = dve(lambda e: e.memset(causal[:], 0.0))
        causal_ready = pool(lambda e: e.affine_select(
            out=causal[:], in_=causal[:], compare_op=ALU.is_ge, fill=NEG, base=0,
            pattern=[[-1, P]], channel_multiplier=1), s)
        heads_ready = dve(lambda e: e.tensor_reduce(
            head_of[:], ident[:].rearrange("p (h d) -> p h d", d=HD0), AX.X, ALU.add), ident_ready)
        ones_ready = dve(lambda e: e.memset(ones_bf[:], 1.0))

        x_in = Slot(sb(ph1, "x_in", [P, NT, D]))
        m_tmp = sb(ph1, "m_tmp", [P, NI, T])
        m_hT = m_tmp[:, 0:ND, :]
        m_rows = m_tmp[:, ND:NI, :]
        xi_pad = sb(ph1, "xi_pad", [P, NI, KC - 1 + T])
        zT = sb(ph1, "zT", [P, NI, T])
        uT = sb(ph1, "uT", [P, NI, T])
        dtT = sb(ph1, "dtT", [P, NI, T])
        dt_low = sb(ph1, "dt_low", [DR, T])
        bc_split = sb(ph1, "bc_split", [6 * NS, T], BF16)
        decay = [Slot(sb(ph1, f"decay{i}", [P, 2, T])) for i in range(3)]
        states = sb(ph1, "states", [P, NI * 2 * T])
        state = [Slot(states[:, i * 2 * T:(i + 1) * 2 * T].rearrange("p (k t) -> p k t", k=2))
                 for i in range(NI)]
        w_in = Slot(states[:].rearrange("p (c n) -> p c n", c=ND))
        series = states[:, 0:NI * T].rearrange("p (c t) -> p c t", c=NI)
        small = states[:, NI * T:].rearrange("p (c t) -> p c t", c=NI).bitcast(I32)
        y_sum = sb(ph1, "y_sum", [P, NI, T])
        m_norm = norm_tiles(ph1, "m_norm", NT)
        m_banks = Ring([Slot(b[:]) for b in banks[0:2]])
        carry = Slot(sb(ph1, "x1", [P, NT, D]))

        s = dve(lambda e: e.memset(xi_pad[:, :, 0:KC - 1], 0.0))
        for i in range(len(decay)):
            pads_ready = dve(lambda e: e.memset(decay[i].ap[:, :, 0:1], 0.0))
        mamba_consts = (a_ready, bc_w_ready, sel_ready, pads_ready)

        PW = NK * P

        class Strand:

            def __init__(self, name, keys, first_bank, n_banks, attn_columns):
                self.kvT = sb(ph1, name + "_kvT", [P, ND, KEYS])
                self.aT = sb(ph1, name + "_aT", [P, NE, T])
                self.v0 = T + keys
                pad = (keys + P - 1) // P * P
                self.pairs = [Slot(sb(ph1, f"{name}_pair{i}", [P, self.v0 + pad])) for i in range(3)]
                self.rows = self.pairs[0].ap[:, 0:NT * D].rearrange("p (t d) -> p t d", t=NT)
                self.attn = sb(ph1, name + "_attn", [P, attn_columns])
                turned = (attn_columns - 4 * PW) // 2
                self.probs = [Slot(self.attn[:, i * PW:(i + 1) * PW]) for i in range(4)]
                self.probsT = [Slot(self.attn[:, 4 * PW + i * turned:4 * PW + (i + 1) * turned]) for i in range(2)]
                self.stat = sb(ph1, name + "_stat", [P, 8, 6])
                self.stat_free = [None] * 8
                self.norm = norm_tiles(ph1, name + "_norm", NT)
                self.banks = Ring([Slot(b[:]) for b in banks[first_bank:first_bank + n_banks]])
                self.gather = Slot(banks[first_bank + n_banks][:, 0:T])
                self.context = Slot(sb(ph1, name + "_context", [P, D]))

        A = Strand("a", T, 2, 2, NT * H * S2)
        X = Strand("x", KEYS, 5, 2, 4 * PW + 2 * NK * T)
        mask_in = Slot(sb(ph1, "mask_in", [P, NT, S2], I32)[:])
        key_mask = Slot(sb(ph1, "key_mask", [1, S2], I32)[:])
        x_a = sb(ph1, "x_a", [P, NT, D])
        between = [Slot(sb(ph1, f"x4_{i}", [P, NT, D])[:]) for i in range(2)]
        bias_row = sb(ph1, "bias_row", [1, S2], BF16)
        bound = sb(ph1, "bound", [P, NT, S2])

        tern = A.attn[:, 0:F0 * ND]
        tsum = A.stat[:, 0, :]
        tern_free = None
        for n in ("f_w1", "f_w2"):
            w = (W[n] if n == "f_w1" else W[n][:]).rearrange("p c n -> p (c n)")
            cnt = float(F0 * D)
            t = tern
            s = dve(lambda e: e.tensor_reduce(tsum[:, 0:1], w, AX.X, ALU.add, apply_absolute_value=True),
                    w1_or_wv.ready, ffn_loaded, tern_free)
            s = pool(lambda e: e.partition_all_reduce(tsum[:, 1:2], tsum[:, 0:1], P, RADD), s)
            s = dve(lambda e: e.tensor_scalar(tsum[:, 2:3], tsum[:, 1:2], 1.0 / cnt, 1e-8, ALU.mult, ALU.max), s)
            s = dve(lambda e: e.reciprocal(tsum[:, 3:4], tsum[:, 2:3]), s)
            s = dve(lambda e: e.tensor_scalar(t, w, tsum[:, 3:4], RNE, ALU.mult, ALU.add), s)
            s = dve(lambda e: e.tensor_scalar(t, t, RNE, 1.0, ALU.subtract, ALU.min), s)
            s = dve(lambda e: e.tensor_scalar(t, t, -1.0, None, ALU.max), s)
            s = dve(lambda e: e.tensor_tensor(t, t, w, ALU.subtract), s)
            s = tern_free = dve(lambda e: e.tensor_tensor(w, w, t, ALU.add), s)
            if n == "f_w1":
                w1_or_wv.ready = s
                w1_saved = sync.dma(w1_store, w1_dram, W[n], s)
        ternary_ready = s

        for sl in X.probs:
            sl.free = dve(lambda e: e.memset(sl.ap[:, KEYS:PW], 0.0))
        for sl in X.pairs:
            sl.free = dve(lambda e: e.memset(sl.ap[:, X.v0 + T:], 0.0))
        pads2_ready = sl.free
        kblk = A.aT[:, NE // 2:, :].rearrange("p c t -> p (c t)")[:, 0:P // HD0 * S2]
        vpad = sb(ph1, "vpad", [S2, H, 2 * HD0])
        vpad_ready = dve(lambda e: e.memset(vpad[:], 0.0))
        last_turn = {}
        handed = {"x1": 0, "x1 read": 0, "x4": 0, "x4 read": 0}

        def mamba(b):
            xs = x_in
            load = sync.dma(x_load, xs.ap[:], I["x"][b].rearrange("(t p) d -> p t d", p=P), xs.free)
            wi = sync.dma(w_in_load, w_in.ap, chunks(I["m_w_in"]), *(sl.free for sl in state))
            m_work = m_banks.next()
            s = layernorm(m_norm, lambda i: xs.ap[:, i, :], lambda i: m_rows[:, i, :], 1e-6, P, NT, load)
            yield
            for t in range(NT):
                for c in range(ND):
                    m = pe(lambda e: e.transpose(m_work.ap[:, c * T + t * P:c * T + (t + 1) * P],
                                                           m_rows[:, t, c * P:(c + 1) * P], ident[:]),
                           s, m_work.free, ident_ready)
            for c in range(ND):
                h = dve(lambda e: e.tensor_scalar(m_hT[:, c, :], m_work.ap[:, c * T:(c + 1) * T],
                                                       W["m_ln_g"][:, c:c + 1], W["m_ln_b"][:, c:c + 1],
                                                       ALU.mult, ALU.add), m, mamba_loaded)
            m_work.free = h
            yield
            for j in range(NI):
                m_work = m_banks.next()
                for q in range(2):
                    for c in range(ND):
                        m = pe(lambda e: e.matmul(
                            m_work.ap[:, q * T:(q + 1) * T],
                            w_in.ap[:, c, (2 * j + q) * P:(2 * j + q + 1) * P], m_hT[:, c, :],
                            start=c == 0, stop=c == ND - 1), h, wi, m_work.free)
                dst = xi_pad[:, 2 * j:2 * j + 2, KC - 1:] if j < NI // 2 else zT[:, 2 * j - NI:2 * j - NI + 2, :]
                m_work.free = xi = act(lambda e: e.activation(
                    dst, m_work.ap.rearrange("p (q t) -> p q t", q=2), ACT.Copy), m)
                yield
            for c in range(NI):
                cv = dve(lambda e: e.tensor_scalar(uT[:, c, :], xi_pad[:, c, 0:T], W["m_conv_w"][:, c, 0:1],
                                                        W["m_conv_b"][:, c:c + 1], ALU.mult, ALU.add), xi)
                for k in range(1, KC):
                    cv = dve(lambda e: e.scalar_tensor_tensor(
                        uT[:, c, :], xi_pad[:, c, k:k + T], W["m_conv_w"][:, c, k:k + 1], uT[:, c, :],
                        ALU.mult, ALU.add), cv)
                if c % 2:
                    yield
            zs = act(lambda e: e.activation(zT[:], zT[:], ACT.Silu), xi)
            us = act(lambda e: e.activation(uT[:], uT[:], ACT.Silu), cv)
            act(lambda e: e.preload_act_table_set(EXP_LN))
            yield
            w_in_free = m
            m_work = m_banks.next()
            for c in range(NI):
                pe(lambda e: e.matmul(m_work.ap[0:DR, 0:T], W["m_w_x"][:, c, 0:DR], uT[:, c, :],
                                           start=c == 0, stop=c == NI - 1), us, m_work.free)
            for c in range(NI):
                m = pe(lambda e: e.matmul(m_work.ap[0:6 * NS, T:2 * T],
                                               w_bc[:, c, :, :].rearrange("p r n -> p (r n)"), uT[:, c, :],
                                               start=c == 0, stop=c == NI - 1), bc_w_ready)
            low = dve(lambda e: e.tensor_copy(dt_low[:], m_work.ap[0:DR, 0:T]), m)
            bcp = m_work.ap[0:6 * NS, T:2 * T]
            r = m_rows[0:6 * NS, 0, :]
            hi = m_hT[0:6 * NS, 0, :].bitcast(BF16)[:, 0:T]
            s = dve(lambda e: e.tensor_copy(hi, bcp), m)
            s1 = dve(lambda e: e.tensor_copy(bc_split[0:2 * NS, :], hi[0:2 * NS]), s, last_turn.get("bc"))
            s2 = dve(lambda e: e.tensor_tensor(r, bcp, hi, ALU.subtract), s)
            m_work.free = s2
            s3 = dve(lambda e: e.tensor_copy(hi, r), s2, s1)
            s4 = dve(lambda e: e.tensor_copy(bc_split[2 * NS:4 * NS, :], hi[2 * NS:4 * NS]), s3)
            s5 = dve(lambda e: e.tensor_tensor(r, r, hi, ALU.subtract), s3)
            bc_ready = dve(lambda e: e.tensor_copy(bc_split[4 * NS:6 * NS, :], r[4 * NS:6 * NS]), s5, s4)
            yield
            for q in range(2):
                m_work = m_banks.next()
                for c in range(2):
                    m = pe(lambda e: e.matmul(
                        m_work.ap[:, c * T:(c + 1) * T], W["m_w_dt"][:, (2 * q + c) * P:(2 * q + c + 1) * P],
                        dt_low[:], start=True, stop=True), low, m_work.free)
                for c in range(2):
                    v = dve(lambda e: e.tensor_scalar(
                        dtT[:, 2 * q + c, :], m_work.ap[:, c * T:(c + 1) * T],
                        W["m_b_dt"][:, 2 * q + c:2 * q + c + 1], None, ALU.add), m)
                m_work.free = v
            s = act(lambda e: e.activation(m_tmp[:], dtT[:], ACT.Abs), v, bc_ready)
            ex = act(lambda e: e.activation(m_tmp[:], m_tmp[:], ACT.Exp, scale=-1.0), s)
            one_plus = y_sum
            w1 = dve(lambda e: e.tensor_scalar(one_plus[:], m_tmp[:], 1.0, None, ALU.add), ex, last_turn.get("y"))
            dve(lambda e: e.tensor_scalar(small, m_tmp[:], 2.0 ** -8, None, ALU.is_lt), w_in_free)
            s = dve(lambda e: e.tensor_scalar(series, m_tmp[:], 1.0 / 3.0, -0.5, ALU.mult, ALU.add))
            s = dve(lambda e: e.tensor_tensor(series, series, m_tmp[:], ALU.mult), s)
            sr = dve(lambda e: e.scalar_tensor_tensor(series, series, 1.0, m_tmp[:], ALU.add, ALU.mult), s)
            s = dve(lambda e: e.scalar_tensor_tensor(m_tmp[:], one_plus[:], -1.0, m_tmp[:], ALU.add, ALU.subtract), w1)
            ln = act(lambda e: e.activation(one_plus[:], one_plus[:], ACT.Ln), s)
            yield
            s = dve(lambda e: e.tensor_tensor(one_plus[:], one_plus[:], m_tmp[:], ALU.subtract), ln)
            s = dve(lambda e: e.copy_predicated(one_plus[:], small, series), s, sr)
            dt = dve(lambda e: e.scalar_tensor_tensor(dtT[:], dtT[:], 0.0, one_plus[:], ALU.max, ALU.add), s)
            for c in range(NI):
                y0 = dve(lambda e: e.tensor_scalar(y_sum[:, c, :], uT[:, c, :], W["m_dp"][:, c:c + 1], None, ALU.mult), dt)
            dtu = dve(lambda e: e.tensor_tensor(uT[:], dtT[:], uT[:], ALU.mult), y0)
            yield
            summed = [y0] * NI
            for n in range(0, NS, 2):
                bank_b, bank_c = m_banks.next(), m_banks.next()
                for k in range(2):
                    mb = pe(lambda e: e.matmul(
                        bank_b.ap[:, k * T:(k + 1) * T], sel[0:6 * NS, n + k:n + k + 1].to_broadcast([6 * NS, P]),
                        bc_split[:], start=True, stop=True), bc_ready, sel_ready, bank_b.free)
                for k in range(2):
                    mc = pe(lambda e: e.matmul(
                        bank_c.ap[:, k * T:(k + 1) * T],
                        sel[0:6 * NS, NS + n + k:NS + n + k + 1].to_broadcast([6 * NS, P]),
                        bc_split[:], start=True, stop=True), bank_c.free)
                sc = [None] * NI

                def decays(c, n=n):
                    d = decay[(n // 2 * NI + c) % len(decay)]
                    for k in range(2):
                        d.ready = act(lambda e: e.activation(
                            d.ap[:, k, 1:T], dtT[:, c, 1:T], ACT.Exp, scale=a_neg[:, c, n + k:n + k + 1]),
                            dt, d.free, a_ready, pads_ready)

                for c in range(2):
                    decays(c)
                yield
                for c in range(NI):
                    out_t = state[c].ap
                    s = dve(lambda e, c=c, o=out_t: e.tensor_tensor(
                        o[:], uT[:, c:c + 1, :].to_broadcast([P, 2, T]),
                        bank_b.ap.rearrange("p (k t) -> p k t", k=2), ALU.mult), mb, dtu, state[c].free)
                    sc[c] = s
                bank_b.free = s
                yield
                for c in range(NI):
                    if c + 2 < NI:
                        decays(c + 2)
                    d = decay[(n // 2 * NI + c) % len(decay)]
                    f = state[c].ap[:].rearrange("p k t -> p (k t)")
                    g = d.ap[:].rearrange("p k t -> p (k t)")
                    d.free = sc[c] = dve(lambda e: e.tensor_tensor_scan(
                        f, g, f, 0.0, ALU.mult, ALU.add), d.ready, sc[c])
                yield
                for c in range(NI):
                    f = state[c].ap[:].rearrange("p k t -> p (k t)")
                    s = dve(lambda e: e.tensor_tensor(f, f, bank_c.ap, ALU.mult), sc[c], mc)
                    if c % 2:
                        for k in range(2):
                            for a in (c - 1, c):
                                ys = summed[a] = state[a].free = pool(lambda e: e.tensor_tensor(
                                    y_sum[:, a, :], y_sum[:, a, :], state[a].ap[:, k, :], ALU.add), s, summed[a])
                bank_c.free = s
                last_turn["bc"] = mc
                yield
            y = m_tmp
            yd = last_turn["y"] = dve(lambda e: e.tensor_tensor(y[:], y_sum[:], zT[:], ALU.mult), ys, zs)
            yield
            m_work = m_banks.next()
            for t in range(NT):
                for c in range(NI):
                    m = pe(lambda e: e.matmul(m_work.ap[:, t * D:(t + 1) * D], y[:, c, t * P:(t + 1) * P],
                                                        W["m_w_out"][:, c, :], start=c == 0, stop=c == NI - 1),
                           yd, m_work.free)
            yield
            while handed["x1 read"] < b:
                yield WAIT
            fl = lambda a: a.rearrange("p t d -> p (t d)")
            m_work.free = xs.free = s = dve(lambda e: e.scalar_tensor_tensor(
                fl(m_rows), fl(xs.ap[:]), 2.0, m_work.ap, ALU.mult, ALU.add), m)
            cy = carry
            cy.ready = layernorm(m_norm, lambda i: m_rows[:, i, :], lambda i: cy.ap[:, i, :], 1e-5, P, NT, s, cy.free)
            yield
            handed["x1"] = b + 1

        fl = lambda a: a.rearrange("p t d -> p (t d)")

        def transposed(st, src, dst, ready, dst_free, rows=P, tiles=NT, width=T):
            bank = st.banks.next()
            for t in range(tiles):
                for c in range(ND):
                    m = pe(lambda e: e.transpose(
                        bank.ap[:, c * width + t * P:c * width + t * P + rows],
                        src(t)[:, c * P:(c + 1) * P], ident[0:rows, 0:rows]), ready, bank.free)
            bank.free = s = dve(lambda e: e.tensor_copy(dst, bank.ap[:, 0:ND * width].rearrange("p (c t) -> p c t", c=ND)),
                                m, dst_free)
            return s

        def rows_out(st, lhs, n, w, *ready):
            bank = st.banks.next()
            for t in range(NT):
                for c in range(n):
                    m = pe(lambda e: e.matmul(bank.ap[:, t * D:(t + 1) * D], lhs[:, c, t * P:(t + 1) * P],
                                                        w[:, c, :], start=c == 0, stop=c == n - 1), *ready, bank.free)
            return bank, m

        def bcast(row):
            return row.unsqueeze(1).to_broadcast([P, NT, D])

        def attention(st, kind, qT, kT, wq, wk, wv, *ready):
            keys = T if kind == "causal" else KEYS
            per_head = 1 if kind == "causal" else NT
            units = [(h, t) for h in range(H) for t in range(per_head)]
            lag = 2 if kind == "causal" else 3
            made, turned = {}, {}
            outs = [None]

            def project(pair):
                sl = st.pairs[pair % 3]
                col = slice(pair * P, (pair + 1) * P)
                bank = st.banks.next()
                for c in range(ND):
                    m = pe(lambda e: e.matmul(bank.ap[:, 0:T], wq[:, c, col], qT[:, c, 0:T], start=c == 0,
                                                   stop=c == ND - 1), *ready, bank.free)
                bank.free = q = act(lambda e: e.activation(sl.ap[:, 0:T], bank.ap[:, 0:T], ACT.Copy,
                                                                      scale=HD ** -0.5), m, sl.free)
                bank = st.banks.next()
                for c in range(ND):
                    m = pe(lambda e: e.matmul(bank.ap[:, 0:keys], wk[:, c, col], kT[:, c, 0:keys],
                                                              start=c == 0, stop=c == ND - 1), *ready, bank.free)
                bank.free = k = dve(lambda e: e.tensor_copy(sl.ap[:, T:T + keys], bank.ap[:, 0:keys]), m, sl.free)
                bank = st.banks.next()
                nk = (keys + P - 1) // P
                for i in range(nk):
                    n = min(P, keys - i * P)
                    for c in range(ND):
                        m = pe(lambda e: e.matmul(
                            bank.ap[0:n, i * P:(i + 1) * P], kT[:, c, i * P:i * P + n], wv[:, c, col],
                            start=c == 0, stop=c == ND - 1), *ready, bank.free)
                v = act(lambda e: e.activation(sl.ap[:, st.v0:st.v0 + T], bank.ap[:, 0:T], ACT.Copy), m, sl.free)
                if nk == NK:
                    n = keys - 2 * P
                    v = act(lambda e: e.activation(sl.ap[0:n, st.v0 + T:st.v0 + T + P], bank.ap[0:n, T:T + P],
                                                              ACT.Copy), m)
                bank.free = v
                st.last_wv = m
                sl.q, sl.k, sl.v = q, k, v

            def scores(u):
                h, t = units[u]
                sl, o = st.pairs[h // 2 % 3], h % 2 * HD
                bank, pr, sums = st.banks.next(), st.probs[u % 4], st.stat[:, u % 8, :]
                qs = lambda i: sl.ap[o:o + HD, i * P:(i + 1) * P]
                if kind == "causal":
                    spans = [(0, P, 0), (P, T, 1)]
                    for a, n, i in spans:
                        pe(lambda e: e.matmul(bank.ap[:, a:a + n], qs(i), sl.ap[o:o + HD, T:T + n],
                                                             start=True, stop=False), sl.q, sl.k, bank.free)
                        m = pe(lambda e: e.matmul(bank.ap[:, a + n - P:a + n], ident_bf[:], causal[:],
                                                            start=False, stop=True),
                               causal_ready, ident_bf_ready)
                else:
                    spans = [(0, KEYS, t)]
                    pe(lambda e: e.matmul(bank.ap[:, 0:KEYS], qs(t), sl.ap[o:o + HD, T:T + KEYS], start=True, stop=False),
                       sl.q, sl.k, bank.free)
                    m = pe(lambda e: e.matmul(bank.ap[:, T:KEYS], ones_bf[:], bias_row[:], start=False, stop=True),
                           mask_done[0])
                for j, (a, n, i) in enumerate(spans):
                    mx = dve(lambda e: e.tensor_reduce(sums[:, j:j + 1], bank.ap[:, a:a + n], AX.X,
                                                                      ALU.max, negate=True), m, st.stat_free[u % 8])
                for j, (a, n, i) in enumerate(spans):
                    ex = act(lambda e: e.activation(
                        pr.ap[:, a:a + n], bank.ap[:, a:a + n], ACT.Exp, bias=sums[:, j:j + 1],
                        accum_out=sums[:, 2 + j:3 + j]), mx, pr.free)
                bank.free = ex
                ns = len(spans)
                rc = dve(lambda e: e.reciprocal(sums[:, 4:4 + ns], sums[:, 2:2 + ns]), ex)
                for j, (a, n, i) in enumerate(spans):
                    s = pool(lambda e: e.tensor_scalar(
                        pr.ap[:, a:a + n], pr.ap[:, a:a + n], sums[:, 4 + j:5 + j], 1.0, ALU.mult, ALU.mult), rc)
                st.stat_free[u % 8] = s
                made[u] = s

            def turn_probs(u):
                h, t = units[u]
                bank, pr, pt = st.banks.next(), st.probs[u % 4], st.probsT[h % 2]
                for i in range(NK):
                    m = pe(lambda e: e.transpose(bank.ap[:, i * P:(i + 1) * P], pr.ap[:, i * P:(i + 1) * P],
                                                      ident[:]), made[u], bank.free)
                pr.free = m
                if kind == "causal":
                    s = dve(lambda e: e.tensor_copy(pt.ap[:, 0:PW], bank.ap[:, 0:PW]), m, pt.free)
                else:
                    dst = pt.ap.rearrange("p (k q) -> p k q", q=T)[:, :, t * P:(t + 1) * P]
                    src = bank.ap[:, 0:PW].rearrange("p (k q) -> p k q", q=P)
                    if u % 2:
                        s = dve(lambda e: e.tensor_copy(dst, src), m, pt.free)
                    else:
                        s = act(lambda e: e.activation(dst, src, ACT.Copy), m, pt.free)
                bank.free = s
                turned[u] = s

            def weigh(h):
                sl, o, pt = st.pairs[h // 2 % 3], h % 2 * HD, st.probsT[h % 2]
                g = st.gather.ap
                us = [turned[u] for u in range(len(units)) if units[u][0] == h]
                parts = [(0, 0, T, 0), (1, T, PW, P)] if kind == "causal" else [(i, i * T, (i + 1) * T, 0) for i in range(NK)]
                for j, (i, a, z, q0) in enumerate(parts):
                    m = pe(lambda e: e.matmul(
                        g[o:o + HD, q0:T], sl.ap[:, st.v0 + i * P + o:st.v0 + i * P + o + HD], pt.ap[:, a:z],
                        start=j == 0, stop=j == len(parts) - 1), *us, sl.v, st.gather.free, pads2_ready)
                pt.free = m
                if h % 2:
                    sl.free = m
                    st.gather.free = outs[0] = act(lambda e: e.activation(st.aT[:, h // 2, :], g, ACT.Copy), m)

            project(0)
            yield
            total = len(units)
            upp = total // NE
            for u in range(total + lag + 1):
                if u < total:
                    scores(u)
                if 0 <= u - lag < total:
                    turn_probs(u - lag)
                v = u - lag - 1
                if 0 <= v < total and (v + 1) % per_head == 0:
                    weigh(units[v][0])
                yield
                if (u + 1) % upp == upp - 1 and (u + 1) // upp + 1 < NE:
                    project((u + 1) // upp + 1)
                    yield
            st.out = outs[0]

        mask_done = [None]

        def load_context_a(b):
            cs, ms = A.context, mask_in
            cs.ready = sync.dma(ctx_a_load, cs.ap[0:S2, :], I["ctx"][b], cs.free)
            ms.ready = sync.dma(mask_a_load, ms.ap, I["mask_q"][b, 0].rearrange("(t p) k -> p t k", p=P), ms.free)

        def load_context_x(b):
            cs, ms = X.context, key_mask
            cs.ready = sync.dma(ctx_x_load, cs.ap[0:S2, :], I["ctx"][b], cs.free)
            ms.ready = sync.dma(mask_x_load, ms.ap, I["mask_k"][b:b + 1, :], ms.free)

        def first_layer_and_causal(b):
            while handed["x1"] <= b:
                yield WAIT
            st = A
            cy, cs, ms, xT = carry, A.context, mask_in, A.kvT[:, :, 0:T]
            x1T = transposed(st, lambda t: cy.ap[:, t, :], xT, cy.ready, None)
            ctxT = st.kvT[:, :, T:KEYS]
            c_T = cs.free = transposed(st, lambda t: cs.ap[0:S2, :], ctxT, cs.ready, None, rows=S2, tiles=1, width=S2)
            s = dve(lambda e: e.tensor_scalar(bound[:], ms.ap, 0.0, NEG, ALU.is_equal, ALU.mult), ms.ready)
            bd = ms.free = dve(lambda e: e.tensor_scalar(bound[:], bound[:], 100.0, None, ALU.add), s)
            if b + 1 < B:
                load_context_a(b + 1)
            yield
            G = P // HD0
            qT0 = st.pairs[0].ap[:, 0:ND * T].rearrange("p (c t) -> p c t", c=ND)
            kT0 = st.pairs[1].ap[:, 0:ND * S2].rearrange("p (c t) -> p c t", c=ND)
            bank = st.banks.next()
            for c2 in range(ND):
                for c in range(ND):
                    m = pe(lambda e: e.matmul(bank.ap[:, c2 * T:(c2 + 1) * T], W["c_wq"][:, c, c2 * P:(c2 + 1) * P],
                                                          xT[:, c, :], start=c == 0, stop=c == ND - 1),
                           x1T, bank.free, cross_loaded, shared.ready)
            for c2 in range(ND):
                q = dve(lambda e: e.tensor_scalar(
                    qT0[:, c2, :], bank.ap[:, c2 * T:(c2 + 1) * T], W["c_bq"][:, c2:c2 + 1], HD0 ** -0.5,
                    ALU.add, ALU.mult), m, st.pairs[0].free)
            bank.free = q
            bank = st.banks.next()
            for c2 in range(ND):
                for c in range(ND):
                    m = pe(lambda e: e.matmul(
                        bank.ap[:, c2 * S2:(c2 + 1) * S2], W["c_wk"][:, c, c2 * P:(c2 + 1) * P], ctxT[:, c, :],
                        start=c == 0, stop=c == ND - 1), c_T, bank.free)
            for c2 in range(ND):
                k = act(lambda e: e.activation(
                    kT0[:, c2, :], bank.ap[:, c2 * S2:(c2 + 1) * S2], ACT.Identity, bias=W["c_bk"][:, c2:c2 + 1]),
                    m, st.pairs[1].free)
            bank.free = k
            bank = st.banks.next()
            for c in range(ND):
                m = pe(lambda e: e.matmul(bank.ap[0:S2, 0:D], ctxT[:, c, :], W["c_wv"][:, c, :],
                                                          start=c == 0, stop=c == ND - 1), c_T, bank.free)
            for par in range(2):
                v = dve(lambda e: e.tensor_tensor(
                    vpad[:, par::2, par * HD0:(par + 1) * HD0],
                    bank.ap[0:S2, 0:D].rearrange("k (h d) -> k h d", d=HD0)[:, par::2, :],
                    W["c_bv"][0:S2, :].rearrange("k (h d) -> k h d", d=HD0)[:, par::2, :], ALU.add), m, vpad_ready)
            bank.free = v
            yield
            sc = [st.attn[:, t * H * S2:(t + 1) * H * S2].rearrange("p (h k) -> p h k", k=S2) for t in range(NT)]
            half = G // 2
            sdone = [None] * NT
            for c in range(ND):
                kb = dve(lambda e: e.tensor_tensor(
                    kblk.rearrange("p (h k) -> p h k", k=S2), kT0[:, c:c + 1, :].to_broadcast([P, G, S2]),
                    head_of[:].unsqueeze(2).to_broadcast([P, G, S2]), ALU.mult), k, kblk_free[0], heads_ready)
                for t in range(NT):
                    for g in range(2):
                        bank = st.banks.next()
                        kblk_free[0] = m = pe(lambda e: e.matmul(
                            bank.ap[:, 0:half * S2], qT0[:, c, t * P:(t + 1) * P],
                            kblk[:, g * half * S2:(g + 1) * half * S2], start=True, stop=True), q, kb, bank.free)
                        h0 = c * G + g * half
                        bank.free = sdone[t] = dve(lambda e: e.scalar_tensor_tensor(
                            sc[t][:, h0:h0 + half, :], bank.ap[:, 0:half * S2].rearrange("p (h k) -> p h k", k=S2), -100.0,
                            bound[:, t:t + 1, :].to_broadcast([P, half, S2]), ALU.max, ALU.min), m, bd)
                        yield
            pm = []
            for t in range(NT):
                m = dve(lambda e: e.tensor_reduce(l0_stat[:, t, 0, :], sc[t], AX.X, ALU.max), sdone[t])
                s = dve(lambda e: e.tensor_tensor(sc[t], sc[t], l0_stat[:, t, 0, :].unsqueeze(2).to_broadcast([P, H, S2]),
                                                       ALU.subtract), m)
                s = act(lambda e: e.activation(sc[t], sc[t], ACT.Exp), s)
                m = dve(lambda e: e.tensor_reduce(l0_stat[:, t, 1, :], sc[t], AX.X, ALU.add), s)
                m = dve(lambda e: e.reciprocal(l0_stat[:, t, 0, :], l0_stat[:, t, 1, :]), m)
                pm.append(pool(lambda e: e.tensor_tensor(
                    sc[t], sc[t], l0_stat[:, t, 0, :].unsqueeze(2).to_broadcast([P, H, S2]), ALU.mult), m))
                yield
            pT = [Slot(st.aT[:, NE // 2 + 2 * i:NE // 2 + 2 * i + 2, :].rearrange("p c t -> p (c t)"), kblk_free[0]) for i in range(2)]
            a0 = st.aT[:, 0:ND, :]
            for hp in range(H // 2):
                bank, pt = st.banks.next(), pT[hp % 2]
                for j in range(2):
                    for t in range(NT):
                        m = pe(lambda e: e.transpose(
                            bank.ap[0:S2, j * T + t * P:j * T + (t + 1) * P], sc[t][:, 2 * hp + j, :], ident[:]),
                            pm[t], bank.free)
                bank.free = s = act(lambda e: e.activation(pt.ap[0:S2, :], bank.ap[0:S2, :], ACT.Copy), m, pt.free)
                o = hp % 4 * 2 * HD0
                g = st.gather.ap[o:o + 2 * HD0, :]
                for j in range(2):
                    pt.free = m = pe(lambda e: e.matmul(
                        g, vpad[:, 2 * hp + j, :], pt.ap[0:S2, j * T:(j + 1) * T], start=j == 0, stop=j == 1,
                        tile_position=(0, o)), s, v, st.gather.free)
                if hp % 4 == 3:
                    st.gather.free = a = act(lambda e: e.activation(a0[:, hp // 4, :], st.gather.ap, ACT.Copy), m)
                if hp % 2:
                    yield
            bank, m = rows_out(st, a0, ND, W["c_wo"], a)
            shared.free = m
            shared.ready = sync.dma(shared_load, W["a_wo"], chunks(I["a_wo"]), m)
            s = dve(lambda e: e.tensor_tensor(x_a[:], cy.ap[:], bank.ap.rearrange("p (t d) -> p t d", t=NT), ALU.add), m)
            bank.free = cy.free = s
            s = dve(lambda e: e.tensor_tensor(x_a[:], x_a[:], bcast(W["c_bo"][:]), ALU.add), s)
            x2 = layernorm(st.norm, lambda i: x_a[:, i, :], lambda i: x_a[:, i, :], 1e-5, P, NT, s)
            yield
            handed["x1 read"] = b + 1
            x2T = transposed(st, lambda t: x_a[:, t, :], xT, x2, None)
            for f in range(0, NF0, 2):
                bank = st.banks.next()
                for q in range(2):
                    for c in range(ND):
                        m = pe(lambda e: e.matmul(
                            bank.ap[:, q * T:(q + 1) * T], W["f_w1"][:, c, (f + q) * P:(f + q + 1) * P], xT[:, c, :],
                            start=c == 0, stop=c == ND - 1), x2T, bank.free, ternary_ready, w1_or_wv.ready)
                for q in range(2):
                    g = dve(lambda e: e.tensor_scalar(
                        st.aT[:, f + q, :], bank.ap[:, q * T:(q + 1) * T], W["f_b1"][:, f + q:f + q + 1], None, ALU.add), m)
                bank.free = g
                yield
            w1_or_wv.ready = sync.dma(w1_load, W["a_wv"], chunks(I["a_wv"]), m, w1_saved)
            g = act(lambda e: e.activation(st.aT[:], st.aT[:], ACT.Gelu), g)
            act(lambda e: e.preload_act_table_set(EXP_LN))
            bank, m = rows_out(st, st.aT, NF0, W["f_w2"], g)
            s = dve(lambda e: e.tensor_tensor(x_a[:], x_a[:], bank.ap.rearrange("p (t d) -> p t d", t=NT), ALU.add), m)
            bank.free = s
            s = dve(lambda e: e.tensor_tensor(x_a[:], x_a[:], bcast(W["f_b2"][:]), ALU.add), s)
            x3 = layernorm(st.norm, lambda i: x_a[:, i, :], lambda i: x_a[:, i, :], 1e-5, P, NT, s)
            yield
            x3T = transposed(st, lambda t: x_a[:, t, :], xT, x3, None)
            yield from attention(st, "causal", xT, xT, W["a_wq"], W["a_wk"], W["a_wv"], x3T, attn_loaded, w1_or_wv.ready)
            w1_free = st.last_wv
            bank, m = rows_out(st, st.aT, NE, W["a_wo"], st.out, shared.ready)
            shared.free = kblk_free[0] = m
            if b + 1 < B:
                load_cross()
                w1_or_wv.ready = sync.dma(w1_load, W["f_w1"], w1_dram, w1_free)
            s = dve(lambda e: e.tensor_tensor(st.rows, x_a[:], bank.ap.rearrange("p (t d) -> p t d", t=NT), ALU.add), m)
            bank.free = s
            s = layernorm(st.norm, lambda i: st.rows[:, i, :], lambda i: st.rows[:, i, :], 1e-3, P, NT, s)
            s = dve(lambda e: e.tensor_tensor(st.rows, st.rows, bcast(W["a_gamma"][:]), ALU.mult), s)
            s = dve(lambda e: e.tensor_tensor(st.rows, st.rows, bcast(W["a_beta"][:]), ALU.add), s)
            s = dve(lambda e: e.tensor_tensor(x_a[:], x_a[:], st.rows, ALU.add), s)
            yield
            while handed["x4 read"] < b - 1:
                yield WAIT
            x4 = between[b % 2]
            x4.ready = layernorm(st.norm, lambda i: x_a[:, i, :], lambda i: x4.ap[:, i, :], 1e-5, P, NT, s, x4.free)
            st.pairs[0].free = x4.ready
            yield
            yield
            handed["x4"] = b + 1

        def perceiver(b):
            while handed["x4"] <= b:
                yield WAIT
            st, cs, x4 = X, X.context, between[b % 2]
            bias_ready = key_mask.free = mask_done[0] = dve(lambda e: e.tensor_scalar(
                bias_row[:], key_mask.ap, 0.0, NEG, ALU.is_equal, ALU.mult), key_mask.ready)
            s = layernorm(st.norm, lambda i: x4.ap[:, i, :], lambda i: st.rows[:, i, :], 1e-5, P, NT, x4.ready, st.pairs[0].free)
            bank = st.banks.next()
            for t in range(NT):
                for c in range(ND):
                    m = pe(lambda e: e.transpose(bank.ap[:, c * T + t * P:c * T + (t + 1) * P],
                                                                      st.rows[:, t, c * P:(c + 1) * P], ident[:]), s, bank.free)
            for c in range(ND):
                lt = dve(lambda e: e.tensor_scalar(
                    st.kvT[:, c, 0:T], bank.ap[:, c * T:(c + 1) * T], W["p_ln_l_w"][:, c:c + 1],
                    W["p_ln_l_b"][:, c:c + 1], ALU.mult, ALU.add), m, perc_loaded)
            bank.free = lt
            s = layernorm(st.norm, lambda i: cs.ap[0:S2, :], lambda i: st.rows[0:S2, 0, :], 1e-5, S2, 1, cs.ready, m)
            cs.free = s
            if b + 1 < B:
                load_context_x(b + 1)
            bank = st.banks.next()
            for c in range(ND):
                m = pe(lambda e: e.transpose(bank.ap[:, c * S2:(c + 1) * S2],
                                                             st.rows[0:S2, 0, c * P:(c + 1) * P], ident[0:S2, 0:S2]), s, bank.free)
            for c in range(ND):
                kv = dve(lambda e: e.tensor_scalar(
                    st.kvT[:, c, T:KEYS], bank.ap[:, c * S2:(c + 1) * S2], W["p_ln_m_w"][:, c:c + 1],
                    W["p_ln_m_b"][:, c:c + 1], ALU.mult, ALU.add), m)
            bank.free = kv
            yield
            st.pairs[0].free = m
            yield from attention(st, "all", st.kvT, st.kvT, W["p_wq"], W["p_wk"], W["p_wv"], kv, lt)
            bank, m = rows_out(st, st.aT, NE, W["p_wo"], st.out)
            s = dve(lambda e: e.tensor_tensor(x4.ap, x4.ap, bank.ap.rearrange("p (t d) -> p t d", t=NT), ALU.add), m)
            bank.free = s
            o5 = st.pairs[1].ap[:, 0:NT * D].rearrange("p (t d) -> p t d", t=NT)
            s = layernorm(st.norm, lambda i: x4.ap[:, i, :], lambda i: o5[:, i, :], 1e-5, P, NT, s, st.pairs[1].free)
            x4.free = s
            am = dve(lambda e: e.tensor_reduce(amax5[:, b:b + 1], fl(o5), AX.X, ALU.max, apply_absolute_value=True), s)
            st.pairs[1].free = sync.dma(spill, x5_dram[b].rearrange("(t p) d -> p t d", p=P), o5, s)
            phase1_last[0], phase1_last[1] = am, st.pairs[1].free
            yield
            handed["x4 read"] = b + 1

        kblk_free = [None]

        l0_stat = sb(ph1, "l0_stat", [P, NT, 2, H])
        phase1_last = [None, None]

        load_context_a(0)
        load_context_x(0)
        def batches(part):
            for b in range(B):
                yield from part(b)

        interleave((("M", 0.0, M_US, batches(mamba)), ("A", A_START, A_US, batches(first_layer_and_causal)),
                    ("X", X_START, X_US, batches(perceiver))), weights)

        ends = [q.steps[-1] for q in (pe, act, pool)]
        for s in ends:
            s.wanted = True
        ph1.close()
        begin = (phase1_last[0], phase1_last[1], *ends)
        W_MAX, A_MAX = 7.0, 32767.0
        LPB = 32
        TB = 2 * T
        NP = B * T // TB if B > 1 else 1
        TB = B * T // NP
        big = sb(ctx, "big", [P, NF1, B * T])
        up_int = sb(ctx, "up_int", [P, NF1, B * T], I16)
        xqT = sb(ctx, "xqT", [P, ND, B * T])
        gateT, upT = sb(ctx, "gateT", [P, ND, F1]), sb(ctx, "upT", [P, ND, F1])
        downT = sb(ctx, "downT", [P, NF1, D])
        rows = [Slot(sb(ctx, f"rows{i}", [P, NT, D])) for i in range(3)]
        q_norm = norm_tiles(ctx, "q_norm", NT)
        part = sb(ctx, "part", [P, 4, 64])
        scales = sb(ctx, "scales", [P, 5, 4])
        ring = Ring([Slot(b[:]) for b in banks])

        def scale_of(which, partial, *after):
            v = scales[:, which, :]
            s = dve(lambda e: e.tensor_reduce(v[:, 0:1], partial, AX.X, ALU.max), *after)
            s = pool(lambda e: e.partition_all_reduce(v[:, 1:2], v[:, 0:1], P, RMAX), s)
            s = dve(lambda e: e.tensor_scalar(v[:, 2:3], v[:, 1:2], 1.0 / A_MAX, 1e-12, ALU.mult, ALU.max), s)
            return v[:, 2:3], v[:, 3:4], dve(lambda e: e.reciprocal(v[:, 3:4], v[:, 2:3]), s)

        sx, sx_inv, sx_ready = scale_of(0, amax5[:], *begin)

        stage = big[:].rearrange("p c t -> p (c t)") if B > 4 else sb(ctx, "stage", [P, 8 * F1 * ND])[:]
        for n, (name, dst) in enumerate((("g_up", upT), ("g_gate", gateT), ("g_down", downT))):
            nr, width = I[name].shape[0] // P, I[name].shape[1]
            size = nr * width
            w = stage[:, n * size:(n + 1) * size]
            q = stage[:, (3 + n) * size:(4 + n) * size]
            blocks = lambda a: a.rearrange("p (b k) -> p b k", k=LPB)
            nb = size // LPB
            sc = stage[:, 7 * size + n * 2 * nb:7 * size + (n * 2 + 1) * nb]
            inv = stage[:, 7 * size + (n * 2 + 1) * nb:7 * size + (n * 2 + 2) * nb]
            load = sync.dma(weight_load[5 + n], w.rearrange("p (c n) -> p c n", c=nr), I[name].rearrange("(c p) n -> p c n", p=P), *begin)
            s = dve(lambda e: e.tensor_reduce(sc, blocks(w), AX.X, ALU.max, apply_absolute_value=True), load)
            s = dve(lambda e: e.tensor_scalar(sc, sc, 1.0 / W_MAX, 1e-12, ALU.mult, ALU.max), s)
            s = dve(lambda e: e.reciprocal(inv, sc), s)
            s = dve(lambda e: e.tensor_tensor(blocks(q), blocks(w), inv.unsqueeze(2).to_broadcast([P, nb, LPB]), ALU.mult), s)
            s = dve(lambda e: e.tensor_scalar(q, q, RNE, RNE, ALU.add, ALU.subtract), s)
            s = dve(lambda e: e.tensor_scalar(q, q, W_MAX, -W_MAX - 1.0, ALU.min, ALU.max), s)
            s = dve(lambda e: e.tensor_tensor(blocks(q), blocks(q), sc.unsqueeze(2).to_broadcast([P, nb, LPB]), ALU.mult), s)
            nc_, qv = width // P, q.rearrange("p (r c) -> p r c", r=nr)
            for c in range(nc_):
                for r0 in range(0, nr, 4):
                    bank, k = ring.next(), min(4, nr - r0)
                    for r in range(k):
                        m = pe(lambda e: e.transpose(bank.ap[:, r * P:(r + 1) * P], qv[:, r0 + r, c * P:(c + 1) * P], ident[:]),
                               s, bank.free, ident_ready)
                    bank.free = ready = act(lambda e: e.activation(dst[:, c, r0 * P:(r0 + k) * P], bank.ap[:, 0:k * P], ACT.Copy), m, *begin)
            w_ready = ready
        staged = ready

        for b in range(B):
            r = rows[b % 3]
            load = sync.dma(reload_rows[b % 3], r.ap[:], x5_dram[b].rearrange("(t p) d -> p t d", p=P), r.free, *begin)
            bank = ring.next()
            for t in range(NT):
                for c in range(ND):
                    m = pe(lambda e: e.transpose(bank.ap[:, c * T + t * P:c * T + (t + 1) * P],
                                                 r.ap[:, t, c * P:(c + 1) * P], ident[:]), load, bank.free)
            r.free = m
            xs = xqT[:, :, b * T:(b + 1) * T]
            s = dve(lambda e: e.tensor_scalar(xs, bank.ap.rearrange("p (c t) -> p c t", c=ND), sx_inv, RNE,
                                              ALU.mult, ALU.add), m, sx_ready)
            bank.free = s
            s = dve(lambda e: e.tensor_scalar(xs, xs, RNE, A_MAX, ALU.subtract, ALU.min), s)
            x_ready = dve(lambda e: e.tensor_scalar(xs, xs, -A_MAX - 1.0, sx, ALU.max, ALU.mult), s)

        def piece(a, p):
            return a[:, :, p * TB:(p + 1) * TB]

        def project_up(w, which, free):
            at = 0
            done = [None] * NP
            for p in range(NP):
                for i in range(NF1):
                    bank = ring.next()
                    for c in range(ND):
                        m = pe(lambda e: e.matmul(bank.ap[:, 0:TB], w[:, c, i * P:(i + 1) * P], piece(xqT, p)[:, c, :],
                                                  start=c == 0, stop=c == ND - 1), x_ready, w_ready, bank.free)
                    bank.free = a = act(lambda e: e.activation(piece(big, p)[:, i, :], bank.ap[:, 0:TB], ACT.Copy), m, free[p], staged)
                    done[p] = dve(lambda e: e.tensor_reduce(part[:, which, at:at + 1], piece(big, p)[:, i, :], AX.X, ALU.max,
                                                            apply_absolute_value=True), a)
                    at += 1
            return done, part[:, which, 0:at]

        done, partial = project_up(upT, 0, [None] * NP)
        su, su_inv, su_ready = scale_of(1, partial, done[-1])
        free = [None] * NP
        rne = sb(ctx, "rne", [P, 1])
        rne_ready = dve(lambda e: e.memset(rne[:], RNE), *begin)
        for p in range(NP):
            s = act(lambda e: e.activation(piece(big, p), piece(big, p), ACT.Identity, bias=rne[:], scale=su_inv), su_ready, rne_ready)
            free[p] = up_ready = dve(lambda e: e.tensor_scalar(piece(up_int, p), piece(big, p), RNE, A_MAX,
                                                               ALU.subtract, ALU.min), s)

        done, partial = project_up(gateT, 1, free)
        sg, sg_inv, sg_ready = scale_of(2, partial, done[-1])
        xq_flat = xqT[:].rearrange("p c t -> p (c t)")
        n_tmp = 2
        tmp = Ring([Slot(xq_flat[:, i * NF1 * TB:(i + 1) * NF1 * TB].rearrange("p (c t) -> p c t", c=NF1)) for i in range(n_tmp)]
                   if B > 4 else
                   [Slot(sb(ctx, f"tmp{i}", [P, NF1, TB])[:]) for i in range(n_tmp)])
        for p in range(NP):
            g, sl = piece(big, p), tmp.next()
            s = act(lambda e: e.activation(g, g, ACT.Identity, bias=rne[:], scale=sg_inv), sg_ready)
            s = dve(lambda e: e.tensor_scalar(g, g, RNE, A_MAX, ALU.subtract, ALU.min), s)
            gq = dve(lambda e: e.tensor_scalar(g, g, -A_MAX - 1.0, sg, ALU.max, ALU.mult), s)
            s = act(lambda e: e.activation(sl.ap, g, ACT.Sigmoid), gq, sl.free)
            s = pool(lambda e: e.tensor_scalar(sl.ap, sl.ap, 65536.0, RNE, ALU.mult, ALU.add), s)
            s = dve(lambda e: e.tensor_scalar(sl.ap, sl.ap, RNE, 65535.0, ALU.subtract, ALU.min), s)
            fg, fs = g, sl.ap
            s = sl.free = dve(lambda e: e.scalar_tensor_tensor(fg, fs, 2.0 ** -16, fg, ALU.mult, ALU.mult), s)
            done = dve(lambda e: e.tensor_reduce(part[:, 2, p:p + 1], g, AX.XY, ALU.max, apply_absolute_value=True), s)
        s2, s2_inv, s2_ready = scale_of(3, part[:, 2, 0:NP], done)
        for p in range(NP):
            g, sl = piece(big, p), tmp.next()
            u = act(lambda e: e.activation(sl.ap, piece(up_int, p), ACT.Copy, scale=su), up_ready, su_ready, sl.free)
            s = act(lambda e: e.activation(g, g, ACT.Identity, bias=rne[:], scale=s2_inv), s2_ready)
            s = dve(lambda e: e.tensor_scalar(g, g, RNE, A_MAX, ALU.subtract, ALU.min), s)
            s = dve(lambda e: e.tensor_scalar(g, g, -A_MAX - 1.0, s2, ALU.max, ALU.mult), s)
            fg, fs = g, sl.ap
            s = sl.free = dve(lambda e: e.tensor_tensor(fg, fg, fs, ALU.mult), s, u)
            done = dve(lambda e: e.tensor_reduce(part[:, 3, p:p + 1], g, AX.XY, ALU.max, apply_absolute_value=True), s)
        so, so_inv, so_ready = scale_of(4, part[:, 3, 0:NP], done)
        act(lambda e: e.preload_act_table_set(EXP_LN))
        for p in range(NP):
            g = piece(big, p)
            s = act(lambda e: e.activation(g, g, ACT.Identity, bias=rne[:], scale=so_inv), so_ready)
            s = dve(lambda e: e.tensor_scalar(g, g, RNE, A_MAX, ALU.subtract, ALU.min), s)
            o_ready = dve(lambda e: e.tensor_scalar(g, g, -A_MAX - 1.0, so, ALU.max, ALU.mult), s)
            for b in range(p * TB // T, (p + 1) * TB // T):
                r = rows[b % 3]
                load = sync.dma(reload_rows[b % 3], r.ap[:], x5_dram[b].rearrange("(t p) d -> p t d", p=P), r.free)
                bank = ring.next()
                for t in range(NT):
                    for i in range(NF1):
                        t0 = b * T + t * P
                        m = pe(lambda e: e.matmul(bank.ap[:, t * D:(t + 1) * D], big[:, i, t0:t0 + P], downT[:, i, :],
                                                  start=i == 0, stop=i == NF1 - 1), o_ready, bank.free)
                fr = r.ap[:].rearrange("p t d -> p (t d)")
                bank.free = s = dve(lambda e: e.tensor_tensor(fr, fr, bank.ap, ALU.add), m, load)
                s = layernorm(q_norm, lambda i: r.ap[:, i, :], lambda i: r.ap[:, i, :], 1e-5, P, NT, s)
                r.free = sync.dma(final_rows[b % 3], out[b].rearrange("(t p) d -> p t d", p=P), r.ap[:], s)
        block = ctx.enter_context(nc.Block())
        for q in (pe, dve, act, pool, sync):
            q.number()

        @block.tensor
        def _(e):
            pe.emit(e)

        @block.vector
        def _(e):
            dve.emit(e)

        @block.scalar
        def _(e):
            e.preload_act_table_set(EXP_LN)
            act.emit(e)

        @block.gpsimd
        def _(e):
            pool.emit(e)

        @block.sync
        def _(e):
            sync.emit(e)
            for c in (spill, *final_rows):
                if c.count:
                    e.wait_ge(c.sem, c.count)


def laid_out(inputs):
    import numpy as np

    a = {k: np.asarray(v) for k, v in inputs.items()}
    m = {k: a["L0_attn_" + k] for k in ("W_in", "W_x", "W_dt", "W_out", "conv_w", "conv_b", "b_dt", "A_log", "Dp", "ln_g", "ln_b")}
    r = {
        "x": a["x"], "ctx": a["ctx_1024"], "mask_q": a["mask_Bx1xSxS2_ik1"], "mask_k": a["mask_BxS2_ik0"],
        "m_w_in": m["W_in"].T, "m_w_x": m["W_x"].T, "m_w_dt": m["W_dt"].T, "m_w_out": m["W_out"].T,
        "m_conv_w": m["conv_w"][:, 0, :], "m_conv_b": m["conv_b"], "m_b_dt": m["b_dt"], "m_a_log": m["A_log"],
        "m_dp": m["Dp"], "m_ln_g": m["ln_g"], "m_ln_b": m["ln_b"],
        "f_w1": a["L0_ffn_W1"].T, "f_b1": a["L0_ffn_b1"], "f_w2": a["L0_ffn_W2"].T, "f_b2": a["L0_ffn_b2"],
        "a_wo": a["L1_attn_Wo"], "a_gamma": a["L1_attn_gamma"], "a_beta": a["L1_attn_beta"],
        "g_gate": a["L1_ffn_w_gate"], "g_up": a["L1_ffn_w_up"], "g_down": a["L1_ffn_w_down"],
    }
    for w in ("q", "k", "v", "o"):
        r["c_w" + w] = a["L0_xattn_w" + w].T
        r["c_b" + w] = a["L0_xattn_b" + w]
        r["p_w" + w] = a["L1_xattn_W" + w]
    for w in ("q", "k", "v"):
        t = a["L1_attn_W" + w].transpose(1, 0, 2)
        r["a_w" + w] = t.reshape(t.shape[0], -1)
    for n in ("ln_m_w", "ln_m_b", "ln_l_w", "ln_l_b"):
        r["p_" + n] = a["L1_xattn_" + n]
    for n in ("m_conv_b", "m_b_dt", "m_dp", "m_ln_g", "m_ln_b", "f_b1", "c_bq", "c_bk",
              "p_ln_m_w", "p_ln_m_b", "p_ln_l_w", "p_ln_l_b"):
        r[n] = r[n].reshape(-1, P).T
    return {k: np.ascontiguousarray(v) for k, v in r.items()}


def kernel(**inputs):
    import concourse.bacc as bacc
    from concourse.bass_utils import run_bass_kernel_spmd

    arrays = laid_out(inputs)
    nc = bacc.Bacc("TRN2", target_bir_lowering=False, num_devices=1)
    ins = {n: nc.dram_tensor(n, a.shape, mybir.dt.from_np(a.dtype), kind="ExternalInput").ap()
           for n, a in arrays.items()}
    out = nc.dram_tensor("out", arrays["x"].shape, F32, kind="ExternalOutput").ap()
    decoder_kernel(nc, ins, out)
    return run_bass_kernel_spmd(nc, [arrays], core_ids=[0]).results[0]["out"]
```

```python
from contextlib import ExitStack

import concourse.bass as bass
from concourse import mybir

F32 = mybir.dt.float32
BF16 = mybir.dt.bfloat16
I32 = mybir.dt.int32
I16 = mybir.dt.int16
U16 = mybir.dt.uint16
ALU = mybir.AluOpType
ACT = mybir.ActivationFunctionType
AX = mybir.AxisListType
RMAX = bass.bass_isa.ReduceOp.max
RADD = bass.bass_isa.ReduceOp.add

P = 128
BANK = 512
NEG = -1e30
RNE = 12582912.0
EXP_LN = "natural_log_exp_and_others"




def columns(ap):
    n = 1
    for size in ap.shape[1:]:
        n *= size
    return n


class Later:

    def __init__(self, engine):
        self.engine = engine

    def matmul(self, out, lhs, *a, **k):
        passes = 1 if lhs.dtype == BF16 else 4
        if out.shape[0] <= P // 2:
            passes /= 2
        return columns(out) * passes, lambda: self.engine.matmul(out, lhs, *a, **k)

    def transpose(self, out, *a, **k):
        return columns(out), lambda: self.engine.transpose(out, *a, **k)

    def activation(self, out, *a, **k):
        return columns(out), lambda: self.engine.activation(out, *a, **k)

    def memset(self, out, *a, **k):
        return columns(out), lambda: self.engine.memset(out, *a, **k)

    def tensor_copy(self, out, *a, **k):
        return columns(out), lambda: self.engine.tensor_copy(out, *a, **k)

    def tensor_tensor(self, out, *a, **k):
        return columns(out), lambda: self.engine.tensor_tensor(out, *a, **k)

    def tensor_scalar(self, out, *a, **k):
        return columns(out), lambda: self.engine.tensor_scalar(out, *a, **k)

    def scalar_tensor_tensor(self, out, *a, **k):
        return columns(out), lambda: self.engine.scalar_tensor_tensor(out, *a, **k)

    def tensor_tensor_scan(self, out, *a, **k):
        return columns(out), lambda: self.engine.tensor_tensor_scan(out, *a, **k)

    def tensor_reduce(self, out, in_, *a, **k):
        return columns(in_), lambda: self.engine.tensor_reduce(out, in_, *a, **k)

    def reciprocal(self, out, *a, **k):
        return columns(out), lambda: self.engine.reciprocal(out, *a, **k)

    def bn_stats(self, out, in_, *a, **k):
        return columns(in_), lambda: self.engine.bn_stats(out, in_, *a, **k)

    def bn_aggr(self, out, in_, *a, **k):
        return columns(in_), lambda: self.engine.bn_aggr(out, in_, *a, **k)

    def affine_select(self, out, *a, **k):
        return columns(out), lambda: self.engine.affine_select(out, *a, **k)

    def partition_all_reduce(self, out, *a, **k):
        return columns(out), lambda: self.engine.partition_all_reduce(out, *a, **k)

    def copy_predicated(self, out, *a, **k):
        return columns(out), lambda: self.engine.copy_predicated(out, *a, **k)

    def preload_act_table_set(self, *a, **k):
        return 1400, lambda: self.engine.preload_act_table_set(*a, **k)

    def dma_start(self, out, in_):
        return columns(out), lambda: self.engine.dma_start(out, in_)


class Step:

    def __init__(self, queue, issue, after, cost):
        self.queue, self.issue, self.after, self.cost, self.end = queue, issue, after, cost, 0.0
        self.glued = False
        self.sem, self.value, self.amount, self.wanted = None, 0, 1, False


DMA_BYTES_PER_US = 180e3
HOP = 0.15


class Queue:

    made = None

    def __init__(self, engine, sem, fixed, column):
        self.later, self.sem, self.steps = Later(engine), sem, []
        self.fixed, self.column, self.clock = fixed, column, 0.0

    def __call__(self, instruction, *after):
        length, issue = instruction(self.later)
        step = Step(self, issue, [a for a in after if a is not None], self.fixed + self.column * length)
        for a in step.after:
            a.wanted = True
        if Queue.made is None:
            self.add(step)
        else:
            Queue.made.append(step)
        return step

    def add(self, step):
        start = max([self.clock] + [a.end + HOP for a in step.after])
        self.clock = step.end = start + step.cost
        self.steps.append(step)

    def dma(self, counter, out, in_, *after):
        step = self(lambda e: e.dma_start(out, in_), *after)
        step.cost = out.shape[0] * columns(out) * 4 / DMA_BYTES_PER_US
        counter.count += 16
        step.sem, step.value, step.amount, step.wanted = counter.sem, counter.count, 16, True
        return step

    def number(self):
        count = 0
        for s in self.steps:
            if s.wanted and s.sem is None:
                count += 1
                s.sem, s.value = self.sem, count

    def emit(self, engine):
        reached = {}
        for s in self.steps:
            for a in s.after:
                if reached.get(id(a.sem), 0) < a.value:
                    engine.wait_ge(a.sem, a.value)
                    reached[id(a.sem)] = a.value
            made = s.issue()
            if s.wanted:
                made.then_inc(s.sem, s.amount)


class Counter:

    def __init__(self, sem):
        self.sem, self.count = sem, 0


class Slot:

    def __init__(self, ap, free=None):
        self.ap, self.free = ap, free


class Ring:

    def __init__(self, slots):
        self.slots, self.at = slots, -1

    def next(self):
        self.at = (self.at + 1) % len(self.slots)
        return self.slots[self.at]


WAIT, END = "wait", "end"


class Lane:

    def __init__(self, name, start, length, generator):
        self.name, self.start, self.at, self.length, self.generator = name, start, start, length, generator
        self.steps, self.clocks, self.alone = [], {}, {}

    def refill(self):
        more = None
        while not self.steps and more is not WAIT:
            Queue.made = self.steps
            more = next(self.generator, END)
            Queue.made = None
            if more is END and not self.steps:
                return False
        return True

    def waiting(self):
        step = self.steps[0]
        return max([0.0] + [a.end + HOP - step.queue.clock for a in step.after])

    def advance(self):
        glued = True
        while glued:
            step = self.steps.pop(0)
            step.queue.add(step)
            glued = step.glued
            t = max([self.clocks.get(step.queue, 0.0)] + [self.alone[a] + HOP for a in step.after if a in self.alone])
            self.alone[step] = self.clocks[step.queue] = t + step.cost
            self.at = max(self.at, self.start + self.alone[step] / self.length)


def interleave(lanes, weights):
    lanes = list(lanes)
    while True:
        lanes = [lane for lane in lanes if lane.refill()]
        ready = [lane for lane in lanes if lane.steps]
        assert ready or not lanes, "each strand waits for another"
        if not ready:
            return
        behind = min(lane.at for lane in ready)
        min(ready, key=lambda lane: lane.waiting() * weights[lane.steps[0].queue] + AHEAD * (lane.at - behind)).advance()


AHEAD = 11.0
M_US, A_US, X_US = 157.0, 151.0, 114.0
A_START, X_START = 0.87, 2.5
WP, WD, WA, WG = 1.14, 1.89, 0.68, 0.0

def decoder_kernel(nc, I, out):
    B, T, D = I["x"].shape
    S2 = I["ctx"].shape[1]
    NT, ND = T // P, D // P
    DI = I["m_w_out"].shape[0]
    NI = DI // P
    NS = I["m_a_log"].shape[1]
    DR = I["m_w_dt"].shape[0]
    KC = I["m_conv_w"].shape[1]
    H = 16
    HD0 = D // H
    F0 = I["f_w1"].shape[1]
    NF0 = F0 // P
    E = I["a_wq"].shape[1]
    HD = E // H
    NE = E // P
    F1 = I["g_gate"].shape[0]
    NF1 = F1 // P
    KEYS = T + S2
    NK = 3
    assert T == 2 * P and D == 2 * P and HD == 64 and NS == 16 and KEYS < NK * P

    ctx = ExitStack()
    with ctx:
        def counter(name):
            return Counter(ctx.enter_context(nc.semaphore(name)))

        pe, dve, act, pool, sync = (
            Queue(engine, ctx.enter_context(nc.semaphore(n)), fixed, column)
                for engine, n, fixed, column in (
                    (nc.tensor, "pe_done", 0.035, 0.42e-3), (nc.vector, "dve_done", 0.07, 1.05e-3),
                    (nc.scalar, "act_done", 0.2, 0.7e-3), (nc.gpsimd, "pool_done", 0.15, 2.1e-3),
                    (nc.sync, "sync_done", 0.1, 0.0)))
        weights = {pe: WP, dve: WD, act: WA, pool: WG, sync: 0.0}
        weight_load = [counter(f"weight_load{i}") for i in range(8)]
        x_load, ctx_a_load, mask_a_load, ctx_x_load, mask_x_load, w_in_load, shared_load, spill = (counter(n) for n in (
            "x_load", "ctx_a_load", "mask_a_load", "ctx_x_load", "mask_x_load", "w_in_load", "shared_load", "spill"))
        w1_load, w1_store = counter("w1_load"), counter("w1_store")
        reload_rows, final_rows = ([counter(f"{n}{i}") for i in range(3)] for n in ("reload_rows", "final_rows"))

        def sb(scope, name, shape, dt=F32):
            return scope.enter_context(nc.sbuf_tensor(name, shape, dt))

        banks = [ctx.enter_context(nc.psum_tensor(f"bank{i}", [P, BANK], F32)) for i in range(8)]
        x5_dram = nc.dram_tensor("x5_spill", (B, T, D), F32)
        x5_dram = x5_dram.ap() if hasattr(x5_dram, "ap") else x5_dram

        w1_dram = nc.dram_tensor("w1_ternary", (P, ND, F0), F32)
        w1_dram = w1_dram.ap() if hasattr(w1_dram, "ap") else w1_dram

        ident = sb(ctx, "ident", [P, P])
        zeroed = dve(lambda e: e.memset(ident[:], 0.0))
        ident_ready = pool(lambda e: e.affine_select(
            out=ident[:], in_=ident[:], compare_op=ALU.not_equal, fill=1.0, base=0,
            pattern=[[-1, P]], channel_multiplier=1), zeroed)
        rne = sb(ctx, "rne", [P, 1])
        rne_ready = dve(lambda e: e.memset(rne[:], RNE))
        amax5 = sb(ctx, "amax5", [P, B])

        def layernorm(scope_tiles, src, dst, eps, rows, tiles, *after):
            st, mv, r, t = scope_tiles
            n = tiles
            for i in range(n):
                s = dve(lambda e: e.bn_stats(st[0:rows, i, :], src(i)), *after)
            for i in range(n):
                s = dve(lambda e: e.bn_aggr(mv[0:rows, i, :], st[0:rows, i, :]), s)
            v = mv[0:rows, 0:n, 1]
            s0 = dve(lambda e: e.tensor_scalar(t[0:rows, 3, 0:n], v, eps, None, ALU.add), s)
            s1 = act(lambda e: e.activation(t[0:rows, 0, 0:n], t[0:rows, 3, 0:n], ACT.Ln), s0)
            s2 = act(lambda e: e.activation(r[0:rows, 0:n], t[0:rows, 0, 0:n], ACT.Exp, scale=-0.5), s1)
            s3 = dve(lambda e: e.tensor_tensor(t[0:rows, 1, 0:n], r[0:rows, 0:n], r[0:rows, 0:n], ALU.mult), s2)
            s4 = dve(lambda e: e.tensor_tensor(t[0:rows, 2, 0:n], t[0:rows, 1, 0:n], t[0:rows, 3, 0:n], ALU.mult), s3)
            s5 = dve(lambda e: e.tensor_scalar(t[0:rows, 2, 0:n], t[0:rows, 2, 0:n], -0.5, 1.5, ALU.mult, ALU.add), s4)
            s6 = dve(lambda e: e.tensor_tensor(r[0:rows, 0:n], r[0:rows, 0:n], t[0:rows, 2, 0:n], ALU.mult), s5)
            for i in range(n):
                s = dve(lambda e: e.tensor_scalar(dst(i), src(i), mv[0:rows, i, 0:1], r[0:rows, i:i + 1],
                                                       ALU.subtract, ALU.mult), s6)
            return s

        def norm_tiles(scope, name, n):
            return (sb(scope, name + "_st", [P, n, 6]), sb(scope, name + "_mv", [P, n, 2]),
                    sb(scope, name + "_r", [P, n]), sb(scope, name + "_t", [P, 4, n]))

        ph1 = ctx.enter_context(ExitStack())
        W = {}

        def weight(name, shape, src, load=0):
            W[name] = sb(ph1, name + "_sb", shape)
            return sync.dma(weight_load[load], W[name][:], src)

        def chunks(ap):
            return ap.rearrange("(c p) n -> p c n", p=P)

        x_in = Slot(sb(ph1, "x_in", [P, NT, D]))
        states = sb(ph1, "states", [P, NI * 2 * T])
        state = [Slot(states[:, i * 2 * T:(i + 1) * 2 * T].rearrange("p (k t) -> p k t", k=2))
                 for i in range(NI)]
        w_in = Slot(states[:].rearrange("p (c n) -> p c n", c=ND))

        def load_x(b):
            x_in.ready = sync.dma(x_load, x_in.ap[:], I["x"][b].rearrange("(t p) d -> p t d", p=P), x_in.free)
            w_in.ready = sync.dma(w_in_load, w_in.ap, chunks(I["m_w_in"]), *(sl.free for sl in state))

        load_x(0)
        weight("m_w_x", [P, NI, DR + 2 * NS], chunks(I["m_w_x"]))
        weight("m_w_dt", [DR, DI], I["m_w_dt"])
        weight("m_w_out", [P, NI, D], chunks(I["m_w_out"]))
        weight("m_conv_w", [P, NI, KC], chunks(I["m_conv_w"]))
        weight("m_a_log", [P, NI, NS], chunks(I["m_a_log"]))
        for n in ("m_conv_b", "m_b_dt", "m_dp"):
            weight(n, [P, NI], I[n])
        for n in ("m_ln_g", "m_ln_b"):
            mamba_loaded = weight(n, [P, ND], I[n])
        shared = Slot(sb(ph1, "cross_or_a_wo", [P, NE, D]))
        cross = ("c_wq", "c_wk", "c_wv", "c_wo")
        for i, n in enumerate(cross):
            W[n] = shared.ap[:, i * ND:(i + 1) * ND, :]
        W["a_wo"] = shared.ap[:]
        w1_or_wv = Slot(sb(ph1, "w1_or_a_wv", [P, ND, F0]))
        W["f_w1"] = W["a_wv"] = w1_or_wv.ap[:]
        assert F0 == E and len(cross) * ND == NE

        def load_cross():
            for n in cross:
                shared.ready = sync.dma(shared_load, W[n], chunks(I[n]), shared.free)

        load_cross()
        for n in ("c_bq", "c_bk"):
            weight(n, [P, ND], I[n], 1)
        for n in ("c_bv", "c_bo"):
            cross_loaded = weight(n, [P, D], I[n].partition_broadcast(P), 1)
        w1_or_wv.ready = sync.dma(w1_load, W["f_w1"], chunks(I["f_w1"]))
        weight("f_b1", [P, NF0], I["f_b1"], 2)
        weight("f_b2", [P, D], I["f_b2"].partition_broadcast(P), 2)
        ffn_loaded = weight("f_w2", [P, NF0, D], chunks(I["f_w2"]), 2)
        for n in ("a_wq", "a_wk"):
            weight(n, [P, ND, E], chunks(I[n]), 3)
        for n in ("a_gamma", "a_beta"):
            attn_loaded = weight(n, [P, D], I[n].partition_broadcast(P), 3)
        for n in ("p_wq", "p_wk", "p_wv"):
            weight(n, [P, ND, E], chunks(I[n]), 4)
        weight("p_wo", [P, NE, D], chunks(I["p_wo"]), 4)
        for n in ("p_ln_m_w", "p_ln_m_b", "p_ln_l_w", "p_ln_l_b"):
            perc_loaded = weight(n, [P, ND], I[n], 4)

        a_neg = sb(ph1, "a_neg", [P, NI, NS])
        w_bc = sb(ph1, "w_bc", [P, NI, 3, 2 * NS])
        sel = sb(ph1, "sel", [P, P], BF16)
        ident_bf = sb(ph1, "ident_bf", [P, P], BF16)
        causal = sb(ph1, "causal", [P, P], BF16)
        head_of = sb(ph1, "head_of", [P, P // HD0])
        ones_bf = sb(ph1, "ones_bf", [1, P], BF16)

        a_exp = act(lambda e: e.activation(a_neg[:], W["m_a_log"][:], ACT.Exp), mamba_loaded)
        a_ready = dve(lambda e: e.tensor_scalar(a_neg[:], a_neg[:], -1.0, None, ALU.mult), a_exp)
        for r in range(3):
            bc_w_ready = dve(lambda e: e.tensor_copy(w_bc[:, :, r, :], W["m_w_x"][:, :, DR:DR + 2 * NS]), mamba_loaded)
        ident_bf_ready = dve(lambda e: e.tensor_copy(ident_bf[:], ident[:]), ident_ready)
        s = dve(lambda e: e.tensor_tensor(sel[:, 0:2 * NS], ident[:, 0:2 * NS], ident[:, 2 * NS:4 * NS], ALU.add), ident_ready)
        sel_ready = dve(lambda e: e.tensor_tensor(sel[:, 0:2 * NS], sel[:, 0:2 * NS], ident[:, 4 * NS:6 * NS], ALU.add), s)
        s = dve(lambda e: e.memset(causal[:], 0.0))
        causal_ready = pool(lambda e: e.affine_select(
            out=causal[:], in_=causal[:], compare_op=ALU.is_ge, fill=NEG, base=0,
            pattern=[[-1, P]], channel_multiplier=1), s)
        heads_ready = dve(lambda e: e.tensor_reduce(
            head_of[:], ident[:].rearrange("p (h d) -> p h d", d=HD0), AX.X, ALU.add), ident_ready)
        ones_ready = dve(lambda e: e.memset(ones_bf[:], 1.0))

        xi_pad = sb(ph1, "xi_pad", [P, NI, KC - 1 + T])
        zT = sb(ph1, "zT", [P, NI, T])
        uT = sb(ph1, "uT", [P, NI, T])
        m_hT = uT[:, 0:ND, :]
        m_rows = uT[:, ND:NI, :]
        m_tmp = xi_pad[:, :, KC - 1:]
        dtT = sb(ph1, "dtT", [P, NI, T])
        dt_low = sb(ph1, "dt_low", [DR, T])
        bc_split = sb(ph1, "bc_split", [6 * NS, T], BF16)
        decay = [Slot(sb(ph1, f"decay{i}", [P, 2, T])) for i in range(3)]
        series = states[:, 0:NI * T].rearrange("p (c t) -> p c t", c=NI)
        small = states[:, NI * T:].rearrange("p (c t) -> p c t", c=NI).bitcast(I32)
        y_sum = sb(ph1, "y_sum", [P, NI, T])
        m_norm = norm_tiles(ph1, "m_norm", NT)
        m_banks = Ring([Slot(b[:]) for b in banks[0:2]])
        carry = Slot(sb(ph1, "x1", [P, NT, D]))

        s = dve(lambda e: e.memset(xi_pad[:, :, 0:KC - 1], 0.0))
        for i in range(len(decay)):
            pads_ready = dve(lambda e: e.memset(decay[i].ap[:, :, 0:1], 0.0))

        PW = NK * P

        class Strand:

            def __init__(self, name, keys, first_bank, attn_columns):
                self.kvT = sb(ph1, name + "_kvT", [P, ND, KEYS])
                self.aT = sb(ph1, name + "_aT", [P, NE, T])
                self.v0 = T + keys
                pad = (keys + P - 1) // P * P
                self.pairs = [Slot(sb(ph1, f"{name}_pair{i}", [P, self.v0 + pad])) for i in range(3)]
                self.rows = self.pairs[0].ap[:, 0:NT * D].rearrange("p (t d) -> p t d", t=NT)
                self.attn = sb(ph1, name + "_attn", [P, attn_columns])
                turned = (attn_columns - 4 * PW) // 3
                self.probs = [Slot(self.attn[:, i * PW:(i + 1) * PW]) for i in range(4)]
                self.probsT = [Slot(self.attn[:, 4 * PW + i * turned:4 * PW + (i + 1) * turned]) for i in range(3)]
                self.stat = sb(ph1, name + "_stat", [P, 8, 6])
                self.stat_free = [None] * 8
                self.norm = norm_tiles(ph1, name + "_norm", NT)
                slots = [Slot(b[:]) for b in banks[first_bank:first_bank + 3]]
                self.banks = Ring(slots)
                self.gather, self.other_banks = slots[2], Ring(slots[0:2])
                self.context = Slot(sb(ph1, name + "_context", [P, D]))

        A = Strand("a", T, 2, 4 * PW + 3 * PW)
        X = Strand("x", KEYS, 5, 4 * PW + 3 * NK * T)
        mask_in = Slot(sb(ph1, "mask_in", [P, NT, S2], I32)[:])
        key_mask = Slot(sb(ph1, "key_mask", [1, S2], I32)[:])
        x_a = sb(ph1, "x_a", [P, NT, D])
        between = [Slot(sb(ph1, f"x4_{i}", [P, NT, D])[:]) for i in range(2)]
        bias_row = sb(ph1, "bias_row", [1, S2], BF16)
        bound = sb(ph1, "bound", [P, NT, S2])

        for sl in X.probs:
            sl.free = dve(lambda e: e.memset(sl.ap[:, KEYS:PW], 0.0))
        for sl in X.pairs:
            sl.free = dve(lambda e: e.memset(sl.ap[:, X.v0 + T:], 0.0))
        pads2_ready = sl.free
        kblk = A.aT[:, ND:, :].rearrange("p c t -> p (c t)")[:, 0:ND * P // HD0 * S2].rearrange("p (c n) -> p c n", c=ND)
        vpad = sb(ph1, "vpad", [S2, H, 2 * HD0])
        vpad_ready = dve(lambda e: e.memset(vpad[:], 0.0))
        last_turn = {}
        handed = {"x1": 0, "x1 read": 0, "x4": 0, "x4 read": 0}

        w1_saved, w2_ready = [None], [None]

        def ternary_weights():
            tern = A.attn[:, 0:F0 * ND]
            tsum = A.stat[:, 0, :]
            tern_free = None
            for n in ("f_w1", "f_w2"):
                w = (W[n] if n == "f_w1" else W[n][:]).rearrange("p c n -> p (c n)")
                cnt = float(F0 * D)
                t = tern
                s = dve(lambda e: e.tensor_reduce(tsum[:, 0:1], w, AX.X, ALU.add, apply_absolute_value=True),
                        w1_or_wv.ready, ffn_loaded, tern_free)
                s = pool(lambda e: e.partition_all_reduce(tsum[:, 1:2], tsum[:, 0:1], P, RADD), s)
                s = dve(lambda e: e.tensor_scalar(tsum[:, 2:3], tsum[:, 1:2], 1.0 / cnt, 1e-8, ALU.mult, ALU.max), s)
                s = dve(lambda e: e.reciprocal(tsum[:, 3:4], tsum[:, 2:3]), s)
                s = act(lambda e: e.activation(t, w, ACT.Identity, bias=rne[:], scale=tsum[:, 3:4]), s, rne_ready)
                s = dve(lambda e: e.tensor_scalar(t, t, RNE, 1.0, ALU.subtract, ALU.min), s)
                s = dve(lambda e: e.tensor_scalar(t, t, -1.0, None, ALU.max), s)
                s = pool(lambda e: e.tensor_tensor(t, t, w, ALU.subtract), s)
                s = tern_free = pool(lambda e: e.tensor_tensor(w, w, t, ALU.add), s)
                if n == "f_w1":
                    w1_or_wv.ready = s
                    w1_saved[0] = sync.dma(w1_store, w1_dram, W[n], s)
            w2_ready[0] = s
            yield

        def mamba(b):
            xs = x_in
            load, wi = xs.ready, w_in.ready
            m_work = m_banks.next()
            s = layernorm(m_norm, lambda i: xs.ap[:, i, :], lambda i: m_rows[:, i, :], 1e-6, P, NT, load)
            yield
            for t in range(NT):
                for c in range(ND):
                    m = pe(lambda e: e.transpose(m_work.ap[:, c * T + t * P:c * T + (t + 1) * P],
                                                           m_rows[:, t, c * P:(c + 1) * P], ident[:]),
                           s, m_work.free, ident_ready)
            for c in range(ND):
                h = dve(lambda e: e.tensor_scalar(m_hT[:, c, :], m_work.ap[:, c * T:(c + 1) * T],
                                                       W["m_ln_g"][:, c:c + 1], W["m_ln_b"][:, c:c + 1],
                                                       ALU.mult, ALU.add), m, mamba_loaded)
            m_work.free = h
            yield
            for j in range(NI):
                m_work = m_banks.next()
                for q in range(2):
                    for c in range(ND):
                        m = pe(lambda e: e.matmul(
                            m_work.ap[:, q * T:(q + 1) * T],
                            w_in.ap[:, c, (2 * j + q) * P:(2 * j + q + 1) * P], m_hT[:, c, :],
                            start=c == 0, stop=c == ND - 1), h, wi, m_work.free)
                dst = xi_pad[:, 2 * j:2 * j + 2, KC - 1:] if j < NI // 2 else zT[:, 2 * j - NI:2 * j - NI + 2, :]
                m_work.free = xi = act(lambda e: e.activation(
                    dst, m_work.ap.rearrange("p (q t) -> p q t", q=2), ACT.Copy), m)
                yield
            for c in range(NI):
                cv = dve(lambda e: e.tensor_scalar(uT[:, c, :], xi_pad[:, c, 0:T], W["m_conv_w"][:, c, 0:1],
                                                        W["m_conv_b"][:, c:c + 1], ALU.mult, ALU.add), xi)
                for k in range(1, KC):
                    cv = dve(lambda e: e.scalar_tensor_tensor(
                        uT[:, c, :], xi_pad[:, c, k:k + T], W["m_conv_w"][:, c, k:k + 1], uT[:, c, :],
                        ALU.mult, ALU.add), cv)
                if c % 2:
                    yield
            zs = act(lambda e: e.activation(zT[:], zT[:], ACT.Silu), xi, cv)
            us = act(lambda e: e.activation(uT[:], uT[:], ACT.Silu), cv)
            act(lambda e: e.preload_act_table_set(EXP_LN))
            zs.glued = us.glued = True
            yield
            w_in_free = m
            m_work = m_banks.next()
            for c in range(NI):
                pe(lambda e: e.matmul(m_work.ap[0:DR, 0:T], W["m_w_x"][:, c, 0:DR], uT[:, c, :],
                                           start=c == 0, stop=c == NI - 1), us, m_work.free)
            for c in range(NI):
                m = pe(lambda e: e.matmul(m_work.ap[0:6 * NS, T:2 * T],
                                               w_bc[:, c, :, :].rearrange("p r n -> p (r n)"), uT[:, c, :],
                                               start=c == 0, stop=c == NI - 1), bc_w_ready)
            low = dve(lambda e: e.tensor_copy(dt_low[:], m_work.ap[0:DR, 0:T]), m)
            bcp = m_work.ap[0:6 * NS, T:2 * T]
            r = m_tmp[0:6 * NS, 1, :]
            hi = m_tmp[0:6 * NS, 0, :].bitcast(BF16)[:, 0:T]
            s = dve(lambda e: e.tensor_copy(hi, bcp), m)
            s1 = dve(lambda e: e.tensor_copy(bc_split[0:2 * NS, :], hi[0:2 * NS]), s, last_turn.get("bc"))
            s2 = dve(lambda e: e.tensor_tensor(r, bcp, hi, ALU.subtract), s)
            m_work.free = s2
            s3 = dve(lambda e: e.tensor_copy(hi, r), s2, s1)
            s4 = dve(lambda e: e.tensor_copy(bc_split[2 * NS:4 * NS, :], hi[2 * NS:4 * NS]), s3)
            s5 = dve(lambda e: e.tensor_tensor(r, r, hi, ALU.subtract), s3)
            bc_ready = dve(lambda e: e.tensor_copy(bc_split[4 * NS:6 * NS, :], r[4 * NS:6 * NS]), s5, s4)
            yield
            for q in range(2):
                m_work = m_banks.next()
                for c in range(2):
                    m = pe(lambda e: e.matmul(
                        m_work.ap[:, c * T:(c + 1) * T], W["m_w_dt"][:, (2 * q + c) * P:(2 * q + c + 1) * P],
                        dt_low[:], start=True, stop=True), low, m_work.free)
                for c in range(2):
                    v = dve(lambda e: e.tensor_scalar(
                        dtT[:, 2 * q + c, :], m_work.ap[:, c * T:(c + 1) * T],
                        W["m_b_dt"][:, 2 * q + c:2 * q + c + 1], None, ALU.add), m)
                m_work.free = v
            s = act(lambda e: e.activation(m_tmp, dtT[:], ACT.Abs), v, bc_ready)
            ex = act(lambda e: e.activation(m_tmp, m_tmp, ACT.Exp, scale=-1.0), s)
            one_plus = y_sum
            w1 = act(lambda e: e.activation(one_plus[:], m_tmp, ACT.Identity, bias=1.0), ex, last_turn.get("y"))
            is_small = dve(lambda e: e.tensor_scalar(small, m_tmp, 2.0 ** -8, None, ALU.is_lt), w_in_free, ex)
            s = pool(lambda e: e.tensor_scalar(series, m_tmp, 1.0 / 3.0, -0.5, ALU.mult, ALU.add), w_in_free, ex)
            s = pool(lambda e: e.tensor_tensor(series, series, m_tmp, ALU.mult), s)
            s = pool(lambda e: e.tensor_tensor(series, series, m_tmp, ALU.mult), s)
            sr = pool(lambda e: e.tensor_tensor(series, series, m_tmp, ALU.add), s)
            yield
            error = dve(lambda e: e.scalar_tensor_tensor(m_tmp, one_plus[:], -1.0, m_tmp, ALU.add, ALU.subtract), w1, is_small, sr)
            ln = act(lambda e: e.activation(one_plus[:], one_plus[:], ACT.Ln), error)
            s = dve(lambda e: e.tensor_tensor(one_plus[:], one_plus[:], m_tmp, ALU.subtract), ln)
            s = dve(lambda e: e.copy_predicated(one_plus[:], small, series), s)
            dt = dve(lambda e: e.scalar_tensor_tensor(dtT[:], dtT[:], 0.0, one_plus[:], ALU.max, ALU.add), s)
            for c in range(NI):
                y0 = pool(lambda e: e.tensor_scalar(y_sum[:, c, :], uT[:, c, :], W["m_dp"][:, c:c + 1], 1.0, ALU.mult, ALU.mult), dt)
            dtu = pool(lambda e: e.tensor_tensor(uT[:], dtT[:], uT[:], ALU.mult), y0)
            yield
            summed = [y0] * NI
            for n in range(0, NS, 2):
                bank_b, bank_c = m_banks.next(), m_banks.next()
                for k in range(2):
                    mb = pe(lambda e: e.matmul(
                        bank_b.ap[:, k * T:(k + 1) * T], sel[0:6 * NS, n + k:n + k + 1].to_broadcast([6 * NS, P]),
                        bc_split[:], start=True, stop=True), bc_ready, sel_ready, bank_b.free)
                for k in range(2):
                    mc = pe(lambda e: e.matmul(
                        bank_c.ap[:, k * T:(k + 1) * T],
                        sel[0:6 * NS, NS + n + k:NS + n + k + 1].to_broadcast([6 * NS, P]),
                        bc_split[:], start=True, stop=True), bank_c.free)
                sc = [None] * NI

                def decays(c, n=n):
                    d = decay[(n // 2 * NI + c) % len(decay)]
                    for k in range(2):
                        d.ready = act(lambda e: e.activation(
                            d.ap[:, k, 1:T], dtT[:, c, 1:T], ACT.Exp, scale=a_neg[:, c, n + k:n + k + 1]),
                            dt, d.free, a_ready, pads_ready)

                for c in range(2):
                    decays(c)
                yield
                for c in range(NI):
                    out_t = state[c].ap
                    s = dve(lambda e, c=c, o=out_t: e.tensor_tensor(
                        o[:], uT[:, c:c + 1, :].to_broadcast([P, 2, T]),
                        bank_b.ap.rearrange("p (k t) -> p k t", k=2), ALU.mult), mb, dtu, state[c].free)
                    sc[c] = s
                bank_b.free = s
                yield
                for c in range(NI):
                    if c + 2 < NI:
                        decays(c + 2)
                    d = decay[(n // 2 * NI + c) % len(decay)]
                    f = state[c].ap[:].rearrange("p k t -> p (k t)")
                    g = d.ap[:].rearrange("p k t -> p (k t)")
                    d.free = sc[c] = dve(lambda e: e.tensor_tensor_scan(
                        f, g, f, 0.0, ALU.mult, ALU.add), d.ready, sc[c])
                yield
                for c in range(NI):
                    f = state[c].ap[:].rearrange("p k t -> p (k t)")
                    s = dve(lambda e: e.tensor_tensor(f, f, bank_c.ap, ALU.mult), sc[c], mc)
                    if c % 2:
                        for k in range(2):
                            for a in (c - 1, c):
                                ys = summed[a] = state[a].free = pool(lambda e: e.tensor_tensor(
                                    y_sum[:, a, :], y_sum[:, a, :], state[a].ap[:, k, :], ALU.add), s, summed[a])
                bank_c.free = s
                last_turn["bc"] = mc
                yield
            y = m_tmp
            yd = last_turn["y"] = pool(lambda e: e.tensor_tensor(y, y_sum[:], zT[:], ALU.mult), ys, zs)
            yield
            m_work = m_banks.next()
            for t in range(NT):
                for c in range(NI):
                    m = pe(lambda e: e.matmul(m_work.ap[:, t * D:(t + 1) * D], y[:, c, t * P:(t + 1) * P],
                                                        W["m_w_out"][:, c, :], start=c == 0, stop=c == NI - 1),
                           yd, m_work.free)
            yield
            while handed["x1 read"] < b:
                yield WAIT
            fl = lambda a: a.rearrange("p t d -> p (t d)")
            m_work.free = xs.free = s = dve(lambda e: e.scalar_tensor_tensor(
                fl(m_rows), fl(xs.ap[:]), 2.0, m_work.ap, ALU.mult, ALU.add), m)
            cy = carry
            cy.ready = layernorm(m_norm, lambda i: m_rows[:, i, :], lambda i: cy.ap[:, i, :], 1e-5, P, NT, s, cy.free)
            if b + 1 < B:
                load_x(b + 1)
            yield
            handed["x1"] = b + 1

        fl = lambda a: a.rearrange("p t d -> p (t d)")

        def transposed(st, src, dst, ready, dst_free, rows=P, tiles=NT, width=T):
            bank = st.banks.next()
            for t in range(tiles):
                for c in range(ND):
                    m = pe(lambda e: e.transpose(
                        bank.ap[:, c * width + t * P:c * width + t * P + rows],
                        src(t)[:, c * P:(c + 1) * P], ident[0:rows, 0:rows]), ready, bank.free)
            bank.free = s = act(lambda e: e.activation(
                dst, bank.ap[:, 0:ND * width].rearrange("p (c t) -> p c t", c=ND), ACT.Copy), m, dst_free)
            return s

        def rows_out(st, lhs, n, w, *ready):
            bank = st.banks.next()
            for t in range(NT):
                for c in range(n):
                    m = pe(lambda e: e.matmul(bank.ap[:, t * D:(t + 1) * D], lhs[:, c, t * P:(t + 1) * P],
                                                        w[:, c, :], start=c == 0, stop=c == n - 1), *ready, bank.free)
            return bank, m

        def bcast(row):
            return row.unsqueeze(1).to_broadcast([P, NT, D])

        def attention(st, kind, qT, kT, wq, wk, wv, *ready):
            keys = T if kind == "causal" else KEYS
            per_head = 1 if kind == "causal" else NT
            units = [(h, t) for h in range(H) for t in range(per_head)]
            lag = 2 if kind == "causal" else 3
            made, turned = {}, {}
            outs = [None]

            def project(pair):
                sl = st.pairs[pair % 3]
                col = slice(pair * P, (pair + 1) * P)
                bank = st.banks.next()
                for c in range(ND):
                    m = pe(lambda e: e.matmul(bank.ap[:, 0:T], wq[:, c, col], qT[:, c, 0:T], start=c == 0,
                                                   stop=c == ND - 1), *ready, bank.free)
                bank.free = q = act(lambda e: e.activation(sl.ap[:, 0:T], bank.ap[:, 0:T], ACT.Copy,
                                                                      scale=HD ** -0.5), m, sl.free)
                bank = st.banks.next()
                for c in range(ND):
                    m = pe(lambda e: e.matmul(bank.ap[:, 0:keys], wk[:, c, col], kT[:, c, 0:keys],
                                                              start=c == 0, stop=c == ND - 1), *ready, bank.free)
                bank.free = k = act(lambda e: e.activation(sl.ap[:, T:T + keys], bank.ap[:, 0:keys], ACT.Copy), m, sl.free)
                bank = st.banks.next()
                nk = (keys + P - 1) // P
                for i in range(nk):
                    n = min(P, keys - i * P)
                    for c in range(ND):
                        m = pe(lambda e: e.matmul(
                            bank.ap[0:n, i * P:(i + 1) * P], kT[:, c, i * P:i * P + n], wv[:, c, col],
                            start=c == 0, stop=c == ND - 1), *ready, bank.free)
                v = act(lambda e: e.activation(sl.ap[:, st.v0:st.v0 + T], bank.ap[:, 0:T], ACT.Copy), m, sl.free)
                if nk == NK:
                    n = keys - 2 * P
                    v = act(lambda e: e.activation(sl.ap[0:n, st.v0 + T:st.v0 + T + P], bank.ap[0:n, T:T + P],
                                                              ACT.Copy), m)
                bank.free = v
                st.last_wv = m
                sl.q, sl.k, sl.v = q, k, v

            def scores(u):
                h, t = units[u]
                sl, o = st.pairs[h // 2 % 3], h % 2 * HD
                bank, pr, sums = st.banks.next(), st.probs[u % 4], st.stat[:, u % 8, :]
                qs = lambda i: sl.ap[o:o + HD, i * P:(i + 1) * P]
                if kind == "causal":
                    spans = [(0, P, 0), (P, T, 1)]
                    for a, n, i in spans:
                        pe(lambda e: e.matmul(bank.ap[:, a:a + n], qs(i), sl.ap[o:o + HD, T:T + n],
                                                             start=True, stop=False), sl.q, sl.k, bank.free)
                        m = pe(lambda e: e.matmul(bank.ap[:, a + n - P:a + n], ident_bf[:], causal[:],
                                                            start=False, stop=True),
                               causal_ready, ident_bf_ready)
                else:
                    spans = [(0, KEYS, t)]
                    pe(lambda e: e.matmul(bank.ap[:, 0:KEYS], qs(t), sl.ap[o:o + HD, T:T + KEYS], start=True, stop=False),
                       sl.q, sl.k, bank.free)
                    m = pe(lambda e: e.matmul(bank.ap[:, T:KEYS], ones_bf[:], bias_row[:], start=False, stop=True),
                           mask_done[0])
                for j, (a, n, i) in enumerate(spans):
                    mx = dve(lambda e: e.tensor_reduce(sums[:, j:j + 1], bank.ap[:, a:a + n], AX.X,
                                                                      ALU.max, negate=True), m, st.stat_free[u % 8])
                for j, (a, n, i) in enumerate(spans):
                    ex = act(lambda e: e.activation(
                        pr.ap[:, a:a + n], bank.ap[:, a:a + n], ACT.Exp, bias=sums[:, j:j + 1],
                        accum_out=sums[:, 2 + j:3 + j]), mx, pr.free)
                bank.free = ex
                ns = len(spans)
                rc = dve(lambda e: e.reciprocal(sums[:, 4:4 + ns], sums[:, 2:2 + ns]), ex)
                for j, (a, n, i) in enumerate(spans):
                    s = pool(lambda e: e.tensor_scalar(
                        pr.ap[:, a:a + n], pr.ap[:, a:a + n], sums[:, 4 + j:5 + j], 1.0, ALU.mult, ALU.mult), rc)
                st.stat_free[u % 8] = s
                made[u] = s

            def turn_probs(u):
                h, t = units[u]
                bank, pr, pt = st.banks.next(), st.probs[u % 4], st.probsT[h % 3]
                for i in range(NK):
                    m = pe(lambda e: e.transpose(bank.ap[:, i * P:(i + 1) * P], pr.ap[:, i * P:(i + 1) * P],
                                                      ident[:]), made[u], bank.free)
                pr.free = m
                if kind == "causal":
                    dst, src = pt.ap[:, 0:PW], bank.ap[:, 0:PW]
                else:
                    dst = pt.ap.rearrange("p (k q) -> p k q", q=T)[:, :, t * P:(t + 1) * P]
                    src = bank.ap[:, 0:PW].rearrange("p (k q) -> p k q", q=P)
                if u % 2:
                    s = dve(lambda e: e.tensor_copy(dst, src), m, pt.free)
                else:
                    s = act(lambda e: e.activation(dst, src, ACT.Copy), m, pt.free)
                bank.free = s
                turned.setdefault(h, []).append(s)

            def weigh(pair):
                sl, bank = st.pairs[pair % 3], st.banks.next()
                g = bank.ap[:, 0:T]
                parts = [(0, 0, T, 0), (1, T, PW, P)] if kind == "causal" else [(i, i * T, (i + 1) * T, 0) for i in range(NK)]
                for j, (i, a, z, q0) in enumerate(parts):
                    for o in (0, HD):
                        pt = st.probsT[(2 * pair + o // HD) % 3]
                        m = pe(lambda e: e.matmul(
                            g[o:o + HD, q0:T], sl.ap[:, st.v0 + i * P + o:st.v0 + i * P + o + HD], pt.ap[:, a:z],
                            start=j == 0, stop=j == len(parts) - 1),
                            *turned[2 * pair + o // HD], sl.v, bank.free, pads2_ready)
                        pt.free = m
                sl.free = m
                bank.free = outs[0] = act(lambda e: e.activation(st.aT[:, pair, :], g, ACT.Copy), m)

            project(0)
            yield
            total = len(units)
            upp = total // NE
            for u in range(total + lag + 1):
                if u < total:
                    scores(u)
                v = u - lag - 1
                if 0 <= v < total and (v + 1) % upp == 0:
                    weigh(v // upp)
                if 0 <= u - lag < total:
                    turn_probs(u - lag)
                yield
                if (u + 1) % upp == upp - 1 and (u + 1) // upp + 1 < NE:
                    project((u + 1) // upp + 1)
                    yield
            st.out = outs[0]

        mask_done = [None]

        def load_context_a(b):
            cs, ms = A.context, mask_in
            cs.ready = sync.dma(ctx_a_load, cs.ap[0:S2, :], I["ctx"][b], cs.free)
            ms.ready = sync.dma(mask_a_load, ms.ap, I["mask_q"][b, 0].rearrange("(t p) k -> p t k", p=P), ms.free)

        def load_context_x(b):
            cs, ms = X.context, key_mask
            cs.ready = sync.dma(ctx_x_load, cs.ap[0:S2, :], I["ctx"][b], cs.free)
            ms.ready = sync.dma(mask_x_load, ms.ap, I["mask_k"][b:b + 1, :], ms.free)

        def first_layer_and_causal(b):
            while handed["x1"] <= b:
                yield WAIT
            st = A
            cy, cs, ms, xT = carry, A.context, mask_in, A.kvT[:, :, 0:T]
            x1T = transposed(st, lambda t: cy.ap[:, t, :], xT, cy.ready, None)
            ctxT = st.kvT[:, :, T:KEYS]
            c_T = cs.free = transposed(st, lambda t: cs.ap[0:S2, :], ctxT, cs.ready, None, rows=S2, tiles=1, width=S2)
            s = dve(lambda e: e.tensor_scalar(bound[:], ms.ap, 0.0, NEG, ALU.is_equal, ALU.mult), ms.ready)
            bd = ms.free = dve(lambda e: e.tensor_scalar(bound[:], bound[:], 100.0, None, ALU.add), s)
            if b + 1 < B:
                load_context_a(b + 1)
            yield
            G = P // HD0
            qT0 = st.pairs[0].ap[:, 0:ND * T].rearrange("p (c t) -> p c t", c=ND)
            kT0 = st.pairs[1].ap[:, 0:ND * S2].rearrange("p (c t) -> p c t", c=ND)
            bank = st.banks.next()
            for c2 in range(ND):
                for c in range(ND):
                    m = pe(lambda e: e.matmul(bank.ap[:, c2 * T:(c2 + 1) * T], W["c_wq"][:, c, c2 * P:(c2 + 1) * P],
                                                          xT[:, c, :], start=c == 0, stop=c == ND - 1),
                           x1T, bank.free, cross_loaded, shared.ready)
            for c2 in range(ND):
                q = dve(lambda e: e.tensor_scalar(
                    qT0[:, c2, :], bank.ap[:, c2 * T:(c2 + 1) * T], W["c_bq"][:, c2:c2 + 1], HD0 ** -0.5,
                    ALU.add, ALU.mult), m, st.pairs[0].free)
            bank.free = q
            bank = st.banks.next()
            for c2 in range(ND):
                for c in range(ND):
                    m = pe(lambda e: e.matmul(
                        bank.ap[:, c2 * S2:(c2 + 1) * S2], W["c_wk"][:, c, c2 * P:(c2 + 1) * P], ctxT[:, c, :],
                        start=c == 0, stop=c == ND - 1), c_T, bank.free)
            for c2 in range(ND):
                k = act(lambda e: e.activation(
                    kT0[:, c2, :], bank.ap[:, c2 * S2:(c2 + 1) * S2], ACT.Identity, bias=W["c_bk"][:, c2:c2 + 1]),
                    m, st.pairs[1].free)
            bank.free = k
            bank = st.banks.next()
            for c in range(ND):
                m = pe(lambda e: e.matmul(bank.ap[0:S2, 0:D], ctxT[:, c, :], W["c_wv"][:, c, :],
                                                          start=c == 0, stop=c == ND - 1), c_T, bank.free)
            for par in range(2):
                v = dve(lambda e: e.tensor_tensor(
                    vpad[:, par::2, par * HD0:(par + 1) * HD0],
                    bank.ap[0:S2, 0:D].rearrange("k (h d) -> k h d", d=HD0)[:, par::2, :],
                    W["c_bv"][0:S2, :].rearrange("k (h d) -> k h d", d=HD0)[:, par::2, :], ALU.add), m, vpad_ready)
            bank.free = v
            yield
            sc = [st.attn[:, t * H * S2:(t + 1) * H * S2].rearrange("p (h k) -> p h k", k=S2) for t in range(NT)]
            half = G // 2
            kbs = []
            for c in range(ND):
                kb = dve(lambda e: e.tensor_tensor(
                    kblk[:, c].rearrange("p (h k) -> p h k", k=S2), kT0[:, c:c + 1, :].to_broadcast([P, G, S2]),
                    head_of[:].unsqueeze(2).to_broadcast([P, G, S2]), ALU.mult), k, kblk_free[0], heads_ready)
                kbs.append(kb)
            pm = []
            for t in range(NT):
                for c in range(ND):
                    for g in range(2):
                        bank = st.banks.next()
                        kblk_free[0] = m = pe(lambda e: e.matmul(
                            bank.ap[:, 0:half * S2], qT0[:, c, t * P:(t + 1) * P],
                            kblk[:, c, g * half * S2:(g + 1) * half * S2], start=True, stop=True), q, kbs[c], bank.free)
                        h0 = c * G + g * half
                        bank.free = s = dve(lambda e: e.scalar_tensor_tensor(
                            sc[t][:, h0:h0 + half, :], bank.ap[:, 0:half * S2].rearrange("p (h k) -> p h k", k=S2), -100.0,
                            bound[:, t:t + 1, :].to_broadcast([P, half, S2]), ALU.max, ALU.min), m, bd, w2_ready[0])
                        yield
                m = dve(lambda e: e.tensor_reduce(l0_stat[:, t, 0, :], sc[t], AX.X, ALU.max), s)
                s = pool(lambda e: e.tensor_tensor(sc[t], sc[t], l0_stat[:, t, 0, :].unsqueeze(2).to_broadcast([P, H, S2]),
                                                   ALU.subtract), m)
                shifted = act(lambda e: e.activation(sc[t], sc[t], ACT.Exp), s)
                pm.append(shifted)
                yield
            for t in range(NT):
                m = dve(lambda e: e.tensor_reduce(l0_stat[:, t, 1, :], sc[t], AX.X, ALU.add), pm[t])
                m = dve(lambda e: e.reciprocal(l0_stat[:, t, 0, :], l0_stat[:, t, 1, :]), m)
                pm[t] = pool(lambda e: e.tensor_tensor(
                    sc[t], sc[t], l0_stat[:, t, 0, :].unsqueeze(2).to_broadcast([P, H, S2]), ALU.mult), m)
                yield
            pT = [Slot(st.aT[:, ND + 2 * i:ND + 2 * i + 2, :].rearrange("p c t -> p (c t)"), kblk_free[0]) for i in range(3)]
            a0 = st.aT[:, 0:ND, :]
            for hp in range(H // 2 + 1):
                if hp < H // 2:
                    bank, pt = st.other_banks.next(), pT[hp % 3]
                    for j in range(2):
                        for t in range(NT):
                            m = pe(lambda e: e.transpose(
                                bank.ap[0:S2, j * T + t * P:j * T + (t + 1) * P], sc[t][:, 2 * hp + j, :], ident[:]),
                                pm[t], bank.free)
                    bank.free = pt.ready = act(lambda e: e.activation(pt.ap[0:S2, :], bank.ap[0:S2, :], ACT.Copy), m, pt.free)
                if hp % 2 or hp == 0:
                    continue
                for j in range(2):
                    for hq in (hp - 2, hp - 1):
                        o, pt = hq % 4 * 2 * HD0, pT[hq % 3]
                        pt.free = m = pe(lambda e: e.matmul(
                            st.gather.ap[o:o + 2 * HD0, 0:T], vpad[:, 2 * hq + j, :], pt.ap[0:S2, j * T:(j + 1) * T],
                            start=j == 0, stop=j == 1, tile_position=(0, o)), pt.ready, v, st.gather.free)
                if hp % 4 == 0:
                    chunk = hp // 4 - 1
                    st.gather.free = a = act(lambda e: e.activation(a0[:, chunk, :], st.gather.ap[:, 0:T], ACT.Copy), m)
                yield
            bank, m = rows_out(st, a0, ND, W["c_wo"], a)
            shared.free = m
            shared.ready = sync.dma(shared_load, W["a_wo"], chunks(I["a_wo"]), m)
            s = dve(lambda e: e.tensor_tensor(x_a[:], cy.ap[:], bank.ap.rearrange("p (t d) -> p t d", t=NT), ALU.add), m)
            bank.free = cy.free = s
            s = dve(lambda e: e.tensor_tensor(x_a[:], x_a[:], bcast(W["c_bo"][:]), ALU.add), s)
            x2 = layernorm(st.norm, lambda i: x_a[:, i, :], lambda i: x_a[:, i, :], 1e-5, P, NT, s)
            yield
            handed["x1 read"] = b + 1
            x2T = transposed(st, lambda t: x_a[:, t, :], xT, x2, None)
            for f in range(0, NF0, 2):
                bank = st.banks.next()
                for q in range(2):
                    for c in range(ND):
                        m = pe(lambda e: e.matmul(
                            bank.ap[:, q * T:(q + 1) * T], W["f_w1"][:, c, (f + q) * P:(f + q + 1) * P], xT[:, c, :],
                            start=c == 0, stop=c == ND - 1), x2T, bank.free, w1_or_wv.ready)
                for q in range(2):
                    g = act(lambda e: e.activation(
                        st.aT[:, f + q, :], bank.ap[:, q * T:(q + 1) * T], ACT.Identity, bias=W["f_b1"][:, f + q:f + q + 1]), m)
                bank.free = g
                yield
            w1_or_wv.ready = sync.dma(w1_load, W["a_wv"], chunks(I["a_wv"]), m, w1_saved[0])
            g = act(lambda e: e.activation(st.aT[:], st.aT[:], ACT.Gelu), g)
            g.glued = True
            act(lambda e: e.preload_act_table_set(EXP_LN))
            bank, m = rows_out(st, st.aT, NF0, W["f_w2"], g, w2_ready[0])
            s = dve(lambda e: e.tensor_tensor(x_a[:], x_a[:], bank.ap.rearrange("p (t d) -> p t d", t=NT), ALU.add), m)
            bank.free = s
            s = dve(lambda e: e.tensor_tensor(x_a[:], x_a[:], bcast(W["f_b2"][:]), ALU.add), s)
            x3 = layernorm(st.norm, lambda i: x_a[:, i, :], lambda i: x_a[:, i, :], 1e-5, P, NT, s)
            yield
            x3T = transposed(st, lambda t: x_a[:, t, :], xT, x3, None)
            yield from attention(st, "causal", xT, xT, W["a_wq"], W["a_wk"], W["a_wv"], x3T, attn_loaded, w1_or_wv.ready)
            w1_free = st.last_wv
            bank, m = rows_out(st, st.aT, NE, W["a_wo"], st.out, shared.ready)
            shared.free = kblk_free[0] = m
            if b + 1 < B:
                load_cross()
                w1_or_wv.ready = sync.dma(w1_load, W["f_w1"], w1_dram, w1_free)
            s = dve(lambda e: e.tensor_tensor(st.rows, x_a[:], bank.ap.rearrange("p (t d) -> p t d", t=NT), ALU.add), m)
            bank.free = s
            s = layernorm(st.norm, lambda i: st.rows[:, i, :], lambda i: st.rows[:, i, :], 1e-3, P, NT, s)
            s = dve(lambda e: e.tensor_tensor(st.rows, st.rows, bcast(W["a_gamma"][:]), ALU.mult), s)
            s = dve(lambda e: e.tensor_tensor(st.rows, st.rows, bcast(W["a_beta"][:]), ALU.add), s)
            s = dve(lambda e: e.tensor_tensor(x_a[:], x_a[:], st.rows, ALU.add), s)
            yield
            while handed["x4 read"] < b - 1:
                yield WAIT
            x4 = between[b % 2]
            x4.ready = layernorm(st.norm, lambda i: x_a[:, i, :], lambda i: x4.ap[:, i, :], 1e-5, P, NT, s, x4.free)
            st.pairs[0].free = x4.ready
            yield
            yield
            handed["x4"] = b + 1

        def perceiver(b):
            while handed["x4"] <= b:
                yield WAIT
            st, cs, x4 = X, X.context, between[b % 2]
            bias_ready = key_mask.free = mask_done[0] = dve(lambda e: e.tensor_scalar(
                bias_row[:], key_mask.ap, 0.0, NEG, ALU.is_equal, ALU.mult), key_mask.ready)
            s = layernorm(st.norm, lambda i: x4.ap[:, i, :], lambda i: st.rows[:, i, :], 1e-5, P, NT, x4.ready, st.pairs[0].free)
            bank = st.banks.next()
            for t in range(NT):
                for c in range(ND):
                    m = pe(lambda e: e.transpose(bank.ap[:, c * T + t * P:c * T + (t + 1) * P],
                                                                      st.rows[:, t, c * P:(c + 1) * P], ident[:]), s, bank.free)
            for c in range(ND):
                lt = dve(lambda e: e.tensor_scalar(
                    st.kvT[:, c, 0:T], bank.ap[:, c * T:(c + 1) * T], W["p_ln_l_w"][:, c:c + 1],
                    W["p_ln_l_b"][:, c:c + 1], ALU.mult, ALU.add), m, perc_loaded)
            bank.free = lt
            s = layernorm(st.norm, lambda i: cs.ap[0:S2, :], lambda i: st.rows[0:S2, 0, :], 1e-5, S2, 1, cs.ready, m)
            cs.free = s
            if b + 1 < B:
                load_context_x(b + 1)
            bank = st.banks.next()
            for c in range(ND):
                m = pe(lambda e: e.transpose(bank.ap[:, c * S2:(c + 1) * S2],
                                                             st.rows[0:S2, 0, c * P:(c + 1) * P], ident[0:S2, 0:S2]), s, bank.free)
            for c in range(ND):
                kv = dve(lambda e: e.tensor_scalar(
                    st.kvT[:, c, T:KEYS], bank.ap[:, c * S2:(c + 1) * S2], W["p_ln_m_w"][:, c:c + 1],
                    W["p_ln_m_b"][:, c:c + 1], ALU.mult, ALU.add), m)
            bank.free = kv
            yield
            st.pairs[0].free = m
            yield from attention(st, "all", st.kvT, st.kvT, W["p_wq"], W["p_wk"], W["p_wv"], kv, lt)
            bank, m = rows_out(st, st.aT, NE, W["p_wo"], st.out)
            s = dve(lambda e: e.tensor_tensor(x4.ap, x4.ap, bank.ap.rearrange("p (t d) -> p t d", t=NT), ALU.add), m)
            bank.free = s
            o5 = st.pairs[1].ap[:, 0:NT * D].rearrange("p (t d) -> p t d", t=NT)
            s = layernorm(st.norm, lambda i: x4.ap[:, i, :], lambda i: o5[:, i, :], 1e-5, P, NT, s, st.pairs[1].free)
            x4.free = s
            am = dve(lambda e: e.tensor_reduce(amax5[:, b:b + 1], fl(o5), AX.X, ALU.max, apply_absolute_value=True), s)
            st.pairs[1].free = sync.dma(spill, x5_dram[b].rearrange("(t p) d -> p t d", p=P), o5, s)
            phase1_last[0], phase1_last[1] = am, st.pairs[1].free
            yield
            handed["x4 read"] = b + 1

        kblk_free = [None]

        l0_stat = sb(ph1, "l0_stat", [P, NT, 2, H])
        phase1_last = [None, None]

        load_context_a(0)
        load_context_x(0)
        def batches(part, first=()):
            yield from first
            for b in range(B):
                yield from part(b)

        interleave((Lane("M", 0.0, M_US, batches(mamba)),
                    Lane("A", A_START, A_US, batches(first_layer_and_causal, ternary_weights())),
                    Lane("X", X_START, X_US, batches(perceiver))), weights)

        ends = [q.steps[-1] for q in (pe, act, pool)]
        for s in ends:
            s.wanted = True
        ph1.close()
        begin = (phase1_last[0], phase1_last[1], *ends)
        W_MAX, A_MAX = 7.0, 32767.0
        LPB = 32
        TB = 2 * T
        NP = B * T // TB
        big = sb(ctx, "big", [P, NF1, B * T])
        up_int = sb(ctx, "up_int", [P, NF1, B * T], I16)
        xqT = sb(ctx, "xqT", [P, ND, B * T])
        gateT, upT = sb(ctx, "gateT", [P, ND, F1]), sb(ctx, "upT", [P, ND, F1])
        downT = sb(ctx, "downT", [P, NF1, D])
        rows = [Slot(sb(ctx, f"rows{i}", [P, NT, D])[:]) for i in range(3)]
        q_norm = norm_tiles(ctx, "q_norm", NT)
        part = sb(ctx, "part", [P, 4, NP * NF1])
        scales = sb(ctx, "scales", [P, 5, 4])
        ring = Ring([Slot(b[:]) for b in banks])

        def scale_of(which, partial, *after):
            v = scales[:, which, :]
            s = dve(lambda e: e.tensor_reduce(v[:, 0:1], partial, AX.X, ALU.max), *after)
            s = pool(lambda e: e.partition_all_reduce(v[:, 1:2], v[:, 0:1], P, RMAX), s)
            s = dve(lambda e: e.tensor_scalar(v[:, 2:3], v[:, 1:2], 1.0 / A_MAX, 1e-12, ALU.mult, ALU.max), s)
            return v[:, 2:3], v[:, 3:4], dve(lambda e: e.reciprocal(v[:, 3:4], v[:, 2:3]), s)

        sx, sx_inv, sx_ready = scale_of(0, amax5[:], *begin)

        stage = up_int[:].rearrange("p c t -> p (c t)").bitcast(F32)
        size = F1 * D // P
        nb = size // LPB
        stages = [stage[:, n * 2 * (size + nb):(n + 1) * 2 * (size + nb)] for n in range(3)]
        names = ("g_up", "g_gate", "g_down")
        loads = [sync.dma(weight_load[5 + n], stages[n][:, 0:size].rearrange("p (c n) -> p c n", n=I[name].shape[1]),
                          chunks(I[name]), *begin) for n, name in enumerate(names)]

        def quantised_weight(n, dst):
            w, q = stages[n][:, 0:size], stages[n][:, size:2 * size]
            sc, inv = (stages[n][:, 2 * size + i * nb:2 * size + (i + 1) * nb] for i in range(2))
            blocks = lambda a: a.rearrange("p (b k) -> p b k", k=LPB)
            s = dve(lambda e: e.tensor_reduce(sc, blocks(w), AX.X, ALU.max, apply_absolute_value=True), loads[n])
            s = dve(lambda e: e.tensor_scalar(sc, sc, 1.0 / W_MAX, 1e-12, ALU.mult, ALU.max), s)
            s = dve(lambda e: e.reciprocal(inv, sc), s)
            s = dve(lambda e: e.tensor_tensor(blocks(q), blocks(w), inv.unsqueeze(2).to_broadcast([P, nb, LPB]), ALU.mult), s)
            s = dve(lambda e: e.tensor_scalar(q, q, RNE, RNE, ALU.add, ALU.subtract), s)
            s = dve(lambda e: e.tensor_tensor(blocks(q), blocks(q), sc.unsqueeze(2).to_broadcast([P, nb, LPB]), ALU.mult), s)
            width = I[names[n]].shape[1]
            nr, nc_ = I[names[n]].shape[0] // P, width // P
            qv = q.rearrange("p (r c) -> p r c", r=nr)
            for c in range(nc_):
                for r0 in range(0, nr, 4):
                    bank, k = ring.next(), min(4, nr - r0)
                    for r in range(k):
                        m = pe(lambda e: e.transpose(bank.ap[:, r * P:(r + 1) * P], qv[:, r0 + r, c * P:(c + 1) * P], ident[:]),
                               s, bank.free)
                    bank.free = ready = act(lambda e: e.activation(dst[:, c, r0 * P:(r0 + k) * P], bank.ap[:, 0:k * P], ACT.Copy),
                                            m, *begin)
            return ready

        def quantised_x(b):
            r = rows[b % 3]
            load = sync.dma(reload_rows[b % 3], r.ap, x5_dram[b].rearrange("(t p) d -> p t d", p=P), r.free, *begin)
            bank = ring.next()
            for t in range(NT):
                for c in range(ND):
                    m = r.free = pe(lambda e: e.transpose(bank.ap[:, c * T + t * P:c * T + (t + 1) * P],
                                                          r.ap[:, t, c * P:(c + 1) * P], ident[:]), load, bank.free)
            xs = xqT[:, :, b * T:(b + 1) * T]
            s = bank.free = act(lambda e: e.activation(xs, bank.ap.rearrange("p (c t) -> p c t", c=ND), ACT.Identity,
                                                       bias=rne[:], scale=sx_inv), m, sx_ready)
            return dve(lambda e: e.tensor_scalar(xs, xs, RNE, sx, ALU.subtract, ALU.mult), s)

        def piece(a, p):
            return a[:, :, p * TB:(p + 1) * TB]

        def project(w, which, p, *after):
            for i in range(NF1):
                bank = ring.next()
                for c in range(ND):
                    m = pe(lambda e: e.matmul(bank.ap[:, 0:TB], w[:, c, i * P:(i + 1) * P], piece(xqT, p)[:, c, :],
                                              start=c == 0, stop=c == ND - 1), bank.free, *after)
                bank.free = a = act(lambda e: e.activation(piece(big, p)[:, i, :], bank.ap[:, 0:TB], ACT.Copy), m, *after)
                at = p * NF1 + i
                done = dve(lambda e: e.tensor_reduce(part[:, which, at:at + 1], piece(big, p)[:, i, :], AX.X, ALU.max,
                                                     apply_absolute_value=True), a)
            return done

        def rounded(a, inverse, *after):
            return act(lambda e: e.activation(a, a, ACT.Identity, bias=rne[:], scale=inverse), *after)

        up_w = quantised_weight(0, upT)
        x_ready = [quantised_x(b) for b in range(4)]
        for p in range(NP):
            up_done = project(upT, 0, p, x_ready[2 * p], x_ready[2 * p + 1], up_w)
            x_ready += [quantised_x(b) for b in range(2 * p + 4, min(2 * p + 6, B))]
            if p == 0:
                gate_w = quantised_weight(1, gateT)
            if p == 1:
                down_w = quantised_weight(2, downT)
        su, su_inv, su_ready = scale_of(1, part[:, 0, :], up_done)

        def store_up(p):
            s = rounded(piece(big, p), su_inv, su_ready)
            return dve(lambda e: e.tensor_scalar(piece(up_int, p), piece(big, p), RNE, None, ALU.subtract), s, gate_w, down_w)

        up_stored = [store_up(0), store_up(1)]
        for p in range(NP):
            gate_done = project(gateT, 1, p, up_stored[p], gate_w)
            if p + 2 < NP:
                up_stored.append(store_up(p + 2))
        sg, sg_inv, sg_ready = scale_of(2, part[:, 1, :], gate_done)

        xq_flat = xqT[:].rearrange("p c t -> p (c t)")
        n_tmp = 2
        tmp = Ring([Slot(xq_flat[:, i * NF1 * TB:(i + 1) * NF1 * TB].rearrange("p (c t) -> p c t", c=NF1)) for i in range(n_tmp)])
        gate_q = [None] * NP
        for p in range(NP + 1):
            if p < NP:
                s = rounded(piece(big, p), sg_inv, sg_ready)
                gate_q[p] = pool(lambda e: e.tensor_scalar(piece(big, p), piece(big, p), -RNE, sg, ALU.add, ALU.mult), s)
            if p > 0:
                g, sl = piece(big, p - 1), tmp.next()
                s = act(lambda e: e.activation(sl.ap, g, ACT.Sigmoid), gate_q[p - 1], sl.free)
                s = act(lambda e: e.activation(sl.ap, sl.ap, ACT.Identity, bias=rne[:], scale=65536.0), s)
                s = dve(lambda e: e.tensor_scalar(sl.ap, sl.ap, RNE, 65535.0, ALU.subtract, ALU.min), s)
                s = sl.free = dve(lambda e: e.scalar_tensor_tensor(g, sl.ap, 2.0 ** -16, g, ALU.mult, ALU.mult), s)
                silu_done = dve(lambda e: e.tensor_reduce(part[:, 2, p - 1:p], g, AX.XY, ALU.max, apply_absolute_value=True), s)
        s2, s2_inv, s2_ready = scale_of(3, part[:, 2, 0:NP], silu_done)

        for p in range(NP):
            g = piece(big, p)
            s = rounded(g, s2_inv, s2_ready)
            s = pool(lambda e: e.tensor_scalar(g, g, -RNE, s2, ALU.add, ALU.mult), s)
            s = dve(lambda e: e.scalar_tensor_tensor(g, piece(up_int, p), su, g, ALU.mult, ALU.mult), s)
            product_done = dve(lambda e: e.tensor_reduce(part[:, 3, p:p + 1], g, AX.XY, ALU.max, apply_absolute_value=True), s)
        so, so_inv, so_ready = scale_of(4, part[:, 3, 0:NP], product_done)
        act(lambda e: e.preload_act_table_set(EXP_LN))

        def product_q(p):
            s = rounded(piece(big, p), so_inv, so_ready)
            return dve(lambda e: e.tensor_scalar(piece(big, p), piece(big, p), RNE, so, ALU.subtract, ALU.mult), s)

        def reload(b):
            r = rows[b % 3]
            return sync.dma(reload_rows[b % 3], r.ap, x5_dram[b].rearrange("(t p) d -> p t d", p=P), r.free)

        o_ready, x_rows = [product_q(0)], [reload(0), reload(1)]
        for b in range(B):
            if b % 2 == 0 and b // 2 + 1 < NP:
                o_ready.append(product_q(b // 2 + 1))
            if b + 2 < B:
                x_rows.append(reload(b + 2))
            r, bank = rows[b % 3], ring.next()
            for t in range(NT):
                for i in range(NF1):
                    t0 = b * T + t * P
                    m = pe(lambda e: e.matmul(bank.ap[:, t * D:(t + 1) * D], big[:, i, t0:t0 + P], downT[:, i, :],
                                              start=i == 0, stop=i == NF1 - 1), o_ready[b // 2], bank.free)
            bank.free = s = dve(lambda e: e.tensor_tensor(fl(r.ap), fl(r.ap), bank.ap, ALU.add), m, x_rows[b])
            s = layernorm(q_norm, lambda i: r.ap[:, i, :], lambda i: r.ap[:, i, :], 1e-5, P, NT, s)
            r.free = sync.dma(final_rows[b % 3], out[b].rearrange("(t p) d -> p t d", p=P), r.ap, s)
        block = ctx.enter_context(nc.Block())
        for q in (pe, dve, act, pool, sync):
            q.number()

        @block.tensor
        def _(e):
            pe.emit(e)

        @block.vector
        def _(e):
            dve.emit(e)

        @block.scalar
        def _(e):
            e.preload_act_table_set(EXP_LN)
            act.emit(e)

        @block.gpsimd
        def _(e):
            pool.emit(e)

        @block.sync
        def _(e):
            sync.emit(e)
            for c in (spill, *final_rows):
                if c.count:
                    e.wait_ge(c.sem, c.count)


def laid_out(inputs):
    import numpy as np

    a = {k: np.asarray(v) for k, v in inputs.items()}
    m = {k: a["L0_attn_" + k] for k in ("W_in", "W_x", "W_dt", "W_out", "conv_w", "conv_b", "b_dt", "A_log", "Dp", "ln_g", "ln_b")}
    r = {
        "x": a["x"], "ctx": a["ctx_1024"], "mask_q": a["mask_Bx1xSxS2_ik1"], "mask_k": a["mask_BxS2_ik0"],
        "m_w_in": m["W_in"].T, "m_w_x": m["W_x"].T, "m_w_dt": m["W_dt"].T, "m_w_out": m["W_out"].T,
        "m_conv_w": m["conv_w"][:, 0, :], "m_conv_b": m["conv_b"], "m_b_dt": m["b_dt"], "m_a_log": m["A_log"],
        "m_dp": m["Dp"], "m_ln_g": m["ln_g"], "m_ln_b": m["ln_b"],
        "f_w1": a["L0_ffn_W1"].T, "f_b1": a["L0_ffn_b1"], "f_w2": a["L0_ffn_W2"].T, "f_b2": a["L0_ffn_b2"],
        "a_wo": a["L1_attn_Wo"], "a_gamma": a["L1_attn_gamma"], "a_beta": a["L1_attn_beta"],
        "g_gate": a["L1_ffn_w_gate"], "g_up": a["L1_ffn_w_up"], "g_down": a["L1_ffn_w_down"],
    }
    for w in ("q", "k", "v", "o"):
        r["c_w" + w] = a["L0_xattn_w" + w].T
        r["c_b" + w] = a["L0_xattn_b" + w]
        r["p_w" + w] = a["L1_xattn_W" + w]
    for w in ("q", "k", "v"):
        t = a["L1_attn_W" + w].transpose(1, 0, 2)
        r["a_w" + w] = t.reshape(t.shape[0], -1)
    for n in ("ln_m_w", "ln_m_b", "ln_l_w", "ln_l_b"):
        r["p_" + n] = a["L1_xattn_" + n]
    for n in ("m_conv_b", "m_b_dt", "m_dp", "m_ln_g", "m_ln_b", "f_b1", "c_bq", "c_bk",
              "p_ln_m_w", "p_ln_m_b", "p_ln_l_w", "p_ln_l_b"):
        r[n] = r[n].reshape(-1, P).T
    return {k: np.ascontiguousarray(v) for k, v in r.items()}


def kernel(**inputs):
    import concourse.bacc as bacc
    from concourse.bass_utils import run_bass_kernel_spmd

    arrays = laid_out(inputs)
    nc = bacc.Bacc("TRN2", target_bir_lowering=False, num_devices=1)
    ins = {n: nc.dram_tensor(n, a.shape, mybir.dt.from_np(a.dtype), kind="ExternalInput").ap()
           for n, a in arrays.items()}
    out = nc.dram_tensor("out", arrays["x"].shape, F32, kind="ExternalOutput").ap()
    decoder_kernel(nc, ins, out)
    return run_bass_kernel_spmd(nc, [arrays], core_ids=[0]).results[0]["out"]
```
